# Optimizing a Trainium2 kernel written in Bass

```python
import numpy as np
import jax
import jax.numpy as jnp

def _softmax(x, axis=-1):
    return jax.nn.softmax(x, axis=axis)

def _gelu(x):
    return jax.nn.gelu(x, approximate=True)

def _silu(x):
    return jax.nn.silu(x)

def _sigmoid(x):
    return jax.nn.sigmoid(x)

def _layernorm(x, axis=-1, eps=1e-05):
    m = jnp.mean(x, axis=axis, keepdims=True)
    v = jnp.var(x, axis=axis, keepdims=True)
    return (x - m) / jnp.sqrt(v + eps)

def _scatter_add(tgt, idx, src, axis=0):
    return tgt.at[idx].add(src)

def _segment_sum(src, seg, n):
    return jax.ops.segment_sum(src, seg, n)
kernel_name = 'mk_seq_postln_d2_jaxref_r8_812db2'

def setup_inputs(seed: int=0):
    np.random.seed(seed)
    _w = jnp.asarray

    def _L0_attn_setup():
        import jax, jax.numpy as jnp
        import numpy as np
        HIDDEN = 512
        HEAD_DIM = 128
        N_Q_HEADS = 32
        N_KV_HEADS = 8
        SLIDING_WINDOW = 128
        ROPE_THETA = 10000.0
        BATCH, SEQ = (1, 256)

        def _rope(t, pos):
            d = t.shape[-1]
            half = d // 2
            inv_freq = ROPE_THETA ** (-jnp.arange(half, dtype=jnp.float32) / half)
            ang = pos[:, None].astype(jnp.float32) * inv_freq[None, :]
            cos = jnp.cos(ang)[None, :, None, :]
            sin = jnp.sin(ang)[None, :, None, :]
            t1, t2 = (t[..., :half], t[..., half:])
            return jnp.concatenate([t1 * cos - t2 * sin, t1 * sin + t2 * cos], axis=-1)
        key = jax.random.key(seed)
        ks = jax.random.split(key, 5)
        w_scale = HIDDEN ** (-0.5)
        return {'x': jax.random.normal(ks[0], (BATCH, SEQ, HIDDEN), jnp.float32), 'wq': jax.random.normal(ks[1], (HIDDEN, N_Q_HEADS * HEAD_DIM), jnp.float32) * w_scale, 'wk': jax.random.normal(ks[2], (HIDDEN, N_KV_HEADS * HEAD_DIM), jnp.float32) * w_scale, 'wv': jax.random.normal(ks[3], (HIDDEN, N_KV_HEADS * HEAD_DIM), jnp.float32) * w_scale, 'wo': jax.random.normal(ks[4], (N_Q_HEADS * HEAD_DIM, HIDDEN), jnp.float32) * w_scale}
    _L0_attn_in = _L0_attn_setup()

    def _L0_ffn_setup():
        import jax, jax.numpy as jnp
        import numpy as np
        M = 512
        K = 512

        def _make_2to4_mask(key, shape):
            scores = jax.random.normal(key, shape)
            g = scores.reshape(shape[0], shape[1] // 4, 4)
            rank = jnp.argsort(jnp.argsort(-jnp.abs(g), axis=-1), axis=-1)
            return (rank < 2).reshape(shape).astype(jnp.float32)
        key = jax.random.key(seed)
        k_x, k_w12, k_b12, k_w3, k_b3, k_m = jax.random.split(key, 6)
        x = jax.random.normal(k_x, (4, 256, K), dtype=jnp.float32)
        w12_dense = jax.random.normal(k_w12, (2 * M, K), dtype=jnp.float32) * (1.0 / np.sqrt(K))
        mask12 = _make_2to4_mask(k_m, (2 * M, K))
        w12 = w12_dense * mask12
        b12 = jax.random.normal(k_b12, (2 * M,), dtype=jnp.float32) * 0.01
        w3 = jax.random.normal(k_w3, (M, M), dtype=jnp.float32) * (1.0 / np.sqrt(M))
        b3 = jax.random.normal(k_b3, (M,), dtype=jnp.float32) * 0.01
        return {'x': x, 'w12': w12, 'b12': b12, 'w3': w3, 'b3': b3}
    _L0_ffn_in = _L0_ffn_setup()

    def _L1_attn_setup():
        import jax, jax.numpy as jnp
        import numpy as np
        import math
        HIDDEN = 512
        NUM_HEADS = 32
        HEAD_DIM = HIDDEN // NUM_HEADS
        SCALE = 1.0 / HEAD_DIM

        def _alibi_slopes(n_heads: int) -> np.ndarray:
            cp2 = 2 ** math.floor(math.log2(n_heads))
            base = 2 ** (-2 ** (-(math.log2(cp2) - 3)))
            slopes = base ** np.arange(1, cp2 + 1, dtype=np.float32)
            if cp2 != n_heads:
                extra_base = 2 ** (-2 ** (-(math.log2(2 * cp2) - 3)))
                n_rem = min(cp2, n_heads - cp2)
                extra = extra_base ** np.arange(1, 1 + 2 * n_rem, 2, dtype=np.float32)
                slopes = np.concatenate([slopes, extra])
            return slopes.astype(np.float32)
        key = jax.random.key(seed)
        k1, k2, k3, k4, k5 = jax.random.split(key, 5)
        B, S = (2, 256)
        return {'hidden_states': jax.random.normal(k1, (B, S, HIDDEN), dtype=jnp.float32), 'w_attn': jax.random.normal(k2, (HIDDEN, 3 * HIDDEN), dtype=jnp.float32) * 0.02, 'b_attn': jnp.zeros((3 * HIDDEN,), dtype=jnp.float32), 'w_proj': jax.random.normal(k3, (HIDDEN, HIDDEN), dtype=jnp.float32) * 0.02, 'b_proj': jnp.zeros((HIDDEN,), dtype=jnp.float32)}
    _L1_attn_in = _L1_attn_setup()

    def _L1_ffn_setup():
        import jax, jax.numpy as jnp
        import numpy as np
        M = 512
        K = 512

        def _make_2to4_mask(key, shape):
            scores = jax.random.normal(key, shape)
            g = scores.reshape(shape[0], shape[1] // 4, 4)
            rank = jnp.argsort(jnp.argsort(-jnp.abs(g), axis=-1), axis=-1)
            return (rank < 2).reshape(shape).astype(jnp.float32)
        key = jax.random.key(seed)
        k_x, k_w12, k_b12, k_w3, k_b3, k_m = jax.random.split(key, 6)
        x = jax.random.normal(k_x, (4, 256, K), dtype=jnp.float32)
        w12_dense = jax.random.normal(k_w12, (2 * M, K), dtype=jnp.float32) * (1.0 / np.sqrt(K))
        mask12 = _make_2to4_mask(k_m, (2 * M, K))
        w12 = w12_dense * mask12
        b12 = jax.random.normal(k_b12, (2 * M,), dtype=jnp.float32) * 0.01
        w3 = jax.random.normal(k_w3, (M, M), dtype=jnp.float32) * (1.0 / np.sqrt(M))
        b3 = jax.random.normal(k_b3, (M,), dtype=jnp.float32) * 0.01
        return {'x': x, 'w12': w12, 'b12': b12, 'w3': w3, 'b3': b3}
    _L1_ffn_in = _L1_ffn_setup()
    _d = {'L0_attn_x': _L0_attn_in['x'], 'L0_attn_wq': _L0_attn_in['wq'], 'L0_attn_wk': _L0_attn_in['wk'], 'L0_attn_wv': _L0_attn_in['wv'], 'L0_attn_wo': _L0_attn_in['wo'], 'L0_ffn_w12': _L0_ffn_in['w12'], 'L0_ffn_b12': _L0_ffn_in['b12'], 'L0_ffn_w3': _L0_ffn_in['w3'], 'L0_ffn_b3': _L0_ffn_in['b3'], 'L1_attn_w_attn': _L1_attn_in['w_attn'], 'L1_attn_b_attn': _L1_attn_in['b_attn'], 'L1_attn_w_proj': _L1_attn_in['w_proj'], 'L1_attn_b_proj': _L1_attn_in['b_proj'], 'L1_ffn_w12': _L1_ffn_in['w12'], 'L1_ffn_b12': _L1_ffn_in['b12'], 'L1_ffn_w3': _L1_ffn_in['w3'], 'L1_ffn_b3': _L1_ffn_in['b3']}
    _x0 = _d['L0_attn_x']
    _d['L0_attn_x'] = jax.random.normal(jax.random.fold_in(jax.random.key(seed), 1), (4, 512, 512), dtype=_x0.dtype)
    del _x0
    return _d

def reference(L0_attn_x, L0_attn_wq, L0_attn_wk, L0_attn_wv, L0_attn_wo, L0_ffn_w12, L0_ffn_b12, L0_ffn_w3, L0_ffn_b3, L1_attn_w_attn, L1_attn_b_attn, L1_attn_w_proj, L1_attn_b_proj, L1_ffn_w12, L1_ffn_b12, L1_ffn_w3, L1_ffn_b3):

    def _L0_attn_ref(x, wq, wk, wv, wo):
        import jax, jax.numpy as jnp
        import numpy as np
        HIDDEN = 512
        HEAD_DIM = 128
        N_Q_HEADS = 32
        N_KV_HEADS = 8
        SLIDING_WINDOW = 128
        ROPE_THETA = 10000.0
        BATCH, SEQ = (1, 256)

        def _rope(t, pos):
            d = t.shape[-1]
            half = d // 2
            inv_freq = ROPE_THETA ** (-jnp.arange(half, dtype=jnp.float32) / half)
            ang = pos[:, None].astype(jnp.float32) * inv_freq[None, :]
            cos = jnp.cos(ang)[None, :, None, :]
            sin = jnp.sin(ang)[None, :, None, :]
            t1, t2 = (t[..., :half], t[..., half:])
            return jnp.concatenate([t1 * cos - t2 * sin, t1 * sin + t2 * cos], axis=-1)
        B, S, _ = x.shape
        G = N_Q_HEADS // N_KV_HEADS
        sm_scale = HEAD_DIM ** (-0.5)
        q = (x @ wq).reshape(B, S, N_Q_HEADS, HEAD_DIM)
        k = (x @ wk).reshape(B, S, N_KV_HEADS, HEAD_DIM)
        v = (x @ wv).reshape(B, S, N_KV_HEADS, HEAD_DIM)
        pos = jnp.arange(S)
        q = _rope(q, pos)
        k = _rope(k, pos)
        qg = q.reshape(B, S, N_KV_HEADS, G, HEAD_DIM)
        scores = jnp.einsum('bqhgd,bshd->bhgqs', qg, k) * sm_scale
        i = pos[:, None]
        j = pos[None, :]
        allowed = (j <= i) & (j > i - SLIDING_WINDOW)
        neg = jnp.finfo(scores.dtype).min
        scores = jnp.where(allowed[None, None, None], scores, neg)
        attn = jax.nn.softmax(scores, axis=-1)
        out = jnp.einsum('bhgqs,bshd->bqhgd', attn, v).reshape(B, S, N_Q_HEADS * HEAD_DIM)
        return out @ wo

    def _L0_ffn_ref(x, w12, b12, w3, b3):
        import jax, jax.numpy as jnp
        import numpy as np
        M = 512
        K = 512

        def _make_2to4_mask(key, shape):
            scores = jax.random.normal(key, shape)
            g = scores.reshape(shape[0], shape[1] // 4, 4)
            rank = jnp.argsort(jnp.argsort(-jnp.abs(g), axis=-1), axis=-1)
            return (rank < 2).reshape(shape).astype(jnp.float32)
        x12 = jnp.einsum('bsk,mk->bsm', x, w12) + b12
        x1, x2 = jnp.split(x12, 2, axis=-1)
        x4 = jax.nn.silu(x1) * x2
        return jnp.einsum('bsm,nm->bsn', x4, w3) + b3

    def _L1_attn_ref(hidden_states, w_attn, b_attn, w_proj, b_proj):
        import jax, jax.numpy as jnp
        import numpy as np
        import math
        HIDDEN = 512
        NUM_HEADS = 32
        HEAD_DIM = HIDDEN // NUM_HEADS
        SCALE = 1.0 / HEAD_DIM

        def _alibi_slopes(n_heads: int) -> np.ndarray:
            cp2 = 2 ** math.floor(math.log2(n_heads))
            base = 2 ** (-2 ** (-(math.log2(cp2) - 3)))
            slopes = base ** np.arange(1, cp2 + 1, dtype=np.float32)
            if cp2 != n_heads:
                extra_base = 2 ** (-2 ** (-(math.log2(2 * cp2) - 3)))
                n_rem = min(cp2, n_heads - cp2)
                extra = extra_base ** np.arange(1, 1 + 2 * n_rem, 2, dtype=np.float32)
                slopes = np.concatenate([slopes, extra])
            return slopes.astype(np.float32)
        B, S, _ = hidden_states.shape
        H, D = (NUM_HEADS, HEAD_DIM)
        qkv = hidden_states @ w_attn + b_attn
        q, k, v = jnp.split(qkv, 3, axis=-1)
        q = q.reshape(B, S, H, D)
        k = k.reshape(B, S, H, D)
        v = v.reshape(B, S, H, D)
        scores = jnp.einsum('bqhd,bkhd->bhqk', q, k) * SCALE
        slopes = jnp.asarray(_alibi_slopes(H))
        pos = jnp.arange(S)
        rel = pos[None, :] - pos[:, None]
        bias = slopes[:, None, None] * rel[None, :, :]
        causal = rel <= 0
        scores = jnp.where(causal[None, None], scores + bias[None], -jnp.inf)
        attn = jax.nn.softmax(scores, axis=-1)
        out = jnp.einsum('bhqk,bkhd->bqhd', attn, v).reshape(B, S, HIDDEN)
        return out @ w_proj + b_proj

    def _L1_ffn_ref(x, w12, b12, w3, b3):
        import jax, jax.numpy as jnp
        import numpy as np
        M = 512
        K = 512

        def _make_2to4_mask(key, shape):
            scores = jax.random.normal(key, shape)
            g = scores.reshape(shape[0], shape[1] // 4, 4)
            rank = jnp.argsort(jnp.argsort(-jnp.abs(g), axis=-1), axis=-1)
            return (rank < 2).reshape(shape).astype(jnp.float32)
        x12 = jnp.einsum('bsk,mk->bsm', x, w12) + b12
        x1, x2 = jnp.split(x12, 2, axis=-1)
        x4 = jax.nn.silu(x1) * x2
        return jnp.einsum('bsm,nm->bsn', x4, w3) + b3
    x = L0_attn_x
    x = _layernorm(x + _L0_attn_ref(x, L0_attn_wq, L0_attn_wk, L0_attn_wv, L0_attn_wo), axis=-1)
    x = _layernorm(x + _L0_ffn_ref(x, L0_ffn_w12, L0_ffn_b12, L0_ffn_w3, L0_ffn_b3), axis=-1)
    x = _layernorm(x + _L1_attn_ref(x, L1_attn_w_attn, L1_attn_b_attn, L1_attn_w_proj, L1_attn_b_proj), axis=-1)
    x = _layernorm(x + _L1_ffn_ref(x, L1_ffn_w12, L1_ffn_b12, L1_ffn_w3, L1_ffn_b3), axis=-1)
    return x

_drawn_inputs = setup_inputs


def setup_inputs(seed=0):
    import zlib

    import numpy as np

    out = dict(_drawn_inputs(seed))
    spreads = {'L1_attn_b_attn': (0.0, 0.1), 'L1_attn_b_proj': (0.0, 0.1)}
    factors = {'L0_ffn_b12': 8.0, 'L0_ffn_b3': 6.205, 'L1_ffn_b12': 8.0, 'L1_ffn_b3': 6.486}
    for name, (base, spread) in spreads.items():
        noise = np.random.default_rng([zlib.crc32(name.encode()), seed]).standard_normal(out[name].shape)
        drawn = base * np.exp(spread * noise) if base else spread * noise
        out[name] = jnp.asarray(drawn.astype(out[name].dtype))
    for name, factor in factors.items():
        out[name] = (out[name] * factor).astype(out[name].dtype)
    return out
```

```python
import numpy as np
import concourse.bass as bass
from concourse import mybir
from contextlib import ExitStack

P = 128
BATCH, SEQ, HID = 4, 512, 512
U = 2
HALVES = BATCH // U
TT = SEQ // P
HC = HID // P
GROUPS, QH, HD = 8, 4, 128
L0_SCALE = float(HD) ** -0.5
STEPS = GROUPS * U
H1, D1 = 32, 16
CH = HID // P
HPC = P // D1
LAYERS = 2
BIG = 3.0e38
EPS = 1e-5
RSQRT_MAGIC = 1597463007.0


def build(nc, x, wq, wkv, wo, w12, b12, w3, wc, battn, wproj, bias_rows, rope, mask0, rel, slopes, ident, headmask, out):
    f32, f32r, i32 = mybir.dt.float32, mybir.dt.float32r, mybir.dt.int32
    ALU, ACT = mybir.AluOpType, mybir.ActivationFunctionType
    ctx = ExitStack()
    with ctx:
        def sb(name, shape, dt=f32):
            return ctx.enter_context(nc.sbuf_tensor(name, shape, dt))

        def sem(name):
            return ctx.enter_context(nc.semaphore(name))

        stage = sb("stage", [P, 2, 1024])
        w_h = {s: sb(f"w{s}_h", [P, HC * 512], f32r) for s in ("q0", "q1", "o", "kv")}
        w_l = {s: sb(f"w{s}_l", [P, HC * 512], f32r) for s in ("q0", "q1", "o", "kv")}
        xn = sb("xn", [P, U, TT, HID])
        xT_h = sb("xT_h", [P, U, HC, SEQ], f32r)
        xT_l = sb("xT_l", [P, U, HC, SEQ], f32r)
        k_h = sb("k_h", [P, 2, SEQ], f32r)
        k_l = sb("k_l", [P, 2, SEQ], f32r)
        q_h = sb("q_h", [P, 2, SEQ], f32r)
        q_l = sb("q_l", [P, 2, SEQ], f32r)
        v_hl = sb("v_hl", [P, 2, 2, TT, P], f32r)
        pT_h = sb("pT_h", [P, 2, 7 * P], f32r)
        pT_l = sb("pT_l", [P, 2, 7 * P], f32r)
        aT_h = sb("aT_h", [P, 4, SEQ], f32r)
        aT_l = sb("aT_l", [P, 4, SEQ], f32r)
        probs = sb("probs", [P, 2, 4, 256])
        probs1 = probs[:, :, :, :].rearrange("p a i k -> p (a i k)").rearrange("p (b k) -> p b k", k=512)
        work = sb("work", [P, 5, 512])
        cos_t = sb("cos_t", [P, SEQ])
        sin_t = sb("sin_t", [P, SEQ])
        mask_t = sb("mask_t", [P, 256])
        rel_t = sb("rel_t", [P, 512])
        ident_t = sb("ident_t", [P, P])
        slopes_t = sb("slopes_t", [P, H1])
        headmask_t = sb("headmask_t", [P, 2])
        bias_t = sb("bias_t", [P, HID])
        b12_t = sb("b12_t", [P, LAYERS, 8])
        nb12_t = sb("nb12_t", [P, LAYERS, 8])
        battn_t = sb("battn_t", [P, 12])
        negmax = sb("negmax", [P, 32])
        sums = sb("sums", [P, 32])
        recips = sb("recips", [P, 32])
        stats = sb("stats", [P, TT, 6])
        meanvar = sb("meanvar", [P, TT, 2])
        newton = sb("newton", [P, 4, TT])

        bank = [ctx.enter_context(nc.psum_tensor(f"bank{i}", [P, 512], f32)) for i in range(8)]
        A, S, T, O = bank[0:2], bank[2:4], bank[4:6], bank[6:8]

        s_const = sem("constants_loaded")
        s_nb = sem("negated_bias_ready")
        s_stage = [sem(f"stage_full{i}") for i in range(2)]
        s_stage_free = [sem(f"stage_free{i}") for i in range(2)]
        slots = ("q0", "q1", "o", "kv0", "kv1", "m")
        s_w = {s: sem(f"weights_ready_{s}") for s in slots}
        s_w_free = {s: sem(f"weights_used_{s}") for s in slots}
        s_split = sem("split_high_done")
        s_x = [sem(f"x_loaded{u}") for u in range(U)]
        s_store = [sem(f"out_stored{u}") for u in range(U)]
        s_bias = sem("bias_row_loaded")
        s_bias_used = sem("bias_row_used")
        s_biased = sem("residual_biased")
        s_ln = sem("layernorm_done")
        s_tr_done = sem("transposed_x")
        s_tr = [sem(f"xT_bank_full{i}") for i in range(2)]
        s_tr_h = sem("xT_high_done")
        s_xT = sem("xT_ready")
        s_tr_free = [sem(f"xT_bank_free{i}") for i in range(2)]
        s_a = [sem(f"proj_bank_full{i}") for i in range(2)]
        s_a_free = [sem(f"proj_bank_free{i}") for i in range(2)]
        s_s = [sem(f"score_bank_full{i}") for i in range(2)]
        s_s_free = [sem(f"score_bank_free{i}") for i in range(2)]
        s_t = [sem(f"transpose_bank_full{i}") for i in range(2)]
        s_t_free = [sem(f"transpose_bank_free{i}") for i in range(2)]
        s_o = [sem(f"out_bank_full{i}") for i in range(2)]
        s_o_free = [sem(f"out_bank_free{i}") for i in range(2)]
        s_swap = [sem(f"swapped{i}") for i in range(2)]
        s_swap_free = [sem(f"swapped_free{i}") for i in range(2)]
        s_rot = sem("rotated")
        s_rot_h = sem("rotated_high_done")
        s_k = sem("k_ready")
        s_q = sem("q_ready")
        s_vT = sem("vT_copied")
        s_v_h = sem("v_high_done")
        s_v = sem("v_ready")
        s_masked = sem("scores_masked")
        s_exp = sem("exp_done")
        s_p = sem("probs_ready")
        s_pT_h = sem("pT_high_done")
        s_pT = sem("pT_ready")
        s_aT_h = sem("aT_high_done")
        s_aT = sem("aT_ready")
        s_h = [sem(f"ffn_up_bank_full{i}") for i in range(2)]
        s_h_free = [sem(f"ffn_up_bank_free{i}") for i in range(2)]
        s_e = sem("ffn_exp_done")
        s_g = sem("gated_done")
        s_g_h = sem("gated_high_done")
        s_gT = sem("gated_ready")
        s_d = [sem(f"ffn_down_bank_full{i}") for i in range(2)]
        s_d_free = [sem(f"ffn_down_bank_free{i}") for i in range(2)]
        s1_t = [sem(f"l1_transpose_bank_full{i}") for i in range(2)]
        s1_t_free = [sem(f"l1_transpose_bank_free{i}") for i in range(2)]
        s1_raw = sem("l1_qk_copied")
        s1_high = sem("l1_high_done")
        s1_qkv = sem("l1_qkv_ready")
        s1_vT = sem("l1_vT_copied")
        s1_s = [sem(f"l1_score_bank_full{i}") for i in range(4)]
        s1_s_free = [sem(f"l1_score_bank_free{i}") for i in range(4)]
        s1_tab = sem("alibi_table_ready")
        s1_masked = sem("l1_scores_masked")
        s1_exp = sem("l1_exp_done")
        s1_p_free = [sem(f"l1_probs_used{i}") for i in range(4)]
        s1_pT_h = sem("l1_pT_high_done")
        s1_pT = sem("l1_pT_ready")
        s1_o = sem("l1_out_full")
        s1_o_low = sem("l1_out_low_copied")
        s1_o_free = sem("l1_out_free")
        s1_nat = sem("l1_out_normalised")
        s1_aT_h = sem("l1_aT_high_done")
        s1_aT = sem("l1_aT_ready")
        s1_pr = sem("l1_proj_full")
        s1_pr_free = sem("l1_proj_used")
        c_dve = sem("vector_chain")
        N_CONST = 10
        s_seen = {e: sem(f"wait_passed_{e}") for e in ("dve", "pool", "pe")}

        def free(eng, s, uses):
            eng.wait_ge(s, uses + 1)

        def word(ap):
            return ap.bitcast(f32)

        FILLS = {"q0": 4 + 1 + 4 + 1, "q1": 4 + 1 + 1, "o": 8 + 3, "kv0": 4, "kv1": 4, "m": 4}

        block = ctx.enter_context(nc.Block())

        @block.sync
        def _(sp):
            for dst, src in ((cos_t, rope[0]), (sin_t, rope[1]), (mask_t, mask0), (rel_t, rel), (ident_t, ident),
                             (slopes_t, slopes), (headmask_t, headmask), (battn_t, battn)):
                sp.dma_start(dst[:, :], src).then_inc(s_const, 16)
            for n in range(LAYERS):
                sp.dma_start(b12_t[:, n, :], b12[n]).then_inc(s_const, 16)

            def load(m, src, cols):
                for i in range(2):
                    free(sp, s_stage_free[i], m)
                    sp.dma_start(stage[:, i, 0:cols // 2], src[:, i * (cols // 2):(i + 1) * (cols // 2)]) \
                        .then_inc(s_stage[i], 16)

            def load_bias(k, row):
                free(sp, s_bias_used, k)
                sp.dma_start(bias_t[:, :], bias_rows[row]).then_inc(s_bias, 16)

            for s in (*s_stage_free, s_bias_used):
                sp.sem_inc(s, 1)
            with sp.Fori(0, HALVES) as hf:
                base = sp.snap(hf * SLABS)
                with sp.Fori(0, GROUPS // 2) as g2:
                    ms = [sp.snap(base + g2 * 6 + k) for k in range(6)]
                    gs = [sp.snap(g2 * 2 + p) for p in range(2)]
                    for p in range(2):
                        load(ms[3 * p], wkv[gs[p]], 1024)
                        load(ms[3 * p + 1], wq[gs[p]], 2048)
                        load(ms[3 * p + 2], wo[gs[p]], 2048)
                bias0 = sp.snap(hf * 3)
                m = [sp.snap(base + 24 + k) for k in range(SLABS - 24)]
                b1, b2 = sp.snap(bias0 + 1), sp.snap(bias0 + 2)
                load(m[0], w12[0, 0], 2048)
                load(m[1], w12[0, 1], 2048)
                load(m[2], w3[0], 2048)
                load(m[3], wc[0], 1536)
                load_bias(bias0, 0)
                load(m[4], wc[1], 1536)
                load(m[5], w12[1, 0], 2048)
                load(m[6], wproj, 2048)
                load_bias(b1, 1)
                for k in range(6):
                    load(m[7 + k], wc[(2 + k) % CH], 1536)
                load(m[13], w12[1, 1], 2048)
                load(m[14], w3[1], 2048)
                load_bias(b2, 2)

        @block.gpsimd
        def _(pool):
            def split(m, slot, fill, cols, also=()):
                free(pool, s_w_free[slot], fill)
                for name, val in also:
                    free(pool, s_w_free[name], val)
                key = {"kv0": "kv", "kv1": "kv", "m": "kv"}.get(slot, slot)
                off = 1024 if slot == "kv1" else 0
                for i in range(2):
                    part = slice(off + i * (cols // 2), off + (i + 1) * (cols // 2))
                    src = stage[:, i, 0:cols // 2]
                    pool.wait_ge(s_stage[i], 16 * m + 16)
                    pool.sem_inc(s_seen["pool"], 1)
                    nc.gpsimd.tensor_copy(w_h[key][:, part], src).then_inc(s_split, 1)
                    pool.wait_ge(s_split, 2 * m + i + 1)
                    low = nc.gpsimd.tensor_tensor(w_l[key][:, part], src, word(w_h[key][:, part]), ALU.subtract)
                    low.then_inc(s_stage_free[i], 1)
                    if i == 1:
                        free(pool, s_stage_free[1], m + 1)
                        pool.sem_inc(s_w[slot], 1)

            def add_bias(hf, k, stage_no):
                pool.wait_ge(s_bias, hf * 48 + 16 * k + 16)
                for u in range(U):
                    pool.wait_ge(s_tr_done, hf * 8 + stage_no * 2 + u + 1)
                    bc = bias_t[:, :]
                    for t in range(TT):
                        last = nc.gpsimd.tensor_tensor(xn[:, u, t, :], xn[:, u, t, :], bc, ALU.add)
                        last.then_inc(s_biased, 1)
                pool.wait_ge(s_biased, hf * 24 + k * 8 + 8)
                pool.sem_inc(s_bias_used, 1)

            for s in s_w_free.values():
                pool.sem_inc(s, 1)
            with pool.Fori(0, HALVES) as hf:
                f = {s: hf * FILLS[s] for s in FILLS}
                with pool.Fori(0, GROUPS // 2) as g2:
                    m = hf * SLABS + g2 * 6
                    for p in range(2):
                        split(m + 3 * p, f"kv{p}", f[f"kv{p}"] + g2, 1024, also=[("m", f["m"])])
                        split(m + 3 * p + 1, f"q{p}", f[f"q{p}"] + g2, 2048)
                        split(m + 3 * p + 2, "o", f["o"] + g2 * 2 + p, 2048)
                m = hf * SLABS + 24
                split(m, "q0", f["q0"] + 4, 2048)
                split(m + 1, "q1", f["q1"] + 4, 2048)
                split(m + 2, "o", f["o"] + 8, 2048)
                split(m + 3, "m", f["m"], 1536, also=[("kv0", f["kv0"] + 4), ("kv1", f["kv1"] + 4)])
                add_bias(hf, 0, 1)
                split(m + 4, "q0", f["q0"] + 5, 1536)
                split(m + 5, "q1", f["q1"] + 5, 2048)
                split(m + 6, "o", f["o"] + 9, 2048)
                add_bias(hf, 1, 2)
                for k in range(6):
                    split(m + 7 + k, ("m", "q0")[k % 2], f["m"] + 1 + k // 2 if k % 2 == 0 else f["q0"] + 6 + k // 2, 1536)
                split(m + 13, "q0", f["q0"] + 9, 2048)
                split(m + 14, "o", f["o"] + 10, 2048)
                add_bias(hf, 2, 3)

        def three(out_ap, ah, al, bh, bl, first=True, last=True, skip=False):
            nc.tensor.matmul(out_ap, ah, bh, start=first, stop=False, skip_group_check=skip)
            nc.tensor.matmul(out_ap, ah, bl, start=False, stop=False, skip_group_check=skip)
            return nc.tensor.matmul(out_ap, al, bh, start=False, stop=last, skip_group_check=skip)

        def project(out_ap, key, width, col, u, off=0):
            for c in range(HC):
                a = off + c * width + col
                last = three(out_ap, w_h[key][:, a:a + P], w_l[key][:, a:a + P],
                             xT_h[:, u, c, :], xT_l[:, u, c, :], c == 0, c == HC - 1)
            return last

        def down(out_ap, key, t):
            for c in range(4):
                last = three(out_ap, aT_h[:, c, t * P:(t + 1) * P], aT_l[:, c, t * P:(t + 1) * P],
                             w_h[key][:, c * 512:(c + 1) * 512], w_l[key][:, c * 512:(c + 1) * 512],
                             c == 0, c == 3)
            return last

        T_BLOCKS = [[(0, 0), (1, 0), (1, 1), (2, 1)], [(2, 2), (3, 2), (3, 3)]]

        @block.tensor
        def _(pe):
            pe.wait_ge(s_const, 16 * N_CONST)

            def transpose_x(hf, st, u):
                if st == 0:
                    pe.wait_ge(s_x[u], hf * 16 + 16)
                else:
                    pe.wait_ge(s_ln, hf * 8 + (st - 1) * 2 + u + 1)
                for c in range(HC):
                    free(pe, s_tr_free[c % 2], (hf * 8 + st * 2 + u) * 2 + c // 2)
                    for t in range(TT):
                        last = nc.tensor.transpose(T[c % 2][:, t * P:(t + 1) * P], xn[:, u, t, c * P:(c + 1) * P],
                                                   ident_t[:, :])
                    last.then_inc(s_tr[c % 2], 1)
                pe.wait_ge(s_tr[1], (hf * 8 + st * 2 + u) * 2 + 2)
                pe.sem_inc(s_tr_done, 1)

            def l0_step(n, hf, g, p, u, front, back):
                n1 = n - 1 if back else None
                pb, ub = (p if u == 1 else 1 - p), 1 - u

                def kv():
                    pe.wait_ge(s_w[f"kv{p}"], hf * FILLS["kv0"] + g + 1)
                    free(pe, s_a_free[0], 3 * n)
                    project(A[0][:, :], "kv", 256, 0, u, off=1024 * p).then_inc(s_a[0], 1)
                    free(pe, s_a_free[1], 3 * n)
                    last = project(A[1][:, :], "kv", 256, P, u, off=1024 * p)
                    last.then_inc(s_a[1], 1)
                    if u == 1:
                        pe.wait_ge(s_a[1], 3 * n + 1)
                        pe.sem_inc(s_w_free[f"kv{p}"], 1)

                def q(h):
                    if h == 0:
                        pe.wait_ge(s_w[f"q{p}"], hf * FILLS[f"q{p}"] + g + 1)
                    free(pe, s_a_free[h % 2], 3 * n + 1 + h // 2)
                    project(A[h % 2][:, :], f"q{p}", 512, h * P, u).then_inc(s_a[h % 2], 1)
                    if h == 3 and u == 1:
                        pe.wait_ge(s_a[1], 3 * n + 3)
                        pe.sem_inc(s_w_free[f"q{p}"], 1)

                def scores(n, h, u):
                    pe.wait_ge(s_q, 4 * n + h + 1)
                    if h == 0:
                        pe.wait_ge(s_k, n + 1)
                    for i in range(TT):
                        if i % 2 == 0:
                            free(pe, s_s_free[i // 2], 4 * n + h)
                        lo = P if i == 0 else 0
                        k0 = (i - 1) * P + lo
                        last = three(S[i // 2][:, (i % 2) * 256 + lo:(i % 2) * 256 + 256],
                                     q_h[:, h % 2, i * P:(i + 1) * P], q_l[:, h % 2, i * P:(i + 1) * P],
                                     k_h[:, u, k0:(i + 1) * P], k_l[:, u, k0:(i + 1) * P])
                        if i % 2 == 1:
                            last.then_inc(s_s[i // 2], 1)

                def transposes(n, h):
                    pe.wait_ge(s_p, 4 * n + h + 1)
                    for b in range(2):
                        free(pe, s_t_free[b], (5 * n + 1 + h) if b == 0 else (4 * n + h))
                        for k, (i, j) in enumerate(T_BLOCKS[b]):
                            c0 = (j - i + 1) * P
                            last = nc.tensor.transpose(T[b][:, k * P:(k + 1) * P],
                                                       probs[:, h % 2, i, c0:c0 + P], ident_t[:, :])
                        last.then_inc(s_t[b], 1)

                def v_transposes():
                    pe.wait_ge(s_vT, n + 1)
                    free(pe, s_t_free[0], 5 * n)
                    for t in range(TT):
                        last = nc.tensor.transpose(T[0][:, t * P:(t + 1) * P], work[:, 4, t * P:(t + 1) * P],
                                                   ident_t[:, :])
                    last.then_inc(s_t[0], 1)

                def pv(n, h, u):
                    b = h % 2
                    pe.wait_ge(s_pT, 4 * n + h + 1)
                    if h == 0:
                        pe.wait_ge(s_v, n + 1)
                    free(pe, s_o_free[b], 4 * n + h // 2)
                    for j in range(TT):
                        w = 2 * P if j < 3 else P
                        seg = slice(j * 2 * P, j * 2 * P + w)
                        last = three(O[b][:, j * P:j * P + w], v_hl[:, u, 0, j, :], v_hl[:, u, 1, j, :],
                                     pT_h[:, h % 2, seg], pT_l[:, h % 2, seg], j == 0, j == 3, skip=True)
                    last.then_inc(s_o[b], 1)

                def wo_tile(n, t):
                    b = t % 2
                    if t == 0:
                        pe.wait_ge(s_aT, 4 * n + 4)
                        pe.wait_ge(s_w["o"], hf * FILLS["o"] + (g * 2 + p if u == 1 else g * 2 + p - 1) + 1)
                    free(pe, s_o_free[b], 4 * n + 2 + t // 2)
                    down(O[b][:, :], "o", t).then_inc(s_o[b], 1)
                    if t == 3 and ub == 1:
                        pe.wait_ge(s_o[1], 4 * n + 4)
                        pe.sem_inc(s_w_free["o"], 1)

                if front:
                    kv()
                if back:
                    scores(n1, 3, ub)
                if front:
                    q(0)
                if back:
                    transposes(n1, 2)
                    pv(n1, 1, ub)
                if front:
                    q(1)
                    scores(n, 0, u)
                if back:
                    transposes(n1, 3)
                if front:
                    v_transposes()
                if back:
                    pv(n1, 2, ub)
                if front:
                    q(2)
                    scores(n, 1, u)
                if back:
                    pv(n1, 3, ub)
                if front:
                    transposes(n, 0)
                if back:
                    wo_tile(n1, 0)
                    wo_tile(n1, 1)
                if front:
                    q(3)
                    scores(n, 2, u)
                    transposes(n, 1)
                if back:
                    wo_tile(n1, 2)
                    wo_tile(n1, 3)
                if front:
                    pv(n, 0, u)

            def ffn_up(hf, layer, u):
                f = hf * 4 + layer * 2 + u
                pe.wait_ge(s_xT, (hf * 8 + (2 * layer + 1) * 2 + u) * 4 + 4)
                if layer == 1:
                    free(pe, s1_pr_free, hf * 8 + 8)
                for m in range(4):
                    key = (("q0", "q1"), ("q1", "q0"))[layer][m // 2]
                    fills = {("q0", 0): 5, ("q1", 0): 5, ("q1", 1): 6, ("q0", 1): 10}[key, layer]
                    if m % 2 == 0:
                        pe.wait_ge(s_w[key], hf * FILLS[key] + fills)
                    free(pe, s_h_free[m % 2], 2 * f + m // 2)
                    b = (A, S)[m % 2]
                    project(b[0][:, :], key, 512, (m % 2) * P, u)
                    project(b[1][:, :], key, 512, 256 + (m % 2) * P, u).then_inc(s_h[m % 2], 1)
                    if m % 2 == 1 and u == 1:
                        pe.wait_ge(s_h[1], 2 * f + m // 2 + 1)
                        pe.sem_inc(s_w_free[key], 1)

            def ffn_down(hf, layer, u):
                f = hf * 4 + layer * 2 + u
                pe.wait_ge(s_gT, 4 * f + 4)
                pe.wait_ge(s_w["o"], hf * FILLS["o"] + (9, 11)[layer])
                for t in range(TT):
                    free(pe, s_d_free[t % 2], 2 * f + t // 2)
                    down(O[t % 2][:, :], "o", t).then_inc(s_d[t % 2], 1)
                if u == 1:
                    pe.wait_ge(s_d[1], 2 * f + 2)
                    pe.sem_inc(s_w_free["o"], 1)

            def l1_chunk(hf, u, c2, cp):
                a = hf * 8 + u * 4 + c2 * 2 + cp
                slot, key = (("m", "kv"), ("q0", "q0"))[cp]
                done = hf * FILLS[slot] + u * 2 + c2 + (0, 5)[cp]
                pe.wait_ge(s_w[slot], done + 1)
                free(pe, s1_t_free[0], 19 * a)
                project(T[0][:, :], key, 384, 0, u).then_inc(s1_t[0], 1)
                free(pe, s1_t_free[1], 18 * a)
                project(T[1][:, :], key, 384, P, u).then_inc(s1_t[1], 1)
                free(pe, s1_t_free[0], 19 * a + 1)
                project(T[0][:, :], key, 384, 2 * P, u).then_inc(s1_t[0], 1)
                pe.wait_ge(s1_t[0], 19 * a + 2)
                pe.sem_inc(s_w_free[slot], 1)

                def scores(G):
                    par, i = divmod(G, 4)
                    for r in range(4):
                        free(pe, s1_s_free[r], 8 * a + G)
                    n = (i + 1) * P
                    rows = [slice(32 * r, 32 * r + 32) for r in range(4)]
                    qs = slice(i * P, (i + 1) * P)
                    for k, (qq, kk) in enumerate(((q_h, k_h), (q_h, k_l), (q_l, k_h))):
                        for r in range(4):
                            last = nc.tensor.matmul(bank[r][:, 0:n], qq[rows[r], par, qs], kk[rows[r], cp, 0:n],
                                                    start=k == 0, stop=k == 2)
                            if k == 2:
                                last.then_inc(s1_s[r], 1)

                def transposes(k):
                    G, r = divmod(k, 4)
                    i = G % 4
                    pe.wait_ge(s1_exp, 32 * a + k + 1)
                    free(pe, s1_t_free[k % 2], (19 * a + 2 if k % 2 == 0 else 18 * a + 2) + k // 2)
                    for j in range(i + 1):
                        last = nc.tensor.transpose(T[k % 2][:, j * P:(j + 1) * P], probs1[:, r, j * P:(j + 1) * P],
                                                   ident_t[:, :])
                    last.then_inc(s1_t[k % 2], 1)
                    pe.wait_ge(s1_t[k % 2], (19 * a + 3 if k % 2 == 0 else 18 * a + 3) + k // 2)
                    pe.sem_inc(s1_p_free[r], 1)

                def pv(k):
                    G, r = divmod(k, 4)
                    par, i = divmod(G, 4)
                    h = 2 * r + par
                    pe.wait_ge(s1_pT, 32 * a + k + 1)
                    if k == 0:
                        free(pe, s1_o_free, a)
                    ob = O[i // 2][:, (i % 2) * 256 + h * 32:(i % 2) * 256 + h * 32 + 32]
                    for j in range(i + 1):
                        ph = pT_h[:, k % 2, j * P:(j + 1) * P]
                        pl = pT_l[:, k % 2, j * P:(j + 1) * P]
                        nc.tensor.matmul(ob, ph, v_hl[:, cp, :, j, h * D1:(h + 1) * D1], start=j == 0, stop=False)
                        last = nc.tensor.matmul(ob[:, 0:D1], pl, v_hl[:, cp, 0, j, h * D1:(h + 1) * D1],
                                                start=False, stop=j == i)
                    if k == 31:
                        last.then_inc(s1_o, 1)

                pe.wait_ge(s1_qkv, 3 * a + 2)
                free(pe, s1_pr_free, hf * 8 + u * 4)
                scores(0)
                pe.wait_ge(s1_vT, a + 1)
                free(pe, s1_t_free[1], 18 * a + 1)
                for t in range(TT):
                    last = nc.tensor.transpose(T[1][:, t * P:(t + 1) * P], probs1[:, 0, t * P:(t + 1) * P], ident_t[:, :])
                last.then_inc(s1_t[1], 1)
                for k in range(32):
                    if k % 4 == 0 and k < 28:
                        scores(k // 4 + 1)
                    transposes(k)
                    if k == 1:
                        pe.wait_ge(s1_qkv, 3 * a + 3)
                    if k > 0:
                        pv(k - 1)
                pv(31)
                pe.wait_ge(s1_nat, a + 1)
                free(pe, s1_t_free[0], 19 * a + 18)
                for t in range(TT):
                    last = nc.tensor.transpose(T[0][:, t * P:(t + 1) * P], work[:, 4, t * P:(t + 1) * P], ident_t[:, :])
                last.then_inc(s1_t[0], 1)

            for s in (*s_tr_free, *s_a_free, *s_s_free, *s_t_free, *s_o_free, *s_h_free, *s_d_free, *s1_t_free, *s1_s_free,
                      s1_o_free, s1_pr_free):
                pe.sem_inc(s, 1)
            with pe.Fori(0, HALVES) as hf:
                for u in range(U):
                    transpose_x(hf, 0, u)
                pe.wait_ge(s_xT, hf * 32 + 8)
                n0 = hf * STEPS
                l0_step(n0, hf, 0, 0, 0, True, False)
                l0_step(n0 + 1, hf, 0, 0, 1, True, True)
                l0_step(n0 + 2, hf, 0, 1, 0, True, True)
                l0_step(n0 + 3, hf, 0, 1, 1, True, True)
                with pe.Fori(1, GROUPS // 2) as g2:
                    for s in range(4):
                        l0_step(n0 + g2 * 4 + s, hf, g2, s // 2, s % 2, True, True)
                l0_step(n0 + STEPS, hf, GROUPS // 2, 0, 0, False, True)

                def ffn(layer):
                    st = 2 * layer + 1
                    transpose_x(hf, st, 0)
                    ffn_up(hf, layer, 0)
                    transpose_x(hf, st, 1)
                    ffn_down(hf, layer, 0)
                    ffn_up(hf, layer, 1)
                    ffn_down(hf, layer, 1)

                ffn(0)
                transpose_x(hf, 2, 0)
                transpose_x(hf, 2, 1)
                pe.wait_ge(s_xT, (hf * 8 + 6) * 4)
                pe.sem_inc(s_seen["pe"], 1)
                with pe.Fori(0, U) as u:
                    with pe.Fori(0, CH // 2) as c2:
                        for cp in range(2):
                            l1_chunk(hf, u, c2, cp)
                    pe.wait_ge(s1_aT, hf * 8 + u * 4 + 4)
                    pe.wait_ge(s_w["o"], hf * FILLS["o"] + 10)
                    for t in range(TT):
                        down(bank[t][:, :], "o", t).then_inc(s1_pr, 1)
                pe.wait_ge(s1_pr, hf * 8 + 8)
                pe.sem_inc(s_w_free["o"], 1)
                ffn(1)

        @block.scalar
        def _(act):
            act.wait_ge(s_const, 16 * N_CONST)
            act.wait_ge(s_nb, 1)

            def copy(dst, src):
                return nc.scalar.activation(dst, src, ACT.Copy)

            def transpose_x(hf, st, u):
                for c in range(HC):
                    act.wait_ge(s_tr[c % 2], (hf * 8 + st * 2 + u) * 2 + c // 2 + 1)
                    copy(xT_h[:, u, c, :], T[c % 2][:, :]).then_inc(s_tr_h, 1)

            def l0_step(n, u, front, back):
                n1 = n - 1 if back else None
                ub = 1 - u

                def swap(item):
                    b = 0 if item == 0 else (item - 1) % 2
                    use = 3 * n if item == 0 else 3 * n + 1 + (item - 1) // 2
                    sbuf = item % 2
                    sidx = (3 * n + item // 2) if sbuf == 0 else (2 * n + item // 2)
                    act.wait_ge(s_a[b], use + 1)
                    free(act, s_swap_free[sbuf], sidx)
                    copy(work[0:64, sbuf, :], A[b][64:128, :])
                    copy(work[64:128, sbuf, :], A[b][0:64, :]).then_inc(s_swap[sbuf], 1)

                def high(item):
                    dst = k_h[:, u, :] if item == 0 else q_h[:, (item - 1) % 2, :]
                    act.wait_ge(s_rot, 5 * n + item + 1)
                    copy(dst, work[:, 2 + item % 2, :]).then_inc(s_rot_h, 1)

                def v_copy():
                    act.wait_ge(s_a[1], 3 * n + 1)
                    copy(work[:, 4, :], A[1][:, :]).then_inc(s_vT, 1)
                    act.wait_ge(s_vT, n + 1)
                    act.sem_inc(s_a_free[1], 1)

                def exps(n, h):
                    for i in range(TT):
                        lo = P if i == 0 else 0
                        act.wait_ge(s_masked, 16 * n + 4 * h + i + 1)
                        col = (h % 2) * 4 + i
                        nc.scalar.activation(probs[:, h % 2, i, lo:256], probs[:, h % 2, i, lo:256], ACT.Exp,
                                             bias=negmax[:, col:col + 1], scale=-1.0,
                                             accum_out=sums[:, col:col + 1]).then_inc(s_exp, 1)

                def pT_high(n, h):
                    for b in range(2):
                        act.wait_ge(s_t[b], (5 * n + 2 + h) if b == 0 else (4 * n + h + 1))
                        w = len(T_BLOCKS[b]) * P
                        copy(pT_h[:, h % 2, b * 512:b * 512 + w], T[b][:, 0:w]).then_inc(s_pT_h, 1)

                def v_high():
                    act.wait_ge(s_t[0], 5 * n + 1)
                    copy(v_hl[:, u, 0, :, :], T[0][:, :].rearrange("p (t d) -> p t d", d=P)).then_inc(s_v_h, 1)

                def aT_high(n, h):
                    act.wait_ge(s_o[h % 2], 4 * n + h // 2 + 1)
                    copy(aT_h[:, h, :], O[h % 2][:, :]).then_inc(s_aT_h, 1)

                if front:
                    swap(0)
                    v_copy()
                    high(0)
                if back:
                    exps(n1, 3)
                if front:
                    swap(1)
                if back:
                    pT_high(n1, 2)
                if front:
                    high(1)
                if back:
                    aT_high(n1, 1)
                if front:
                    swap(2)
                    exps(n, 0)
                    high(2)
                if back:
                    pT_high(n1, 3)
                if front:
                    v_high()
                if back:
                    aT_high(n1, 2)
                if front:
                    swap(3)
                    exps(n, 1)
                    high(3)
                if back:
                    aT_high(n1, 3)
                if front:
                    pT_high(n, 0)
                    swap(4)
                    exps(n, 2)
                    high(4)
                    pT_high(n, 1)
                    aT_high(n, 0)

            def ffn_up(hf, layer, u):
                f = hf * 4 + layer * 2 + u
                for m in range(4):
                    b = (A, S)[m % 2]
                    act.wait_ge(s_h[m % 2], 2 * f + m // 2 + 1)
                    if m >= 2:
                        act.wait_ge(s_g, 4 * f + m - 1)
                    nc.scalar.activation(work[:, m % 2, :], b[0][:, :], ACT.Exp, scale=-1.0,
                                         bias=nb12_t[:, layer, m:m + 1]).then_inc(s_e, 1)
                    if m >= 1:
                        gated_high(f, m - 1)
                gated_high(f, 3)

            def gated_high(f, m):
                act.wait_ge(s_g, 4 * f + m + 1)
                copy(aT_h[:, m, :], work[:, 2 + m % 2, :]).then_inc(s_g_h, 1)

            def l1_chunk(hf, u, c2, cp):
                a = hf * 8 + u * 4 + c2 * 2 + cp
                cc = c2 * 2 + cp
                ident_f = ACT.Identity

                def table(r, par):
                    nc.scalar.activation(work[:, r, :], rel_t[:, :], ACT.Copy,
                                         scale=slopes_t[:, bass.ds(cc * HPC + 2 * r + par, 1)]).then_inc(s1_tab, 1)

                act.wait_ge(s1_t[0], 19 * a + 1)
                nc.scalar.activation(probs1[:, 1, :], T[0][:, :], ident_f,
                                     bias=battn_t[:, bass.ds(cc, 1)]).then_inc(s1_raw, 1)
                act.wait_ge(s1_raw, 2 * a + 1)
                act.sem_inc(s1_t_free[0], 1)
                for e in range(2):
                    nc.scalar.activation(q_h[:, e, :], probs1[:, 1, :], ACT.Copy,
                                         scale=headmask_t[:, e:e + 1]).then_inc(s1_high, 1)
                act.wait_ge(s1_t[1], 18 * a + 1)
                nc.scalar.activation(probs1[:, 2, :], T[1][:, :], ident_f,
                                     bias=battn_t[:, bass.ds(cc + CH, 1)]).then_inc(s1_raw, 1)
                act.wait_ge(s1_raw, 2 * a + 2)
                act.sem_inc(s1_t_free[1], 1)
                copy(k_h[:, cp, :], probs1[:, 2, :]).then_inc(s1_high, 1)
                act.wait_ge(s1_t[0], 19 * a + 2)
                nc.scalar.activation(probs1[:, 0, :], T[0][:, :], ident_f,
                                     bias=battn_t[:, bass.ds(cc + 2 * CH, 1)]).then_inc(s1_vT, 1)
                act.wait_ge(s1_vT, a + 1)
                act.sem_inc(s1_t_free[0], 1)
                for r in range(4):
                    table(r, 0)

                def exp(k):
                    G, r = divmod(k, 4)
                    par, i = divmod(G, 4)
                    w = (i + 1) * P
                    col = i * HPC + 2 * r + par
                    act.wait_ge(s1_masked, 32 * a + k + 1)
                    nc.scalar.activation(probs1[:, r, 0:w], probs1[:, r, 0:w], ACT.Exp, bias=negmax[:, k:k + 1],
                                         scale=-1.0, accum_out=sums[:, col:col + 1]).then_inc(s1_exp, 1)
                    if G == 3:
                        table(r, 1)

                def pT_high(k):
                    w = (k // 4 % 4 + 1) * P
                    act.wait_ge(s1_t[k % 2], (19 * a + 3 if k % 2 == 0 else 18 * a + 3) + k // 2)
                    copy(pT_h[:, k % 2, 0:w], T[k % 2][:, 0:w]).then_inc(s1_pT_h, 1)

                act.wait_ge(s1_t[1], 18 * a + 2)
                copy(v_hl[:, cp, 0, :, :], T[1][:, :].rearrange("p (t d) -> p t d", d=P)).then_inc(s1_high, 1)
                for k in range(4):
                    exp(k)
                for k in range(32):
                    pT_high(k)
                    if k + 4 < 32:
                        exp(k + 4)
                act.wait_ge(s1_o, a + 1)
                for b in range(2):
                    lowp = O[b][:, :].rearrange("p (i h e) -> p i h e", h=HPC, e=32)[:, :, :, D1:32]
                    dst = probs1[:, 3, b * 256:(b + 1) * 256].rearrange("p (i h e) -> p i h e", h=HPC, e=D1)
                    copy(dst, lowp).then_inc(s1_o_low, 1)
                act.wait_ge(s1_t[0], 19 * a + 19)
                copy(aT_h[:, bass.ds(cc, 1), :], T[0][:, :]).then_inc(s1_aT_h, 1)

            for s in s_swap_free:
                act.sem_inc(s, 1)
            with act.Fori(0, HALVES) as hf:
                for u in range(U):
                    act.dma_start(xn[:, u, :, :], x[hf * U + u]).then_inc(s_x[u], 16)
                transpose_x(hf, 0, 0)
                transpose_x(hf, 0, 1)
                n0 = hf * STEPS
                for s in range(4):
                    l0_step(n0 + s, s % 2, True, s > 0)
                with act.Fori(1, GROUPS // 2) as g2:
                    for s in range(4):
                        l0_step(n0 + g2 * 4 + s, s % 2, True, True)
                l0_step(n0 + STEPS, 0, False, True)

                def ffn(layer):
                    st = 2 * layer + 1
                    transpose_x(hf, st, 0)
                    ffn_up(hf, layer, 0)
                    transpose_x(hf, st, 1)
                    ffn_up(hf, layer, 1)

                ffn(0)
                transpose_x(hf, 2, 0)
                transpose_x(hf, 2, 1)
                with act.Fori(0, U) as u:
                    with act.Fori(0, CH // 2) as c2:
                        for cp in range(2):
                            l1_chunk(hf, u, c2, cp)
                ffn(1)
                for u in range(U):
                    act.wait_ge(s_ln, hf * 8 + 7 + u)
                    act.dma_start(out[hf * U + u], xn[:, u, :, :]).then_inc(s_store[u], 16)
                for u in range(U):
                    act.wait_ge(s_store[u], hf * 16 + 16)

        @block.vector
        def _(dve):
            count = [0]

            def link(ins):
                count[0] += 1
                ins.then_inc(c_dve, 1)
                dve.wait_ge(c_dve, count[0])

            def restart():
                if count[0]:
                    dve.sem_clear(c_dve)
                    count[0] = 0

            def low(dst, src, high):
                return nc.vector.tensor_tensor(dst, src, word(high), ALU.subtract)

            dve.wait_ge(s_const, 16 * N_CONST)
            nc.vector.tensor_scalar(nb12_t[:, :, :], b12_t[:, :, :], -1.0, None, ALU.mult).then_inc(s_nb, 1)

            def transpose_x(hf, st, u):
                for c in range(HC):
                    dve.wait_ge(s_tr_h, (hf * 8 + st * 2 + u) * 4 + c + 1)
                    low(xT_l[:, u, c, :], T[c % 2][:, :], xT_h[:, u, c, :]).then_inc(s_xT, 1)
                    dve.wait_ge(s_xT, (hf * 8 + st * 2 + u) * 4 + c + 1)
                    dve.sem_inc(s_tr_free[c % 2], 1)

            def l0_step(n, u, front, back):
                n1 = n - 1 if back else None
                ub = 1 - u

                def rotate(item):
                    b = 0 if item == 0 else (item - 1) % 2
                    sbuf = item % 2
                    sidx = (3 * n + item // 2) if sbuf == 0 else (2 * n + item // 2)
                    rot = work[:, 2 + item % 2, :]
                    dve.wait_ge(s_swap[sbuf], sidx + 1)
                    nc.vector.tensor_tensor(rot, A[b][:, :], cos_t[:, :], ALU.mult).then_inc(s_a_free[b], 1)
                    link(nc.vector.tensor_tensor(work[:, sbuf, :], work[:, sbuf, :], sin_t[:, :], ALU.mult))
                    nc.vector.tensor_tensor(rot, rot, work[:, sbuf, :], ALU.add).then_inc(s_rot, 1)
                    dve.wait_ge(s_rot, 5 * n + item + 1)
                    dve.sem_inc(s_swap_free[sbuf], 1)

                def rot_low(item):
                    dve.wait_ge(s_rot_h, 5 * n + item + 1)
                    rot = work[:, 2 + item % 2, :]
                    if item == 0:
                        low(k_l[:, u, :], rot, k_h[:, u, :]).then_inc(s_k, 1)
                    else:
                        q = (item - 1) % 2
                        low(q_l[:, q, :], rot, q_h[:, q, :]).then_inc(s_q, 1)

                def mask(n, h):
                    for i in range(TT):
                        lo = P if i == 0 else 0
                        col = (h % 2) * 4 + i
                        if i % 2 == 0:
                            dve.wait_ge(s_s[i // 2], 4 * n + h + 1)
                            dve.sem_inc(s_seen["dve"], 1)
                        nc.vector.tensor_tensor_reduce(
                            out=probs[:, h % 2, i, lo:256], in0=S[i // 2][:, (i % 2) * 256 + lo:(i % 2) * 256 + 256],
                            in1=mask_t[:, lo:256], scale=-L0_SCALE, scalar=BIG, op0=ALU.add, op1=ALU.min,
                            accum_out=negmax[:, col:col + 1]).then_inc(s_masked, 1)
                        if i % 2 == 1:
                            dve.wait_ge(s_masked, 16 * n + 4 * h + i + 1)
                            dve.sem_inc(s_s_free[i // 2], 1)

                def normalise(n, h):
                    c0 = (h % 2) * 4
                    dve.wait_ge(s_exp, 16 * n + 4 * h + 4)
                    link(nc.vector.reciprocal(recips[:, c0:c0 + 4], sums[:, c0:c0 + 4]))
                    for i in range(TT):
                        lo = P if i == 0 else 0
                        p = probs[:, h % 2, i, lo:256]
                        last = nc.vector.tensor_scalar(p, p, recips[:, c0 + i:c0 + i + 1], None, ALU.mult)
                    last.then_inc(s_p, 1)

                def pT_low(n, h):
                    for b in range(2):
                        w = len(T_BLOCKS[b]) * P
                        seg = slice(b * 512, b * 512 + w)
                        dve.wait_ge(s_pT_h, 8 * n + 2 * h + b + 1)
                        last = low(pT_l[:, h % 2, seg], T[b][:, 0:w], pT_h[:, h % 2, seg])
                        last.then_inc(s_t_free[b], 1)
                    free(dve, s_t_free[1], 4 * n + h + 1)
                    dve.sem_inc(s_pT, 1)

                def v_low():
                    dve.wait_ge(s_v_h, n + 1)
                    low(v_hl[:, u, 1, :, :], T[0][:, :].rearrange("p (t d) -> p t d", d=P),
                        v_hl[:, u, 0, :, :]).then_inc(s_v, 1)
                    dve.wait_ge(s_v, n + 1)
                    dve.sem_inc(s_t_free[0], 1)

                def aT_low(n, h):
                    dve.wait_ge(s_aT_h, 4 * n + h + 1)
                    low(aT_l[:, h, :], O[h % 2][:, :], aT_h[:, h, :]).then_inc(s_aT, 1)
                    dve.wait_ge(s_aT, 4 * n + h + 1)
                    dve.sem_inc(s_o_free[h % 2], 1)

                def accumulate(n, u, t):
                    dve.wait_ge(s_o[t % 2], 4 * n + 3 + t // 2)
                    nc.vector.tensor_tensor(xn[:, u, t, :], O[t % 2][:, :], xn[:, u, t, :], ALU.add)\
                        .then_inc(s_o_free[t % 2], 1)

                restart()
                if front:
                    rotate(0)
                    rot_low(0)
                if back:
                    mask(n1, 3)
                if front:
                    rotate(1)
                if back:
                    normalise(n1, 3)
                if front:
                    rot_low(1)
                if back:
                    pT_low(n1, 2)
                    aT_low(n1, 1)
                if front:
                    rotate(2)
                    mask(n, 0)
                    rot_low(2)
                if back:
                    pT_low(n1, 3)
                if front:
                    normalise(n, 0)
                    v_low()
                if back:
                    aT_low(n1, 2)
                if front:
                    rotate(3)
                    mask(n, 1)
                    rot_low(3)
                    normalise(n, 1)
                if back:
                    aT_low(n1, 3)
                if front:
                    pT_low(n, 0)
                if back:
                    accumulate(n1, ub, 0)
                    accumulate(n1, ub, 1)
                if front:
                    rotate(4)
                    mask(n, 2)
                    rot_low(4)
                    normalise(n, 2)
                    pT_low(n, 1)
                if back:
                    accumulate(n1, ub, 2)
                    accumulate(n1, ub, 3)
                if front:
                    aT_low(n, 0)

            def layernorm(u):
                for t in range(TT):
                    last = nc.vector.bn_stats(stats[:, t, :], xn[:, u, t, :])
                    if t == TT - 1:
                        link(last)
                for t in range(TT):
                    last = nc.vector.bn_aggr(meanvar[:, t, :], stats[:, t, :])
                link(last)
                var, y, y2, z = (newton[:, k, :] for k in range(4))
                link(nc.vector.tensor_scalar(var, meanvar[:, :, 1], EPS, None, ALU.add))
                link(nc.vector.tensor_scalar(y.bitcast(i32), var.bitcast(i32), 1, None, ALU.logical_shift_right))
                link(nc.vector.tensor_scalar(y.bitcast(i32), y.bitcast(i32), -1.0, RSQRT_MAGIC, ALU.mult, ALU.add))
                for _ in range(3):
                    link(nc.vector.tensor_tensor(y2, y, y, ALU.mult))
                    link(nc.vector.scalar_tensor_tensor(z, y2, -0.5, var, ALU.mult, ALU.mult))
                    link(nc.vector.scalar_tensor_tensor(y, z, 1.5, y, ALU.add, ALU.mult))
                for t in range(TT):
                    last = nc.vector.tensor_scalar(xn[:, u, t, :], xn[:, u, t, :], meanvar[:, t, 0:1],
                                                   newton[:, 1, t:t + 1], ALU.subtract, ALU.mult)
                last.then_inc(s_ln, 1)

            def ffn_up(hf, layer, u):
                f = hf * 4 + layer * 2 + u
                restart()

                def gated_low(m):
                    dve.wait_ge(s_g_h, 4 * f + m + 1)
                    low(aT_l[:, m, :], work[:, 2 + m % 2, :], aT_h[:, m, :]).then_inc(s_gT, 1)

                for m in range(4):
                    b = (A, S)[m % 2]
                    e = work[:, m % 2, :]
                    g = work[:, 2 + m % 2, :]
                    dve.wait_ge(s_e, 4 * f + m + 1)
                    link(nc.vector.tensor_scalar(e, e, 1.0, None, ALU.add))
                    link(nc.vector.reciprocal(e, e))
                    link(nc.vector.scalar_tensor_tensor(g, b[0][:, :], b12_t[:, layer, m:m + 1], e, ALU.add, ALU.mult))
                    nc.vector.scalar_tensor_tensor(g, b[1][:, :], b12_t[:, layer, 4 + m:5 + m], g,
                                                   ALU.add, ALU.mult).then_inc(s_g, 1)
                    dve.wait_ge(s_g, 4 * f + m + 1)
                    dve.sem_inc(s_h_free[m % 2], 1)
                    if m >= 1:
                        gated_low(m - 1)
                gated_low(3)

            def ffn_down(hf, layer, u):
                f = hf * 4 + layer * 2 + u
                restart()
                dve.wait_ge(s_biased, hf * 24 + layer * 16 + u * 4 + 4)
                for t in range(TT):
                    dve.wait_ge(s_d[t % 2], 2 * f + t // 2 + 1)
                    nc.vector.tensor_tensor(xn[:, u, t, :], O[t % 2][:, :], xn[:, u, t, :], ALU.add)\
                        .then_inc(s_d_free[t % 2], 1)
                free(dve, s_d_free[0], 2 * f + 2)
                free(dve, s_d_free[1], 2 * f + 2)
                layernorm(u)

            def l1_chunk(hf, u, c2, cp):
                a = hf * 8 + u * 4 + c2 * 2 + cp
                cc = c2 * 2 + cp
                restart()
                for e in range(2):
                    dve.wait_ge(s1_high, 4 * a + e + 1)
                    last = nc.vector.scalar_tensor_tensor(q_l[:, e, :], probs1[:, 1, :], headmask_t[:, e:e + 1],
                                                          word(q_h[:, e, :]), ALU.mult, ALU.subtract)
                last.then_inc(s1_qkv, 1)
                dve.wait_ge(s1_high, 4 * a + 3)
                low(k_l[:, cp, :], probs1[:, 2, :], k_h[:, cp, :]).then_inc(s1_qkv, 1)

                def mask(k):
                    G, r = divmod(k, 4)
                    par, i = divmod(G, 4)
                    w = (i + 1) * P
                    dve.wait_ge(s1_s[r], 8 * a + G + 1)
                    dve.wait_ge(s1_tab, 8 * a + 4 * par + r + 1)
                    free(dve, s1_p_free[r], 8 * a + G)
                    dve.sem_inc(s_seen["dve"], 1)
                    nc.vector.tensor_tensor_reduce(
                        out=probs1[:, r, 0:w], in0=bank[r][:, 0:w], in1=work[:, r, 512 - w:512],
                        scale=-1.0, scalar=BIG, op0=ALU.add, op1=ALU.min,
                        accum_out=negmax[:, k:k + 1]).then_inc(s1_masked, 1)
                    dve.wait_ge(s1_masked, 32 * a + k + 1)
                    dve.sem_inc(s1_s_free[r], 1)

                def pT_low(k):
                    w = (k // 4 % 4 + 1) * P
                    dve.wait_ge(s1_pT_h, 32 * a + k + 1)
                    low(pT_l[:, k % 2, 0:w], T[k % 2][:, 0:w], pT_h[:, k % 2, 0:w]).then_inc(s1_pT, 1)
                    dve.wait_ge(s1_pT, 32 * a + k + 1)
                    dve.sem_inc(s1_t_free[k % 2], 1)

                dve.wait_ge(s1_high, 4 * a + 4)
                low(v_hl[:, cp, 1, :, :], T[1][:, :].rearrange("p (t d) -> p t d", d=P),
                    v_hl[:, cp, 0, :, :]).then_inc(s1_qkv, 1)
                dve.wait_ge(s1_qkv, 3 * a + 3)
                dve.sem_inc(s1_t_free[1], 1)
                for k in range(4):
                    mask(k)
                for k in range(32):
                    if k + 4 < 32:
                        mask(k + 4)
                    pT_low(k)
                nat = work[:, 4, :].rearrange("p (i h e) -> p i h e", h=HPC, e=D1)
                for b in range(2):
                    dve.wait_ge(s1_o_low, 2 * a + b + 1)
                    hi = O[b][:, :].rearrange("p (i h e) -> p i h e", h=HPC, e=32)[:, :, :, 0:D1]
                    lo = probs1[:, 3, b * 256:(b + 1) * 256].rearrange("p (i h e) -> p i h e", h=HPC, e=D1)
                    last = nc.vector.tensor_tensor(nat[:, 2 * b:2 * b + 2, :, :], hi, lo, ALU.add)
                link(last)
                dve.sem_inc(s1_o_free, 1)
                link(nc.vector.reciprocal(recips[:, :], sums[:, :]))
                n2 = work[:, 4, :].rearrange("p (s e) -> p s e", e=D1)
                nc.vector.tensor_tensor(n2, n2, recips[:, :].unsqueeze(2).to_broadcast([P, 32, D1]),
                                        ALU.mult).then_inc(s1_nat, 1)
                dve.wait_ge(s1_aT_h, a + 1)
                low(aT_l[:, bass.ds(cc, 1), :], T[0][:, :], aT_h[:, bass.ds(cc, 1), :]).then_inc(s1_aT, 1)
                dve.wait_ge(s1_aT, a + 1)
                dve.sem_inc(s1_t_free[0], 1)

            def l1_residual(hf, u):
                dve.wait_ge(s_biased, hf * 24 + 8 + u * 4 + 4)
                for t in range(TT):
                    dve.wait_ge(s1_pr, hf * 8 + u * 4 + t + 1)
                    nc.vector.tensor_tensor(xn[:, u, t, :], bank[t][:, :], xn[:, u, t, :], ALU.add)\
                        .then_inc(s1_pr_free, 1)
                free(dve, s1_pr_free, hf * 8 + u * 4 + 4)
                dve.sem_inc(s_seen["dve"], 1)
                layernorm(u)

            for s in s1_p_free:
                dve.sem_inc(s, 1)
            with dve.Fori(0, HALVES) as hf:
                restart()
                transpose_x(hf, 0, 0)
                transpose_x(hf, 0, 1)
                n0 = hf * STEPS
                for s in range(4):
                    l0_step(n0 + s, s % 2, True, s > 0)
                restart()
                with dve.Fori(1, GROUPS // 2) as g2:
                    for s in range(4):
                        l0_step(n0 + g2 * 4 + s, s % 2, True, True)
                    restart()
                free(dve, s_o_free[1], 4 * (n0 + STEPS - 1))
                layernorm(0)
                l0_step(n0 + STEPS, 0, False, True)
                free(dve, s_o_free[1], 4 * (n0 + STEPS))
                layernorm(1)

                def ffn(layer):
                    st = 2 * layer + 1
                    transpose_x(hf, st, 0)
                    ffn_up(hf, layer, 0)
                    transpose_x(hf, st, 1)
                    ffn_down(hf, layer, 0)
                    ffn_up(hf, layer, 1)
                    ffn_down(hf, layer, 1)

                ffn(0)
                transpose_x(hf, 2, 0)
                transpose_x(hf, 2, 1)
                restart()
                with dve.Fori(0, U) as u:
                    with dve.Fori(0, CH // 2) as c2:
                        for cp in range(2):
                            l1_chunk(hf, u, c2, cp)
                        restart()
                    l1_residual(hf, u)
                    restart()
                ffn(1)
                restart()


SLABS = 24 + 15


def kernel(**inputs):
    import concourse.bacc as bacc
    from concourse.bass_utils import run_bass_kernel_spmd as run

    g = {k: np.asarray(v) for k, v in inputs.items()}

    def slab(w):
        return np.ascontiguousarray(w.reshape(4, P, -1).transpose(1, 0, 2).reshape(P, -1))

    arrays = {"x": np.ascontiguousarray(g["L0_attn_x"].reshape(BATCH, TT, P, HID).transpose(0, 2, 1, 3))}
    gq = QH * HD
    arrays["wq"] = np.stack([slab(g["L0_attn_wq"][:, k * gq:(k + 1) * gq]) for k in range(GROUPS)])
    arrays["wkv"] = np.stack([slab(np.concatenate([g[n][:, k * HD:(k + 1) * HD] for n in ("L0_attn_wk", "L0_attn_wv")], 1))
                              for k in range(GROUPS)])
    arrays["wo"] = np.stack([slab(g["L0_attn_wo"][k * gq:(k + 1) * gq]) for k in range(GROUPS)])
    arrays["w12"] = np.stack([np.stack([slab(np.concatenate([g[f"L{n}_ffn_w12"].T[:, s * 256:(s + 1) * 256],
                                                             g[f"L{n}_ffn_w12"].T[:, 512 + s * 256:768 + s * 256]], 1))
                                        for s in range(2)]) for n in range(2)])
    arrays["b12"] = np.stack([np.ascontiguousarray(g[f"L{n}_ffn_b12"].reshape(8, P).T) for n in range(2)])
    arrays["w3"] = np.stack([slab(g[f"L{n}_ffn_w3"].T) for n in range(2)])
    wa = g["L1_attn_w_attn"]
    arrays["wc"] = np.stack([slab(np.concatenate([wa[:, k * HID + c * P:k * HID + (c + 1) * P] for k in range(3)], 1))
                             for c in range(CH)])
    arrays["battn"] = np.ascontiguousarray(g["L1_attn_b_attn"].reshape(12, P).T)
    arrays["wproj"] = slab(g["L1_attn_w_proj"])
    arrays["bias_rows"] = np.stack([np.ascontiguousarray(np.broadcast_to(g[n], (P, HID)))
                                    for n in ("L0_ffn_b3", "L1_attn_b_proj", "L1_ffn_b3")])
    half = HD // 2
    inv = (np.float32(10000.0) ** (-np.arange(half, dtype=np.float32) / np.float32(half))).astype(np.float32)
    ang = (inv[:, None] * np.arange(SEQ, dtype=np.float32)[None, :]).astype(np.float32)
    cos, sin = np.cos(ang).astype(np.float32), np.sin(ang).astype(np.float32)
    arrays["rope"] = np.stack([np.concatenate([cos, cos]), np.concatenate([-sin, sin])])
    qi, kj = np.arange(P)[:, None], np.arange(P)[None, :]
    zero = np.zeros((P, P), np.float32)
    arrays["mask0"] = np.concatenate([np.where(kj > qi, zero, -BIG), np.where(kj <= qi, zero, -BIG)], 1).astype(np.float32)
    r = np.arange(512)[None, :] - 384 - qi
    arrays["rel"] = np.where(r <= 0, r, -BIG).astype(np.float32)
    base = 2.0 ** (-2.0 ** (-(np.log2(H1) - 3)))
    sl = (base ** np.arange(1, H1 + 1, dtype=np.float32)).astype(np.float32)
    arrays["slopes"] = np.ascontiguousarray(np.broadcast_to(sl, (P, H1)))
    arrays["ident"] = np.eye(P, dtype=np.float32)
    odd = (np.arange(P) // D1) % 2
    arrays["headmask"] = np.stack([(odd == e) / D1 for e in range(2)], 1).astype(np.float32)

    nc = bacc.Bacc("TRN2", target_bir_lowering=False, num_devices=1)
    args = {k: nc.dram_tensor(f"in_{k}", v.shape, mybir.dt.from_np(v.dtype), kind="ExternalInput").ap()
            for k, v in arrays.items()}
    out = nc.dram_tensor("out", (BATCH, P, TT, HID), mybir.dt.float32, kind="ExternalOutput").ap()
    build(nc, out=out, **args)
    got = run(nc, [{f"in_{k}": v for k, v in arrays.items()}], core_ids=[0]).results[0]["out"]
    return np.ascontiguousarray(got.transpose(0, 2, 1, 3)).reshape(BATCH, SEQ, HID)
```

```python
import numpy as np
import concourse.bass as bass
from concourse import mybir
from contextlib import ExitStack

P = 128
BATCH, SEQ, HID = 4, 512, 512
U = 2
HALVES = BATCH // U
TT = SEQ // P
HC = HID // P
GROUPS, QH, HD = 8, 4, 128
L0_SCALE = float(HD) ** -0.5
STEPS = GROUPS * U
H1, D1 = 32, 16
CH = HID // P
HPC = P // D1
TRI = TT * (TT + 1) // 2
LAYERS = 2
BIG = 3.0e38
EPS = 1e-5
RSQRT_MAGIC = 1597463007.0


def build(nc, x, wq, wkv, wo, w12, b12, w3, wc, battn, wproj, bias_rows, rope, mask0, rel, slopes, ident, headmask, out):
    f32, f32r, i32 = mybir.dt.float32, mybir.dt.float32r, mybir.dt.int32
    ALU, ACT = mybir.AluOpType, mybir.ActivationFunctionType
    ctx = ExitStack()
    with ctx:
        def sb(name, shape, dt=f32):
            return ctx.enter_context(nc.sbuf_tensor(name, shape, dt))

        def sem(name):
            return ctx.enter_context(nc.semaphore(name))

        stage = sb("stage", [P, 2, 1024])
        w_h = {s: sb(f"w{s}_h", [P, HC * 512], f32r) for s in ("q0", "q1", "o", "kv")}
        w_l = {s: sb(f"w{s}_l", [P, HC * 512], f32r) for s in ("q0", "q1", "o", "kv")}
        xn = sb("xn", [P, U, TT, HID])
        xT_h = sb("xT_h", [P, U, HC, SEQ], f32r)
        xT_l = sb("xT_l", [P, U, HC, SEQ], f32r)
        k_h = sb("k_h", [P, 2, SEQ], f32r)
        k_l = sb("k_l", [P, 2, SEQ], f32r)
        q_h = sb("q_h", [P, 2, SEQ], f32r)
        q_l = sb("q_l", [P, 2, SEQ], f32r)
        v_hl = sb("v_hl", [P, 2, 2, TT, P], f32r)
        pT_h = sb("pT_h", [P, 2, 7 * P], f32r)
        pT_l = sb("pT_l", [P, 2, 7 * P], f32r)
        aT_h = sb("aT_h", [P, 4, SEQ], f32r)
        aT_l = sb("aT_l", [P, 4, SEQ], f32r)
        probs_all = sb("probs", [P, 2 * TRI * P])
        probs = probs_all[:, 0:2048].rearrange("p (a i k) -> p a i k", i=4, k=256)
        probs1 = probs_all[:, :].rearrange("p (a k) -> p a k", a=2)
        pT1_h = pT_h[:, :, :].rearrange("p a k -> p (a k)")
        pT1_l = pT_l[:, :, :].rearrange("p a k -> p (a k)")
        v_one = [[v_hl[:, 1, part, :, :] for part in range(2)],
                 [pT[:, TRI * P:TRI * P + 512].rearrange("p (t d) -> p t d", d=P) for pT in (pT1_h, pT1_l)]]
        zeros = sb("zeros", [P, P])
        work = sb("work", [P, 5, 512])
        cos_t = sb("cos_t", [P, SEQ])
        sin_t = sb("sin_t", [P, SEQ])
        mask_t = sb("mask_t", [P, 256])
        rel_t = sb("rel_t", [P, 512])
        ident_t = sb("ident_t", [P, P])
        slopes_t = sb("slopes_t", [P, H1])
        headmask_t = sb("headmask_t", [P, 2])
        bias_t = sb("bias_t", [P, HID])
        b12_t = sb("b12_t", [P, LAYERS, 8])
        nb12_t = sb("nb12_t", [P, LAYERS, 8])
        battn_t = sb("battn_t", [P, 12])
        negmax = sb("negmax", [P, 32])
        sums = sb("sums", [P, 2, 32])
        recips = sb("recips", [P, 32])
        stats = sb("stats", [P, TT, 6])
        meanvar = sb("meanvar", [P, TT, 2])
        newton = sb("newton", [P, 4, TT])

        bank = [ctx.enter_context(nc.psum_tensor(f"bank{i}", [P, 512], f32)) for i in range(8)]
        A, S, T, O = bank[0:2], bank[2:4], bank[4:6], bank[6:8]

        s_const = sem("constants_loaded")
        s_nb = sem("negated_bias_ready")
        s_zero = sem("zeros_ready")
        s_stage = [sem(f"stage_full{i}") for i in range(2)]
        s_stage_free = [sem(f"stage_free{i}") for i in range(2)]
        slots = ("q0", "q1", "o", "kv0", "kv1", "m")
        s_w = {s: sem(f"weights_ready_{s}") for s in slots}
        s_w_free = {s: sem(f"weights_used_{s}") for s in slots}
        s_split = sem("split_high_done")
        s_x = [sem(f"x_loaded{u}") for u in range(U)]
        s_store = [sem(f"out_stored{u}") for u in range(U)]
        s_bias = sem("bias_row_loaded")
        s_bias_used = sem("bias_row_used")
        s_biased = sem("residual_biased")
        s_ln = sem("layernorm_done")
        s_tr_done = sem("transposed_x")
        s_tr = [sem(f"xT_bank_full{i}") for i in range(2)]
        s_tr_h = sem("xT_high_done")
        s_xT = sem("xT_ready")
        s_tr_free = [sem(f"xT_bank_free{i}") for i in range(2)]
        s_a = [sem(f"proj_bank_full{i}") for i in range(2)]
        s_a_free = [sem(f"proj_bank_free{i}") for i in range(2)]
        s_s = [sem(f"score_bank_full{i}") for i in range(2)]
        s_s_free = [sem(f"score_bank_free{i}") for i in range(2)]
        s_t = [sem(f"transpose_bank_full{i}") for i in range(2)]
        s_t_free = [sem(f"transpose_bank_free{i}") for i in range(2)]
        s_o = [sem(f"out_bank_full{i}") for i in range(2)]
        s_o_free = [sem(f"out_bank_free{i}") for i in range(2)]
        s_swap = [sem(f"swapped{i}") for i in range(2)]
        s_swap_free = [sem(f"swapped_free{i}") for i in range(2)]
        s_rot = sem("rotated")
        s_rot_h = sem("rotated_high_done")
        s_k = sem("k_ready")
        s_q = sem("q_ready")
        s_vT = sem("vT_copied")
        s_v_h = sem("v_high_done")
        s_v = sem("v_ready")
        s_masked = sem("scores_masked")
        s_exp = sem("exp_done")
        s_p = sem("probs_ready")
        s_pT_h = sem("pT_high_done")
        s_pT = sem("pT_ready")
        s_aT_h = sem("aT_high_done")
        s_aT = sem("aT_ready")
        s_h = [sem(f"ffn_up_bank_full{i}") for i in range(2)]
        s_h_free = [sem(f"ffn_up_bank_free{i}") for i in range(2)]
        s_e = sem("ffn_exp_done")
        s_g = sem("gated_done")
        s_g_h = sem("gated_high_done")
        s_gT = sem("gated_ready")
        s_d = [sem(f"ffn_down_bank_full{i}") for i in range(2)]
        s_d_free = [sem(f"ffn_down_bank_free{i}") for i in range(2)]
        s1_prep = sem("l1_prep_bank_full")
        s1_raw = sem("l1_kqv_copied")
        s1_kh = sem("l1_k_high_done")
        s1_k = sem("l1_k_ready")
        s1_qh = sem("l1_q_high_done")
        s1_q = sem("l1_q_ready")
        s1_vh = sem("l1_v_high_done")
        s1_v = sem("l1_v_ready")
        s1_vone = sem("l1_head_v_ready")
        s1_s = [sem(f"l1_score_bank_full{i}") for i in range(4)]
        s1_tab = sem("alibi_table_ready")
        s1_masked = sem("l1_scores_masked")
        s1_exp = sem("l1_exp_done")
        s1_t = [sem(f"l1_transpose_bank_full{i}") for i in range(2)]
        s1_pT_h = sem("l1_pT_high_done")
        s1_pT = sem("l1_pT_ready")
        s1_pv = sem("l1_head_pv_done")
        s1_recip = sem("l1_reciprocals_ready")
        s1_rows = sem("l1_reciprocal_rows_copied")
        s1_nat = sem("l1_out_normalised")
        s1_aT_h = sem("l1_aT_high_done")
        s1_aT = sem("l1_aT_ready")
        s1_pr = sem("l1_proj_full")
        s1_pr_free = sem("l1_proj_used")
        c_dve = sem("vector_chain")
        N_CONST = 10
        s_seen = {e: sem(f"wait_passed_{e}") for e in ("dve", "pool", "pe")}

        def free(eng, s, uses):
            eng.wait_ge(s, uses + 1)

        def word(ap):
            return ap.bitcast(f32)

        FILLS = {"q0": 4 + 1 + 4 + 1, "q1": 4 + 1 + 1, "o": 8 + 3, "kv0": 4, "kv1": 4, "m": 4}

        block = ctx.enter_context(nc.Block())

        @block.sync
        def _(sp):
            def load_x(hf, u):
                if hf > 0:
                    sp.wait_ge(s_store[u], 16 * hf)
                sp.dma_start(xn[:, u, :, :], x[hf * U + u]).then_inc(s_x[u], 16)

            def store(hf, u):
                sp.wait_ge(s_ln, hf * 8 + 7 + u)
                sp.dma_start(out[hf * U + u], xn[:, u, :, :]).then_inc(s_store[u], 16)

            def load(m, src, cols):
                for i in range(2):
                    free(sp, s_stage_free[i], m)
                    sp.dma_start(stage[:, i, 0:cols // 2], src[:, i * (cols // 2):(i + 1) * (cols // 2)]) \
                        .then_inc(s_stage[i], 16)

            def load_bias(k, row):
                free(sp, s_bias_used, k)
                sp.dma_start(bias_t[:, :], bias_rows[row]).then_inc(s_bias, 16)

            sp.dma_start(ident_t[:, :], ident).then_inc(s_const, 16)
            load_x(0, 0)
            for dst, src in ((cos_t, rope[0]), (sin_t, rope[1]), (mask_t, mask0), (rel_t, rel),
                             (slopes_t, slopes), (headmask_t, headmask), (battn_t, battn)):
                sp.dma_start(dst[:, :], src).then_inc(s_const, 16)
            for n in range(LAYERS):
                sp.dma_start(b12_t[:, n, :], b12[n]).then_inc(s_const, 16)
            for s in (*s_stage_free, s_bias_used):
                sp.sem_inc(s, 1)
            for hf in range(HALVES):
                m = hf * SLABS
                load(m, wkv[0], 1024)
                load(m + 1, wq[0], 2048)
                if hf > 0:
                    store(hf - 1, 0)
                    load_x(hf, 0)
                    store(hf - 1, 1)
                load_x(hf, 1)
                load(m + 2, wo[0], 2048)
                load(m + 3, wkv[1], 1024)
                load(m + 4, wq[1], 2048)
                load(m + 5, wo[1], 2048)
                with sp.Fori(1, GROUPS // 2) as g2:
                    ms = [sp.snap(g2 * 6 + m + k) for k in range(6)]
                    gs = [sp.snap(g2 * 2 + p) for p in range(2)]
                    for p in range(2):
                        load(ms[3 * p], wkv[gs[p]], 1024)
                        load(ms[3 * p + 1], wq[gs[p]], 2048)
                        load(ms[3 * p + 2], wo[gs[p]], 2048)
                m += 24
                load(m, w12[0, 0], 2048)
                load(m + 1, w12[0, 1], 2048)
                load(m + 2, w3[0], 2048)
                load(m + 3, wc[0], 1536)
                load_bias(hf * 3, 0)
                load(m + 4, wc[1], 1536)
                load(m + 5, w12[1, 0], 2048)
                load(m + 6, wproj, 2048)
                load_bias(hf * 3 + 1, 1)
                for k in range(6):
                    load(m + 7 + k, wc[(2 + k) % CH], 1536)
                load(m + 13, w12[1, 1], 2048)
                load(m + 14, w3[1], 2048)
                load_bias(hf * 3 + 2, 2)
            for u in range(U):
                store(HALVES - 1, u)
            for u in range(U):
                sp.wait_ge(s_store[u], 16 * HALVES)

        @block.gpsimd
        def _(pool):
            def split(m, slot, fill, cols, also=()):
                free(pool, s_w_free[slot], fill)
                for name, val in also:
                    free(pool, s_w_free[name], val)
                key = {"kv0": "kv", "kv1": "kv", "m": "kv"}.get(slot, slot)
                off = 1024 if slot == "kv1" else 0
                for i in range(2):
                    part = slice(off + i * (cols // 2), off + (i + 1) * (cols // 2))
                    src = stage[:, i, 0:cols // 2]
                    pool.wait_ge(s_stage[i], 16 * m + 16)
                    pool.sem_inc(s_seen["pool"], 1)
                    nc.gpsimd.tensor_copy(w_h[key][:, part], src).then_inc(s_split, 1)
                    pool.wait_ge(s_split, 2 * m + i + 1)
                    low = nc.gpsimd.tensor_tensor(w_l[key][:, part], src, word(w_h[key][:, part]), ALU.subtract)
                    low.then_inc(s_stage_free[i], 1)
                    if i == 1:
                        free(pool, s_stage_free[1], m + 1)
                        pool.sem_inc(s_w[slot], 1)

            def add_bias(hf, k, stage_no):
                pool.wait_ge(s_bias, hf * 48 + 16 * k + 16)
                for u in range(U):
                    pool.wait_ge(s_tr_done, hf * 8 + stage_no * 2 + u + 1)
                    bc = bias_t[:, :]
                    for t in range(TT):
                        last = nc.gpsimd.tensor_tensor(xn[:, u, t, :], xn[:, u, t, :], bc, ALU.add)
                        last.then_inc(s_biased, 1)
                pool.wait_ge(s_biased, hf * 24 + k * 8 + 8)
                pool.sem_inc(s_bias_used, 1)

            for s in s_w_free.values():
                pool.sem_inc(s, 1)
            with pool.Fori(0, HALVES) as hf:
                f = {s: hf * FILLS[s] for s in FILLS}
                with pool.Fori(0, GROUPS // 2) as g2:
                    m = hf * SLABS + g2 * 6
                    for p in range(2):
                        split(m + 3 * p, f"kv{p}", f[f"kv{p}"] + g2, 1024, also=[("m", f["m"])])
                        split(m + 3 * p + 1, f"q{p}", f[f"q{p}"] + g2, 2048)
                        split(m + 3 * p + 2, "o", f["o"] + g2 * 2 + p, 2048)
                m = hf * SLABS + 24
                split(m, "q0", f["q0"] + 4, 2048)
                split(m + 1, "q1", f["q1"] + 4, 2048)
                split(m + 2, "o", f["o"] + 8, 2048)
                split(m + 3, "m", f["m"], 1536, also=[("kv0", f["kv0"] + 4), ("kv1", f["kv1"] + 4)])
                add_bias(hf, 0, 1)
                split(m + 4, "q0", f["q0"] + 5, 1536)
                split(m + 5, "q1", f["q1"] + 5, 2048)
                split(m + 6, "o", f["o"] + 9, 2048)
                add_bias(hf, 1, 2)
                for k in range(6):
                    split(m + 7 + k, ("m", "q0")[k % 2], f["m"] + 1 + k // 2 if k % 2 == 0 else f["q0"] + 6 + k // 2, 1536)
                split(m + 13, "q0", f["q0"] + 9, 2048)
                split(m + 14, "o", f["o"] + 10, 2048)
                add_bias(hf, 2, 3)

        def three(out_ap, ah, al, bh, bl, first=True, last=True, skip=False):
            nc.tensor.matmul(out_ap, ah, bh, start=first, stop=False, skip_group_check=skip)
            nc.tensor.matmul(out_ap, ah, bl, start=False, stop=False, skip_group_check=skip)
            return nc.tensor.matmul(out_ap, al, bh, start=False, stop=last, skip_group_check=skip)

        def project(out_ap, key, width, col, u, off=0):
            for c in range(HC):
                a = off + c * width + col
                last = three(out_ap, w_h[key][:, a:a + P], w_l[key][:, a:a + P],
                             xT_h[:, u, c, :], xT_l[:, u, c, :], c == 0, c == HC - 1)
            return last

        def down(out_ap, key, t):
            for c in range(4):
                last = three(out_ap, aT_h[:, c, t * P:(t + 1) * P], aT_l[:, c, t * P:(t + 1) * P],
                             w_h[key][:, c * 512:(c + 1) * 512], w_l[key][:, c * 512:(c + 1) * 512],
                             c == 0, c == 3)
            return last

        Q_BANK = ((1, 0), (1, 1), (0, 2), (1, 2))

        T_BLOCKS = [[(0, 0), (1, 0), (1, 1), (2, 1)], [(2, 2), (3, 2), (3, 3)]]

        PT_UNIT = ((0, 512), (512, 384), (896, 256), (1152, 128))

        def prep_use(c):
            return 5 * c - 1 if c else 0

        def rows_use(c):
            return 5 * c + 8 if c + 1 < CH else 5 * CH - 1

        @block.tensor
        def _(pe):
            pe.wait_ge(s_const, 16 * N_CONST)

            def transpose_x(hf, st, u):
                if st == 0:
                    pe.wait_ge(s_x[u], hf * 16 + 16)
                else:
                    pe.wait_ge(s_ln, hf * 8 + (st - 1) * 2 + u + 1)
                for c in range(HC):
                    free(pe, s_tr_free[c % 2], (hf * 8 + st * 2 + u) * 2 + c // 2)
                    for t in range(TT):
                        last = nc.tensor.transpose(T[c % 2][:, t * P:(t + 1) * P], xn[:, u, t, c * P:(c + 1) * P],
                                                   ident_t[:, :])
                    last.then_inc(s_tr[c % 2], 1)
                pe.wait_ge(s_tr[1], (hf * 8 + st * 2 + u) * 2 + 2)
                pe.sem_inc(s_tr_done, 1)

            def l0_step(n, hf, g, p, u, front, back):
                n1 = n - 1 if back else None
                pb, ub = (p if u == 1 else 1 - p), 1 - u

                def k():
                    pe.wait_ge(s_w[f"kv{p}"], hf * FILLS["kv0"] + g + 1)
                    free(pe, s_a_free[0], 3 * n)
                    project(A[0][:, :], "kv", 256, 0, u, off=1024 * p).then_inc(s_a[0], 1)

                def v():
                    free(pe, s_a_free[0], 3 * n + 1)
                    project(A[0][:, :], "kv", 256, P, u, off=1024 * p).then_inc(s_a[0], 1)

                def kv_used():
                    if u == 1:
                        pe.wait_ge(s_a[0], 3 * n + 2)
                        pe.sem_inc(s_w_free[f"kv{p}"], 1)

                def q(h):
                    if h == 0:
                        pe.wait_ge(s_w[f"q{p}"], hf * FILLS[f"q{p}"] + g + 1)
                    b, use = Q_BANK[h]
                    free(pe, s_a_free[b], 3 * n + use)
                    project(A[b][:, :], f"q{p}", 512, h * P, u).then_inc(s_a[b], 1)

                def q_used():
                    if u == 1:
                        pe.wait_ge(s_a[1], 3 * n + 3)
                        pe.sem_inc(s_w_free[f"q{p}"], 1)

                def scores(n, h, u):
                    pe.wait_ge(s_q, 4 * n + h + 1)
                    if h == 0:
                        pe.wait_ge(s_k, n + 1)
                    for i in range(TT):
                        if i % 2 == 0:
                            free(pe, s_s_free[i // 2], 4 * n + h)
                        lo = P if i == 0 else 0
                        k0 = (i - 1) * P + lo
                        last = three(S[i // 2][:, (i % 2) * 256 + lo:(i % 2) * 256 + 256],
                                     q_h[:, h % 2, i * P:(i + 1) * P], q_l[:, h % 2, i * P:(i + 1) * P],
                                     k_h[:, u, k0:(i + 1) * P], k_l[:, u, k0:(i + 1) * P])
                        if i % 2 == 1:
                            last.then_inc(s_s[i // 2], 1)

                def transposes(n, h):
                    pe.wait_ge(s_p, 4 * n + h + 1)
                    for b in range(2):
                        free(pe, s_t_free[b], (5 * n + h + (h > 0)) if b == 0 else (4 * n + h))
                        for k, (i, j) in enumerate(T_BLOCKS[b]):
                            c0 = (j - i + 1) * P
                            last = nc.tensor.transpose(T[b][:, k * P:(k + 1) * P],
                                                       probs[:, h % 2, i, c0:c0 + P], ident_t[:, :])
                        last.then_inc(s_t[b], 1)

                def v_transposes():
                    pe.wait_ge(s_vT, n + 1)
                    free(pe, s_t_free[0], 5 * n + 1)
                    for t in range(TT):
                        last = nc.tensor.transpose(T[0][:, t * P:(t + 1) * P], work[:, 4, t * P:(t + 1) * P],
                                                   ident_t[:, :])
                    last.then_inc(s_t[0], 1)

                def pv(n, h, u):
                    b = h % 2
                    pe.wait_ge(s_pT, 4 * n + h + 1)
                    if h == 0:
                        pe.wait_ge(s_v, n + 1)
                    free(pe, s_o_free[b], 4 * n + h // 2)
                    for j in range(TT):
                        w = 2 * P if j < 3 else P
                        seg = slice(j * 2 * P, j * 2 * P + w)
                        last = three(O[b][:, j * P:j * P + w], v_hl[:, u, 0, j, :], v_hl[:, u, 1, j, :],
                                     pT_h[:, h % 2, seg], pT_l[:, h % 2, seg], j == 0, j == 3, skip=True)
                    last.then_inc(s_o[b], 1)

                def wo_tile(n, t):
                    b = t % 2
                    if t == 0:
                        pe.wait_ge(s_aT, 4 * n + 4)
                        pe.wait_ge(s_w["o"], hf * FILLS["o"] + (g * 2 + p if u == 1 else g * 2 + p - 1) + 1)
                    free(pe, s_o_free[b], 4 * n + 2 + t // 2)
                    down(O[b][:, :], "o", t).then_inc(s_o[b], 1)

                def wo_used(n):
                    if ub == 1:
                        pe.wait_ge(s_o[1], 4 * n + 4)
                        pe.sem_inc(s_w_free["o"], 1)

                if front:
                    k()
                if back:
                    pv(n1, 1, ub)
                if front:
                    q(0)
                if back:
                    transposes(n1, 3)
                    pv(n1, 2, ub)
                if front:
                    v()
                    q(1)
                if back:
                    pv(n1, 3, ub)
                if front:
                    kv_used()
                    scores(n, 0, u)
                    q(2)
                if back:
                    wo_tile(n1, 0)
                if front:
                    scores(n, 1, u)
                    transposes(n, 0)
                if back:
                    wo_tile(n1, 1)
                if front:
                    scores(n, 2, u)
                    v_transposes()
                    q(3)
                    transposes(n, 1)
                if back:
                    wo_tile(n1, 2)
                if front:
                    q_used()
                if back:
                    wo_tile(n1, 3)
                if front:
                    scores(n, 3, u)
                    pv(n, 0, u)
                    transposes(n, 2)
                if back:
                    wo_used(n1)

            def ffn_up(hf, layer, u, ms):
                f = hf * 4 + layer * 2 + u
                pe.wait_ge(s_xT, (hf * 8 + (2 * layer + 1) * 2 + u) * 4 + 4)
                if layer == 1:
                    free(pe, s1_pr_free, hf * 8 + 8)
                for m in ms:
                    key = (("q0", "q1"), ("q1", "q0"))[layer][m // 2]
                    fills = {("q0", 0): 5, ("q1", 0): 5, ("q1", 1): 6, ("q0", 1): 10}[key, layer]
                    if m % 2 == 0:
                        pe.wait_ge(s_w[key], hf * FILLS[key] + fills)
                    free(pe, s_h_free[m % 2], 2 * f + m // 2)
                    b = (A, S)[m % 2]
                    project(b[0][:, :], key, 512, (m % 2) * P, u)
                    project(b[1][:, :], key, 512, 256 + (m % 2) * P, u).then_inc(s_h[m % 2], 1)
                    if m % 2 == 1 and u == 1:
                        pe.wait_ge(s_h[1], 2 * f + m // 2 + 1)
                        pe.sem_inc(s_w_free[key], 1)

            def ffn_down(hf, layer, u):
                f = hf * 4 + layer * 2 + u
                pe.wait_ge(s_gT, 4 * f + 4)
                pe.wait_ge(s_w["o"], hf * FILLS["o"] + (9, 11)[layer])
                for t in range(TT):
                    free(pe, s_d_free[t % 2], 2 * f + t // 2)
                    down(O[t % 2][:, :], "o", t).then_inc(s_d[t % 2], 1)
                if u == 1:
                    pe.wait_ge(s_d[1], 2 * f + 2)
                    pe.sem_inc(s_w_free["o"], 1)

            def l1_batch(a0, hf, u):
                def project_chunk(c, col, width=384):
                    return project(O[c % 2][:, :], "q0" if c % 2 else "kv", width, col * P, u)

                def k(c):
                    slot = ("m", "q0")[c % 2]
                    pe.wait_ge(s_w[slot], hf * FILLS[slot] + u * 2 + (1, 6)[c % 2] + c // 2)
                    free(pe, s1_nat, a0 + max(c - 1, 0))
                    project_chunk(c, 1).then_inc(s1_prep, 1)

                def q(c):
                    pe.wait_ge(s1_raw, 3 * (a0 + c) + 1)
                    project_chunk(c, 0).then_inc(s1_prep, 1)

                def v(c):
                    pe.wait_ge(s1_raw, 3 * (a0 + c) + 2)
                    project_chunk(c, 2).then_inc(s1_prep, 1)

                def v_transposes(c):
                    pe.wait_ge(s1_raw, 3 * (a0 + c) + 3)
                    pe.sem_inc(s_w_free[("m", "q0")[c % 2]], 1)
                    for t in range(TT):
                        last = nc.tensor.transpose(O[c % 2][:, t * P:(t + 1) * P], work[:, 4, t * P:(t + 1) * P],
                                                   ident_t[:, :])
                    last.then_inc(s1_prep, 1)

                def reciprocal_rows(c):
                    b = O[(c + 1) % 2]
                    pe.wait_ge(s1_recip, a0 + c + 1)
                    if c < CH - 1:
                        pe.wait_ge(s1_v, a0 + c + 2)
                    else:
                        free(pe, s1_nat, a0 + c)
                    for t in range(TT):
                        last = nc.tensor.transpose(b[:, t * P:(t + 1) * P], work[:, 3, t * P:(t + 1) * P], ident_t[:, :])
                    last.then_inc(s1_prep, 1)

                def scores(H, i):
                    c, k = divmod(H, HPC)
                    par, r = divmod(k, 4)
                    if i == 0 and k == 0:
                        pe.wait_ge(s1_k, a0 + c + 1)
                    if i == 0 and r == 0:
                        pe.wait_ge(s1_q, 2 * (a0 + c) + par + 1)
                    rows = slice(32 * r, 32 * r + 32)
                    qs = slice(i * P, (i + 1) * P)
                    n = (i + 1) * P
                    three(bank[i][:, 0:n], q_h[rows, par, qs], q_l[rows, par, qs],
                          k_h[rows, c % 2, 0:n], k_l[rows, c % 2, 0:n]).then_inc(s1_s[i], 1)

                def transposes(H, j):
                    Hg = a0 * HPC + H
                    if j == 0:
                        pe.wait_ge(s1_exp, 4 * Hg + 4)
                    if j >= 2:
                        pe.wait_ge(s1_pT, 4 * Hg + j - 1)
                    for i in range(j, TT):
                        p0 = (i * (i + 1) // 2 + j) * P
                        last = nc.tensor.transpose(T[j % 2][:, (i - j) * P:(i - j + 1) * P],
                                                   probs1[:, H % 2, p0:p0 + P], ident_t[:, :])
                    last.then_inc(s1_t[j % 2], 1)

                def pv(H, j):
                    c, k = divmod(H, HPC)
                    Hg = a0 * HPC + H
                    if j == 0:
                        pe.wait_ge(s1_vone, Hg + 2)
                        if k == 0:
                            free(pe, s1_rows, a0 + c)
                    pe.wait_ge(s1_pT, 4 * Hg + j + 1)
                    vo = v_one[H % 2]
                    off, w = PT_UNIT[j]
                    last = three(O[c % 2][:, j * P:512], vo[0][:, j, :], vo[1][:, j, :],
                                 pT1_h[:, off:off + w], pT1_l[:, off:off + w], k == 0 and j == 0,
                                 k == HPC - 1 and j == TT - 1, skip=True)
                    if j == TT - 1:
                        last.then_inc(s1_pv, 1)

                k(0)
                q(0)
                v(0)
                v_transposes(0)
                free(pe, s1_pr_free, a0)
                for i in range(TT):
                    scores(0, i)
                for H in range(H1):
                    c, k8 = divmod(H, HPC)
                    ahead = H + 1 < H1
                    transposes(H, 0)
                    if k8 == 0 and c:
                        reciprocal_rows(c - 1)
                    if ahead:
                        scores(H + 1, 0)
                        scores(H + 1, 1)
                    transposes(H, 1)
                    if ahead:
                        scores(H + 1, 2)
                        scores(H + 1, 3)
                    transposes(H, 2)
                    if c + 1 < CH and 2 <= k8 <= 5:
                        (k, q, v, v_transposes)[k8 - 2](c + 1)
                    for j in range(TT):
                        pv(H, j)
                        if j == 0:
                            transposes(H, 3)
                        if H == H1 - 1 and j == 1:
                            reciprocal_rows(c)

            for s in (*s_tr_free, *s_a_free, *s_s_free, *s_t_free, *s_o_free, *s_h_free, *s_d_free, s1_nat, s1_rows,
                      s1_pr_free, s1_pv, s1_pv):
                pe.sem_inc(s, 1)
            with pe.Fori(0, HALVES) as hf:
                n0 = hf * STEPS
                transpose_x(hf, 0, 0)
                pe.wait_ge(s_xT, hf * 32 + 4)
                l0_step(n0, hf, 0, 0, 0, True, False)
                free(pe, s_t_free[0], n0 * 5 + 4)
                free(pe, s_t_free[1], n0 * 4 + 3)
                transpose_x(hf, 0, 1)
                pe.wait_ge(s_xT, hf * 32 + 8)
                l0_step(n0 + 1, hf, 0, 0, 1, True, True)
                l0_step(n0 + 2, hf, 0, 1, 0, True, True)
                l0_step(n0 + 3, hf, 0, 1, 1, True, True)
                with pe.Fori(1, GROUPS // 2) as g2:
                    for s in range(4):
                        l0_step(n0 + g2 * 4 + s, hf, g2, s // 2, s % 2, True, True)
                l0_step(n0 + STEPS, hf, GROUPS // 2, 0, 0, False, True)

                def ffn(layer):
                    st = 2 * layer + 1
                    transpose_x(hf, st, 0)
                    ffn_up(hf, layer, 0, (0, 1))
                    transpose_x(hf, st, 1)
                    ffn_up(hf, layer, 0, (2, 3))
                    ffn_up(hf, layer, 1, (0, 1))
                    ffn_down(hf, layer, 0)
                    ffn_up(hf, layer, 1, (2, 3))
                    ffn_down(hf, layer, 1)

                ffn(0)
                transpose_x(hf, 2, 0)
                transpose_x(hf, 2, 1)
                pe.wait_ge(s_xT, (hf * 8 + 6) * 4)
                pe.sem_inc(s_seen["pe"], 1)
                with pe.Fori(0, U) as u:
                    l1_batch(hf * 8 + u * 4, hf, u)
                    pe.wait_ge(s1_aT, hf * 8 + u * 4 + 5)
                    pe.wait_ge(s_w["o"], hf * FILLS["o"] + 10)
                    for t in range(TT):
                        down(bank[t][:, :], "o", t).then_inc(s1_pr, 1)
                pe.wait_ge(s1_pr, hf * 8 + 8)
                pe.sem_inc(s_w_free["o"], 1)
                ffn(1)

        @block.scalar
        def _(act):
            act.wait_ge(s_const, 16 * N_CONST)
            act.wait_ge(s_nb, 1)

            def copy(dst, src):
                return nc.scalar.activation(dst, src, ACT.Copy)

            def transpose_x(hf, st, u):
                for c in range(HC):
                    act.wait_ge(s_tr[c % 2], (hf * 8 + st * 2 + u) * 2 + c // 2 + 1)
                    copy(xT_h[:, u, c, :], T[c % 2][:, :]).then_inc(s_tr_h, 1)

            def l0_step(n, u, front, back):
                n1 = n - 1 if back else None
                ub = 1 - u

                def swap(item):
                    b, use = (0, 0) if item == 0 else Q_BANK[item - 1]
                    sbuf = item % 2
                    sidx = (3 * n + item // 2) if sbuf == 0 else (2 * n + item // 2)
                    act.wait_ge(s_a[b], 3 * n + use + 1)
                    free(act, s_swap_free[sbuf], sidx)
                    copy(work[0:64, sbuf, :], A[b][64:128, :])
                    copy(work[64:128, sbuf, :], A[b][0:64, :]).then_inc(s_swap[sbuf], 1)

                def high(item):
                    dst = k_h[:, u, :] if item == 0 else q_h[:, (item - 1) % 2, :]
                    act.wait_ge(s_rot, 5 * n + item + 1)
                    copy(dst, work[:, 2 + item % 2, :]).then_inc(s_rot_h, 1)

                def v_copy():
                    act.wait_ge(s_a[0], 3 * n + 2)
                    copy(work[:, 4, :], A[0][:, :]).then_inc(s_vT, 1)
                    act.wait_ge(s_vT, n + 1)
                    act.sem_inc(s_a_free[0], 1)

                def exps(n, h):
                    for i in range(TT):
                        lo = P if i == 0 else 0
                        act.wait_ge(s_masked, 16 * n + 4 * h + i + 1)
                        col = (h % 2) * 4 + i
                        nc.scalar.activation(probs[:, h % 2, i, lo:256], probs[:, h % 2, i, lo:256], ACT.Exp,
                                             bias=negmax[:, col:col + 1], scale=-1.0,
                                             accum_out=sums[:, 0, col:col + 1]).then_inc(s_exp, 1)

                def pT_high(n, h):
                    for b in range(2):
                        act.wait_ge(s_t[b], (5 * n + 1 + h + (h > 0)) if b == 0 else (4 * n + h + 1))
                        w = len(T_BLOCKS[b]) * P
                        copy(pT_h[:, h % 2, b * 512:b * 512 + w], T[b][:, 0:w]).then_inc(s_pT_h, 1)

                def v_high():
                    act.wait_ge(s_t[0], 5 * n + 2)
                    copy(v_hl[:, u, 0, :, :], T[0][:, :].rearrange("p (t d) -> p t d", d=P)).then_inc(s_v_h, 1)

                def aT_high(n, h):
                    act.wait_ge(s_o[h % 2], 4 * n + h // 2 + 1)
                    copy(aT_h[:, h, :], O[h % 2][:, :]).then_inc(s_aT_h, 1)

                if front:
                    swap(0)
                    high(0)
                if back:
                    aT_high(n1, 1)
                if front:
                    swap(1)
                    high(1)
                if back:
                    pT_high(n1, 3)
                    aT_high(n1, 2)
                if front:
                    v_copy()
                    swap(2)
                if back:
                    aT_high(n1, 3)
                if front:
                    high(2)
                    exps(n, 0)
                    swap(3)
                    high(3)
                    pT_high(n, 0)
                    exps(n, 1)
                    v_high()
                    swap(4)
                    exps(n, 2)
                    high(4)
                    pT_high(n, 1)
                    exps(n, 3)
                    aT_high(n, 0)
                    pT_high(n, 2)

            def ffn_exp(hf, layer, u, m):
                f = hf * 4 + layer * 2 + u
                act.wait_ge(s_h[m % 2], 2 * f + m // 2 + 1)
                if m >= 2:
                    act.wait_ge(s_g, 4 * f + m - 1)
                nc.scalar.activation(work[:, m % 2, :], (A, S)[m % 2][0][:, :], ACT.Exp, scale=-1.0,
                                     bias=nb12_t[:, layer, m:m + 1]).then_inc(s_e, 1)

            def gated_high(f, m):
                act.wait_ge(s_g, 4 * f + m + 1)
                copy(aT_h[:, m, :], work[:, 2 + m % 2, :]).then_inc(s_g_h, 1)

            def l1_batch(a0):
                def raw(c, k, col, buf):
                    act.wait_ge(s1_prep, 5 * a0 + prep_use(c) + k + 1)
                    if k == 2:
                        act.wait_ge(s1_aT, a0 + max(c - 1, 0) + 1)
                    nc.scalar.activation(work[:, buf, :], O[c % 2][:, :], ACT.Identity,
                                         bias=battn_t[:, col * CH + c:col * CH + c + 1]).then_inc(s1_raw, 1)
                    act.wait_ge(s1_raw, 3 * (a0 + c) + k + 1)

                def k_prep(c):
                    raw(c, 0, 1, 3)
                    copy(k_h[:, c % 2, :], work[:, 3, :]).then_inc(s1_kh, 1)

                def q_prep(c):
                    raw(c, 1, 0, 2)

                def q_high(c, e):
                    nc.scalar.activation(q_h[:, e, :], work[:, 2, :], ACT.Copy,
                                         scale=headmask_t[:, e:e + 1]).then_inc(s1_qh, 1)

                def v_prep(c):
                    raw(c, 2, 2, 4)

                def v_high(c):
                    act.wait_ge(s1_prep, 5 * a0 + prep_use(c) + 4)
                    act.wait_ge(s1_vone, HPC * (a0 + c) + 1)
                    copy(v_hl[:, 0, 0, :, :], O[c % 2][:, :].rearrange("p (t d) -> p t d", d=P)).then_inc(s1_vh, 1)

                def rows_copy(c):
                    act.wait_ge(s1_prep, 5 * a0 + rows_use(c) + 1)
                    if c == CH - 1:
                        act.wait_ge(s1_aT, a0 + c + 1)
                    copy(work[:, 4, :], O[(c + 1) % 2][:, :]).then_inc(s1_rows, 1)

                def aT_high(c):
                    act.wait_ge(s1_nat, a0 + c + 2)
                    copy(aT_h[:, c, :], work[:, 4, :]).then_inc(s1_aT_h, 1)

                def table(H):
                    c, k = divmod(H, HPC)
                    par, r = divmod(k, 4)
                    h = c * HPC + 2 * r + par
                    nc.scalar.activation(work[:, H % 2, :], rel_t[:, :], ACT.Copy,
                                         scale=slopes_t[:, h:h + 1]).then_inc(s1_tab, 1)

                def exp(H, i):
                    c, k = divmod(H, HPC)
                    par, r = divmod(k, 4)
                    p0, w = i * (i + 1) // 2 * P, (i + 1) * P
                    col = i * HPC + 2 * r + par
                    act.wait_ge(s1_masked, 4 * (a0 * HPC + H) + i + 1)
                    nm = k * 4 + i
                    nc.scalar.activation(probs1[:, H % 2, p0:p0 + w], probs1[:, H % 2, p0:p0 + w], ACT.Exp,
                                         bias=negmax[:, nm:nm + 1], scale=-1.0,
                                         accum_out=sums[:, c % 2, col:col + 1]).then_inc(s1_exp, 1)

                def pT_high(H, j):
                    off, w = PT_UNIT[j]
                    act.wait_ge(s1_t[j % 2], 2 * (a0 * HPC + H) + j // 2 + 1)
                    copy(pT1_h[:, off:off + w], T[j % 2][:, 0:w]).then_inc(s1_pT_h, 1)

                table(0)
                table(1)
                k_prep(0)
                q_prep(0)
                q_high(0, 0)
                q_high(0, 1)
                v_prep(0)
                v_high(0)
                for i in range(TT):
                    exp(0, i)
                for H in range(H1):
                    c, k8 = divmod(H, HPC)
                    ahead = H + 1 < H1
                    pT_high(H, 0)
                    if k8 == 0 and c:
                        rows_copy(c - 1)
                    if ahead:
                        exp(H + 1, 0)
                        exp(H + 1, 1)
                    pT_high(H, 1)
                    if ahead:
                        exp(H + 1, 2)
                    pT_high(H, 2)
                    if ahead:
                        exp(H + 1, 3)
                    if c + 1 < CH:
                        if k8 == 2:
                            k_prep(c + 1)
                        if k8 == 3:
                            q_prep(c + 1)
                            q_high(c + 1, 0)
                        if k8 == 4:
                            v_prep(c + 1)
                        if k8 == 6:
                            q_high(c + 1, 1)
                    pT_high(H, 3)
                    if H + 2 < H1:
                        table(H + 2)
                    if k8 == 0 and c:
                        aT_high(c - 1)
                    if c + 1 < CH and k8 == 6:
                        v_high(c + 1)
                    if H == H1 - 1:
                        rows_copy(c)
                aT_high(CH - 1)

            for s in s_swap_free:
                act.sem_inc(s, 1)
            with act.Fori(0, HALVES) as hf:
                n0 = hf * STEPS
                transpose_x(hf, 0, 0)
                l0_step(n0, 0, True, False)
                transpose_x(hf, 0, 1)
                for s in range(1, 4):
                    l0_step(n0 + s, s % 2, True, True)
                with act.Fori(1, GROUPS // 2) as g2:
                    for s in range(4):
                        l0_step(n0 + g2 * 4 + s, s % 2, True, True)
                l0_step(n0 + STEPS, 0, False, True)

                def ffn(layer):
                    st = 2 * layer + 1
                    f0, f1 = (hf * 4 + layer * 2 + u for u in range(U))
                    transpose_x(hf, st, 0)
                    ffn_exp(hf, layer, 0, 0)
                    ffn_exp(hf, layer, 0, 1)
                    transpose_x(hf, st, 1)
                    gated_high(f0, 0)
                    ffn_exp(hf, layer, 0, 2)
                    gated_high(f0, 1)
                    ffn_exp(hf, layer, 0, 3)
                    gated_high(f0, 2)
                    gated_high(f0, 3)
                    ffn_exp(hf, layer, 1, 0)
                    ffn_exp(hf, layer, 1, 1)
                    act.wait_ge(s_d[1], 2 * f0 + 2)
                    gated_high(f1, 0)
                    gated_high(f1, 1)
                    ffn_exp(hf, layer, 1, 2)
                    ffn_exp(hf, layer, 1, 3)
                    gated_high(f1, 2)
                    gated_high(f1, 3)

                ffn(0)
                transpose_x(hf, 2, 0)
                transpose_x(hf, 2, 1)
                with act.Fori(0, U) as u:
                    l1_batch(hf * 8 + u * 4)
                ffn(1)

        @block.vector
        def _(dve):
            count = [0]

            def link(ins):
                count[0] += 1
                ins.then_inc(c_dve, 1)
                dve.wait_ge(c_dve, count[0])

            def restart():
                if count[0]:
                    dve.sem_clear(c_dve)
                    count[0] = 0

            def low(dst, src, high):
                return nc.vector.tensor_tensor(dst, src, word(high), ALU.subtract)

            dve.wait_ge(s_const, 16 * N_CONST)
            nc.vector.tensor_scalar(nb12_t[:, :, :], b12_t[:, :, :], -1.0, None, ALU.mult).then_inc(s_nb, 1)

            def transpose_x(hf, st, u):
                for c in range(HC):
                    dve.wait_ge(s_tr_h, (hf * 8 + st * 2 + u) * 4 + c + 1)
                    low(xT_l[:, u, c, :], T[c % 2][:, :], xT_h[:, u, c, :]).then_inc(s_xT, 1)
                    dve.wait_ge(s_xT, (hf * 8 + st * 2 + u) * 4 + c + 1)
                    dve.sem_inc(s_tr_free[c % 2], 1)

            def l0_step(n, u, front, back):
                n1 = n - 1 if back else None
                ub = 1 - u

                def rotate(item):
                    b = 0 if item == 0 else Q_BANK[item - 1][0]
                    sbuf = item % 2
                    sidx = (3 * n + item // 2) if sbuf == 0 else (2 * n + item // 2)
                    rot = work[:, 2 + item % 2, :]
                    dve.wait_ge(s_swap[sbuf], sidx + 1)
                    nc.vector.tensor_tensor(rot, A[b][:, :], cos_t[:, :], ALU.mult).then_inc(s_a_free[b], 1)
                    link(nc.vector.tensor_tensor(work[:, sbuf, :], work[:, sbuf, :], sin_t[:, :], ALU.mult))
                    nc.vector.tensor_tensor(rot, rot, work[:, sbuf, :], ALU.add).then_inc(s_rot, 1)
                    dve.wait_ge(s_rot, 5 * n + item + 1)
                    dve.sem_inc(s_swap_free[sbuf], 1)

                def rot_low(item):
                    dve.wait_ge(s_rot_h, 5 * n + item + 1)
                    rot = work[:, 2 + item % 2, :]
                    if item == 0:
                        low(k_l[:, u, :], rot, k_h[:, u, :]).then_inc(s_k, 1)
                    else:
                        q = (item - 1) % 2
                        low(q_l[:, q, :], rot, q_h[:, q, :]).then_inc(s_q, 1)

                def mask(n, h):
                    for i in range(TT):
                        lo = P if i == 0 else 0
                        col = (h % 2) * 4 + i
                        if i % 2 == 0:
                            dve.wait_ge(s_s[i // 2], 4 * n + h + 1)
                            dve.sem_inc(s_seen["dve"], 1)
                        nc.vector.tensor_tensor_reduce(
                            out=probs[:, h % 2, i, lo:256], in0=S[i // 2][:, (i % 2) * 256 + lo:(i % 2) * 256 + 256],
                            in1=mask_t[:, lo:256], scale=-L0_SCALE, scalar=BIG, op0=ALU.add, op1=ALU.min,
                            accum_out=negmax[:, col:col + 1]).then_inc(s_masked, 1)
                        if i % 2 == 1:
                            dve.wait_ge(s_masked, 16 * n + 4 * h + i + 1)
                            dve.sem_inc(s_s_free[i // 2], 1)

                def normalise(n, h):
                    c0 = (h % 2) * 4
                    dve.wait_ge(s_exp, 16 * n + 4 * h + 4)
                    link(nc.vector.reciprocal(recips[:, c0:c0 + 4], sums[:, 0, c0:c0 + 4]))
                    for i in range(TT):
                        lo = P if i == 0 else 0
                        p = probs[:, h % 2, i, lo:256]
                        last = nc.vector.tensor_scalar(p, p, recips[:, c0 + i:c0 + i + 1], None, ALU.mult)
                    last.then_inc(s_p, 1)

                def pT_low(n, h):
                    for b in range(2):
                        w = len(T_BLOCKS[b]) * P
                        seg = slice(b * 512, b * 512 + w)
                        dve.wait_ge(s_pT_h, 8 * n + 2 * h + b + 1)
                        last = low(pT_l[:, h % 2, seg], T[b][:, 0:w], pT_h[:, h % 2, seg])
                        last.then_inc(s_t_free[b], 1)
                    free(dve, s_t_free[1], 4 * n + h + 1)
                    dve.sem_inc(s_pT, 1)

                def v_low():
                    dve.wait_ge(s_v_h, n + 1)
                    low(v_hl[:, u, 1, :, :], T[0][:, :].rearrange("p (t d) -> p t d", d=P),
                        v_hl[:, u, 0, :, :]).then_inc(s_v, 1)
                    dve.wait_ge(s_v, n + 1)
                    dve.sem_inc(s_t_free[0], 1)

                def aT_low(n, h):
                    dve.wait_ge(s_aT_h, 4 * n + h + 1)
                    low(aT_l[:, h, :], O[h % 2][:, :], aT_h[:, h, :]).then_inc(s_aT, 1)
                    dve.wait_ge(s_aT, 4 * n + h + 1)
                    dve.sem_inc(s_o_free[h % 2], 1)

                def accumulate(n, u, t):
                    dve.wait_ge(s_o[t % 2], 4 * n + 3 + t // 2)
                    nc.vector.tensor_tensor(xn[:, u, t, :], O[t % 2][:, :], xn[:, u, t, :], ALU.add)\
                        .then_inc(s_o_free[t % 2], 1)

                restart()
                if front:
                    rotate(0)
                    rot_low(0)
                if back:
                    aT_low(n1, 1)
                if front:
                    rotate(1)
                    rot_low(1)
                if back:
                    pT_low(n1, 3)
                    aT_low(n1, 2)
                if front:
                    rotate(2)
                if back:
                    aT_low(n1, 3)
                if front:
                    rot_low(2)
                    mask(n, 0)
                    normalise(n, 0)
                    rotate(3)
                    mask(n, 1)
                    rot_low(3)
                    pT_low(n, 0)
                if back:
                    accumulate(n1, ub, 0)
                if front:
                    normalise(n, 1)
                    v_low()
                if back:
                    accumulate(n1, ub, 1)
                if front:
                    mask(n, 2)
                    rotate(4)
                if back:
                    accumulate(n1, ub, 2)
                if front:
                    rot_low(4)
                    normalise(n, 2)
                    pT_low(n, 1)
                if back:
                    accumulate(n1, ub, 3)
                if front:
                    mask(n, 3)
                    aT_low(n, 0)
                    pT_low(n, 2)
                    normalise(n, 3)

            def layernorm(u):
                for t in range(TT):
                    last = nc.vector.bn_stats(stats[:, t, :], xn[:, u, t, :])
                    if t == TT - 1:
                        link(last)
                for t in range(TT):
                    last = nc.vector.bn_aggr(meanvar[:, t, :], stats[:, t, :])
                link(last)
                var, y, y2, z = (newton[:, k, :] for k in range(4))
                link(nc.vector.tensor_scalar(var, meanvar[:, :, 1], EPS, None, ALU.add))
                link(nc.vector.tensor_scalar(y.bitcast(i32), var.bitcast(i32), 1, None, ALU.logical_shift_right))
                link(nc.vector.tensor_scalar(y.bitcast(i32), y.bitcast(i32), -1.0, RSQRT_MAGIC, ALU.mult, ALU.add))
                for _ in range(3):
                    link(nc.vector.tensor_tensor(y2, y, y, ALU.mult))
                    link(nc.vector.scalar_tensor_tensor(z, y2, -0.5, var, ALU.mult, ALU.mult))
                    link(nc.vector.scalar_tensor_tensor(y, z, 1.5, y, ALU.add, ALU.mult))
                for t in range(TT):
                    last = nc.vector.tensor_scalar(xn[:, u, t, :], xn[:, u, t, :], meanvar[:, t, 0:1],
                                                   newton[:, 1, t:t + 1], ALU.subtract, ALU.mult)
                last.then_inc(s_ln, 1)

            def ffn_gate(hf, layer, u, m):
                f = hf * 4 + layer * 2 + u
                b = (A, S)[m % 2]
                e = work[:, m % 2, :]
                g = work[:, 2 + m % 2, :]
                dve.wait_ge(s_e, 4 * f + m + 1)
                link(nc.vector.tensor_scalar(e, e, 1.0, None, ALU.add))
                link(nc.vector.reciprocal(e, e))
                link(nc.vector.scalar_tensor_tensor(g, b[0][:, :], b12_t[:, layer, m:m + 1], e, ALU.add, ALU.mult))
                nc.vector.scalar_tensor_tensor(g, b[1][:, :], b12_t[:, layer, 4 + m:5 + m], g,
                                               ALU.add, ALU.mult).then_inc(s_g, 1)
                dve.wait_ge(s_g, 4 * f + m + 1)
                dve.sem_inc(s_h_free[m % 2], 1)

            def gated_low(hf, layer, u, m):
                dve.wait_ge(s_g_h, 4 * (hf * 4 + layer * 2 + u) + m + 1)
                low(aT_l[:, m, :], work[:, 2 + m % 2, :], aT_h[:, m, :]).then_inc(s_gT, 1)

            def ffn_residual(hf, layer, u):
                f = hf * 4 + layer * 2 + u
                dve.wait_ge(s_biased, hf * 24 + layer * 16 + u * 4 + 4)
                for t in range(TT):
                    dve.wait_ge(s_d[t % 2], 2 * f + t // 2 + 1)
                    nc.vector.tensor_tensor(xn[:, u, t, :], O[t % 2][:, :], xn[:, u, t, :], ALU.add)\
                        .then_inc(s_d_free[t % 2], 1)

            def ffn_layernorm(hf, layer, u):
                f = hf * 4 + layer * 2 + u
                free(dve, s_d_free[0], 2 * f + 2)
                free(dve, s_d_free[1], 2 * f + 2)
                layernorm(u)

            def l1_batch(a0):
                def k_low(c):
                    dve.wait_ge(s1_kh, a0 + c + 1)
                    low(k_l[:, c % 2, :], work[:, 3, :], k_h[:, c % 2, :]).then_inc(s1_k, 1)

                def q_low(c, e):
                    dve.wait_ge(s1_qh, 2 * (a0 + c) + e + 1)
                    nc.vector.scalar_tensor_tensor(q_l[:, e, :], work[:, 2, :], headmask_t[:, e:e + 1],
                                                   word(q_h[:, e, :]), ALU.mult, ALU.subtract).then_inc(s1_q, 1)

                def v_low(c):
                    dve.wait_ge(s1_vh, a0 + c + 1)
                    low(v_hl[:, 0, 1, :, :], O[c % 2][:, :].rearrange("p (t d) -> p t d", d=P),
                        v_hl[:, 0, 0, :, :]).then_inc(s1_v, 1)

                def head_columns(v, H):
                    par, r = divmod(H % HPC, 4)
                    h = 2 * r + par
                    return v[:, :, h * D1:(h + 1) * D1]

                def v_head(H):
                    c, k = divmod(H, HPC)
                    vo = v_one[H % 2]
                    dve.wait_ge(s1_pv, a0 * HPC + H + 1)
                    for part in range(2):
                        nc.vector.tensor_copy(head_columns(vo[part], H - 2), zeros[:, 0:TT * D1].rearrange("p (t e) -> p t e", e=D1))
                    if k == 0:
                        dve.wait_ge(s1_v, a0 + c + 1)
                    for part in range(2):
                        last = nc.vector.tensor_copy(head_columns(vo[part], H), word(head_columns(v_hl[:, 0, part, :, :], H)))
                    last.then_inc(s1_vone, 1)

                def mask(H, i):
                    Hg = a0 * HPC + H
                    p0, w = i * (i + 1) // 2 * P, (i + 1) * P
                    nm = H % HPC * 4 + i
                    if i == 0:
                        dve.wait_ge(s1_tab, Hg + 1)
                    dve.wait_ge(s1_s[i], Hg + 1)
                    dve.sem_inc(s_seen["dve"], 1)
                    nc.vector.tensor_tensor_reduce(
                        out=probs1[:, H % 2, p0:p0 + w], in0=bank[i][:, 0:w], in1=work[:, H % 2, 512 - w:512],
                        scale=-1.0, scalar=BIG, op0=ALU.add, op1=ALU.min,
                        accum_out=negmax[:, nm:nm + 1]).then_inc(s1_masked, 1)

                def pT_low(H, j):
                    off, w = PT_UNIT[j]
                    dve.wait_ge(s1_pT_h, 4 * (a0 * HPC + H) + j + 1)
                    low(pT1_l[:, off:off + w], T[j % 2][:, 0:w], pT1_h[:, off:off + w]).then_inc(s1_pT, 1)

                def reciprocals(c):
                    dve.wait_ge(s1_exp, 4 * HPC * (a0 + c + 1))
                    link(nc.vector.reciprocal(recips[:, :], sums[:, c % 2, :]))
                    nc.vector.tensor_copy(work[:, 3, :].rearrange("p (s e) -> p s e", e=D1),
                                          recips[:, :].unsqueeze(2).to_broadcast([P, 32, D1])).then_inc(s1_recip, 1)

                def normalise(c):
                    dve.wait_ge(s1_pv, HPC * (a0 + c + 1) + 2)
                    dve.wait_ge(s1_rows, a0 + c + 2)
                    nc.vector.tensor_tensor(work[:, 4, :], O[c % 2][:, :], work[:, 4, :], ALU.mult).then_inc(s1_nat, 1)

                def aT_low(c):
                    dve.wait_ge(s1_aT_h, a0 + c + 1)
                    low(aT_l[:, c, :], work[:, 4, :], aT_h[:, c, :]).then_inc(s1_aT, 1)

                k_low(0)
                q_low(0, 0)
                q_low(0, 1)
                v_low(0)
                for i in range(TT):
                    mask(0, i)
                v_head(0)
                for H in range(H1):
                    c, k8 = divmod(H, HPC)
                    ahead = H + 1 < H1
                    if H == H1 - 1:
                        reciprocals(c)
                    if ahead:
                        mask(H + 1, 0)
                        mask(H + 1, 1)
                    pT_low(H, 0)
                    if ahead:
                        mask(H + 1, 2)
                    pT_low(H, 1)
                    if ahead:
                        mask(H + 1, 3)
                    pT_low(H, 2)
                    pT_low(H, 3)
                    if ahead:
                        if k8 == 7:
                            reciprocals(c)
                        v_head(H + 1)
                    if k8 == 0 and c:
                        normalise(c - 1)
                    if k8 == 1 and c:
                        aT_low(c - 1)
                    if c + 1 < CH:
                        if k8 == 2:
                            k_low(c + 1)
                        if k8 == 3:
                            q_low(c + 1, 0)
                        if k8 == 6:
                            q_low(c + 1, 1)
                            v_low(c + 1)
                normalise(CH - 1)
                aT_low(CH - 1)

            def l1_residual(hf, u):
                dve.wait_ge(s_biased, hf * 24 + 8 + u * 4 + 4)
                for t in range(TT):
                    dve.wait_ge(s1_pr, hf * 8 + u * 4 + t + 1)
                    nc.vector.tensor_tensor(xn[:, u, t, :], bank[t][:, :], xn[:, u, t, :], ALU.add)\
                        .then_inc(s1_pr_free, 1)
                free(dve, s1_pr_free, hf * 8 + u * 4 + 4)
                dve.sem_inc(s_seen["dve"], 1)
                layernorm(u)

            nc.vector.memset(zeros[:, :], 0.0).then_inc(s_zero, 1)
            dve.wait_ge(s_zero, 1)
            for s in (s1_vone, s1_aT):
                dve.sem_inc(s, 1)
            with dve.Fori(0, HALVES) as hf:
                restart()
                n0 = hf * STEPS
                transpose_x(hf, 0, 0)
                l0_step(n0, 0, True, False)
                transpose_x(hf, 0, 1)
                for s in range(1, 4):
                    l0_step(n0 + s, s % 2, True, True)
                restart()
                with dve.Fori(1, GROUPS // 2) as g2:
                    for s in range(4):
                        l0_step(n0 + g2 * 4 + s, s % 2, True, True)
                    restart()
                free(dve, s_o_free[1], 4 * (n0 + STEPS - 1))
                layernorm(0)
                l0_step(n0 + STEPS, 0, False, True)

                def ffn(layer):
                    st = 2 * layer + 1
                    transpose_x(hf, st, 0)
                    if layer == 0:
                        free(dve, s_o_free[1], 4 * (n0 + STEPS))
                        layernorm(1)
                    restart()
                    ffn_gate(hf, layer, 0, 0)
                    transpose_x(hf, st, 1)
                    for m in range(1, 4):
                        ffn_gate(hf, layer, 0, m)
                        gated_low(hf, layer, 0, m - 1)
                    gated_low(hf, layer, 0, 3)
                    ffn_gate(hf, layer, 1, 0)
                    ffn_gate(hf, layer, 1, 1)
                    ffn_residual(hf, layer, 0)
                    gated_low(hf, layer, 1, 0)
                    gated_low(hf, layer, 1, 1)
                    ffn_gate(hf, layer, 1, 2)
                    ffn_gate(hf, layer, 1, 3)
                    gated_low(hf, layer, 1, 2)
                    gated_low(hf, layer, 1, 3)
                    restart()
                    ffn_layernorm(hf, layer, 0)
                    ffn_residual(hf, layer, 1)
                    if layer == 0:
                        transpose_x(hf, 2, 0)
                    ffn_layernorm(hf, layer, 1)
                    if layer == 0:
                        transpose_x(hf, 2, 1)

                ffn(0)
                restart()
                for vo in v_one:
                    for part in vo:
                        for t in range(TT):
                            nc.vector.tensor_copy(part[:, t, :], zeros[:, :])
                with dve.Fori(0, U) as u:
                    l1_batch(hf * 8 + u * 4)
                    l1_residual(hf, u)
                    restart()
                ffn(1)
                restart()


SLABS = 24 + 15


def kernel(**inputs):
    import concourse.bacc as bacc
    from concourse.bass_utils import run_bass_kernel_spmd as run

    g = {k: np.asarray(v) for k, v in inputs.items()}

    def slab(w):
        return np.ascontiguousarray(w.reshape(4, P, -1).transpose(1, 0, 2).reshape(P, -1))

    arrays = {"x": np.ascontiguousarray(g["L0_attn_x"].reshape(BATCH, TT, P, HID).transpose(0, 2, 1, 3))}
    gq = QH * HD
    arrays["wq"] = np.stack([slab(g["L0_attn_wq"][:, k * gq:(k + 1) * gq]) for k in range(GROUPS)])
    arrays["wkv"] = np.stack([slab(np.concatenate([g[n][:, k * HD:(k + 1) * HD] for n in ("L0_attn_wk", "L0_attn_wv")], 1))
                              for k in range(GROUPS)])
    arrays["wo"] = np.stack([slab(g["L0_attn_wo"][k * gq:(k + 1) * gq]) for k in range(GROUPS)])
    arrays["w12"] = np.stack([np.stack([slab(np.concatenate([g[f"L{n}_ffn_w12"].T[:, s * 256:(s + 1) * 256],
                                                             g[f"L{n}_ffn_w12"].T[:, 512 + s * 256:768 + s * 256]], 1))
                                        for s in range(2)]) for n in range(2)])
    arrays["b12"] = np.stack([np.ascontiguousarray(g[f"L{n}_ffn_b12"].reshape(8, P).T) for n in range(2)])
    arrays["w3"] = np.stack([slab(g[f"L{n}_ffn_w3"].T) for n in range(2)])
    wa = g["L1_attn_w_attn"]
    arrays["wc"] = np.stack([slab(np.concatenate([wa[:, k * HID + c * P:k * HID + (c + 1) * P] for k in range(3)], 1))
                             for c in range(CH)])
    arrays["battn"] = np.ascontiguousarray(g["L1_attn_b_attn"].reshape(12, P).T)
    arrays["wproj"] = slab(g["L1_attn_w_proj"])
    arrays["bias_rows"] = np.stack([np.ascontiguousarray(np.broadcast_to(g[n], (P, HID)))
                                    for n in ("L0_ffn_b3", "L1_attn_b_proj", "L1_ffn_b3")])
    half = HD // 2
    inv = (np.float32(10000.0) ** (-np.arange(half, dtype=np.float32) / np.float32(half))).astype(np.float32)
    ang = (inv[:, None] * np.arange(SEQ, dtype=np.float32)[None, :]).astype(np.float32)
    cos, sin = np.cos(ang).astype(np.float32), np.sin(ang).astype(np.float32)
    arrays["rope"] = np.stack([np.concatenate([cos, cos]), np.concatenate([-sin, sin])])
    qi, kj = np.arange(P)[:, None], np.arange(P)[None, :]
    zero = np.zeros((P, P), np.float32)
    arrays["mask0"] = np.concatenate([np.where(kj > qi, zero, -BIG), np.where(kj <= qi, zero, -BIG)], 1).astype(np.float32)
    r = np.arange(512)[None, :] - 384 - qi
    arrays["rel"] = np.where(r <= 0, r, -BIG).astype(np.float32)
    base = 2.0 ** (-2.0 ** (-(np.log2(H1) - 3)))
    sl = (base ** np.arange(1, H1 + 1, dtype=np.float32)).astype(np.float32)
    arrays["slopes"] = np.ascontiguousarray(np.broadcast_to(sl, (P, H1)))
    arrays["ident"] = np.eye(P, dtype=np.float32)
    odd = (np.arange(P) // D1) % 2
    arrays["headmask"] = np.stack([(odd == e) / D1 for e in range(2)], 1).astype(np.float32)

    nc = bacc.Bacc("TRN2", target_bir_lowering=False, num_devices=1)
    args = {k: nc.dram_tensor(f"in_{k}", v.shape, mybir.dt.from_np(v.dtype), kind="ExternalInput").ap()
            for k, v in arrays.items()}
    out = nc.dram_tensor("out", (BATCH, P, TT, HID), mybir.dt.float32, kind="ExternalOutput").ap()
    build(nc, out=out, **args)
    got = run(nc, [{f"in_{k}": v for k, v in arrays.items()}], core_ids=[0]).results[0]["out"]
    return np.ascontiguousarray(got.transpose(0, 2, 1, 3)).reshape(BATCH, SEQ, HID)
```

```python
import numpy as np
import concourse.bass as bass
from concourse import mybir
from contextlib import ExitStack

P = 128
BATCH, SEQ, HID = 4, 512, 512
U = 2
HALVES = BATCH // U
TT = SEQ // P
HC = HID // P
GROUPS, QH, HD = 8, 4, 128
L0_SCALE = float(HD) ** -0.5
STEPS = GROUPS * U
H1, D1 = 32, 16
CH = HID // P
HPC = P // D1
TRI = TT * (TT + 1) // 2
LAYERS = 2
BIG = 3.0e38
EPS = 1e-5
RSQRT_MAGIC = 1597463007.0


def build(nc, x, wq, wkv, wo, w12, b12, w3, wc, battn, wproj, bias_rows, rope, mask0, rel, slopes, ident, headmask, out):
    f32, f32r, i32 = mybir.dt.float32, mybir.dt.float32r, mybir.dt.int32
    ALU, ACT = mybir.AluOpType, mybir.ActivationFunctionType
    ctx = ExitStack()
    with ctx:
        def sb(name, shape, dt=f32):
            return ctx.enter_context(nc.sbuf_tensor(name, shape, dt))

        def sem(name):
            return ctx.enter_context(nc.semaphore(name))

        stage = sb("stage", [P, 2, 1024])
        w_h = {s: sb(f"w{s}_h", [P, HC * 512], f32r) for s in ("q0", "q1", "o", "kv")}
        w_l = {s: sb(f"w{s}_l", [P, HC * 512], f32r) for s in ("q0", "q1", "o", "kv")}
        xn = sb("xn", [P, U, TT, HID])
        xT_h = sb("xT_h", [P, U, HC, SEQ], f32r)
        xT_l = sb("xT_l", [P, U, HC, SEQ], f32r)
        k_h = sb("k_h", [P, 2, SEQ], f32r)
        k_l = sb("k_l", [P, 2, SEQ], f32r)
        q_h = sb("q_h", [P, 2, SEQ], f32r)
        q_l = sb("q_l", [P, 2, SEQ], f32r)
        v_hl = sb("v_hl", [P, 2, 2, TT, P], f32r)
        pT_h = sb("pT_h", [P, 2, 7 * P], f32r)
        pT_l = sb("pT_l", [P, 2, 7 * P], f32r)
        aT_h = sb("aT_h", [P, 4, SEQ], f32r)
        aT_l = sb("aT_l", [P, 4, SEQ], f32r)
        probs_all = sb("probs", [P, 2 * TRI * P])
        probs = probs_all[:, 0:2048].rearrange("p (a i k) -> p a i k", i=4, k=256)
        probs1 = probs_all[:, :].rearrange("p (a k) -> p a k", a=2)
        pT1_h = pT_h[:, :, :].rearrange("p a k -> p (a k)")
        pT1_l = pT_l[:, :, :].rearrange("p a k -> p (a k)")
        v_one = [[v_hl[:, 1, part, :, :] for part in range(2)],
                 [pT[:, TRI * P:TRI * P + 512].rearrange("p (t d) -> p t d", d=P) for pT in (pT1_h, pT1_l)]]
        zeros = sb("zeros", [P, P])
        work = sb("work", [P, 5, 512])
        cos_t = sb("cos_t", [P, SEQ])
        sin_t = sb("sin_t", [P, SEQ])
        mask_t = sb("mask_t", [P, 256])
        rel_t = sb("rel_t", [P, 512])
        ident_t = sb("ident_t", [P, P])
        slopes_t = sb("slopes_t", [P, H1])
        headmask_t = sb("headmask_t", [P, 2])
        bias_t = sb("bias_t", [P, HID])
        b12_t = sb("b12_t", [P, LAYERS, 8])
        hb12_t = sb("hb12_t", [P, LAYERS, 8])
        battn_t = sb("battn_t", [P, 12])
        negmax = sb("negmax", [P, 32])
        sums = sb("sums", [P, 2, 32])
        recips = sb("recips", [P, 32])
        stats = sb("stats", [P, TT, 6])
        meanvar = sb("meanvar", [P, TT, 2])
        newton = sb("newton", [P, 4, TT])

        bank = [ctx.enter_context(nc.psum_tensor(f"bank{i}", [P, 512], f32)) for i in range(8)]
        A, S, T, O = bank[0:2], bank[2:4], bank[4:6], bank[6:8]

        s_ident = sem("identity_loaded")
        s_const = sem("constants_loaded")
        s_hb = sem("halved_bias_ready")
        s_zero = sem("zeros_ready")
        s_stage = [sem(f"stage_full{i}") for i in range(2)]
        s_stage_free = [sem(f"stage_free{i}") for i in range(2)]
        slots = ("q0", "q1", "o", "kv0", "kv1", "m")
        s_w = {s: sem(f"weights_ready_{s}") for s in slots}
        s_w_free = {s: sem(f"weights_used_{s}") for s in slots}
        s_split = sem("split_high_done")
        s_x = [sem(f"x_loaded{u}") for u in range(U)]
        s_store = [sem(f"out_stored{u}") for u in range(U)]
        s_bias = sem("bias_row_loaded")
        s_bias_used = sem("bias_row_used")
        s_biased = sem("residual_biased")
        s_ln = sem("layernorm_done")
        s_tr_done = sem("transposed_x")
        s_tr = [sem(f"xT_bank_full{i}") for i in range(2)]
        s_tr_h = sem("xT_high_done")
        s_xT = sem("xT_ready")
        s_tr_free = [sem(f"xT_bank_free{i}") for i in range(2)]
        s_a = [sem(f"proj_bank_full{i}") for i in range(2)]
        s_a_free = [sem(f"proj_bank_free{i}") for i in range(2)]
        s_s = [sem(f"score_bank_full{i}") for i in range(2)]
        s_s_free = [sem(f"score_bank_free{i}") for i in range(2)]
        s_t = [sem(f"transpose_bank_full{i}") for i in range(2)]
        s_t_free = [sem(f"transpose_bank_free{i}") for i in range(2)]
        s_o = [sem(f"out_bank_full{i}") for i in range(2)]
        s_o_free = [sem(f"out_bank_free{i}") for i in range(2)]
        s_swap = [sem(f"swapped{i}") for i in range(2)]
        s_swap_free = [sem(f"swapped_free{i}") for i in range(2)]
        s_rot = sem("rotated")
        s_rot_h = sem("rotated_high_done")
        s_k = sem("k_ready")
        s_q = sem("q_ready")
        s_vT = sem("vT_copied")
        s_v_h = sem("v_high_done")
        s_v = sem("v_ready")
        s_masked = sem("scores_masked")
        s_exp = sem("exp_done")
        s_p = sem("probs_ready")
        s_pT_h = sem("pT_high_done")
        s_pT = sem("pT_ready")
        s_aT_h = sem("aT_high_done")
        s_aT = sem("aT_ready")
        s_h = [sem(f"ffn_up_bank_full{i}") for i in range(2)]
        s_h_free = [sem(f"ffn_up_bank_free{i}") for i in range(2)]
        s_tanh = sem("ffn_tanh_done")
        s_g = sem("gated_done")
        s_g_h = sem("gated_high_done")
        s_gT = sem("gated_ready")
        s_d = [sem(f"ffn_down_bank_full{i}") for i in range(2)]
        s_d_free = [sem(f"ffn_down_bank_free{i}") for i in range(2)]
        s1_prep = sem("l1_prep_bank_full")
        s1_raw = sem("l1_kqv_copied")
        s1_kh = sem("l1_k_high_done")
        s1_k = sem("l1_k_ready")
        s1_qh = sem("l1_q_high_done")
        s1_q = sem("l1_q_ready")
        s1_vh = sem("l1_v_high_done")
        s1_v = sem("l1_v_ready")
        s1_vone = sem("l1_head_v_ready")
        s1_s = [sem(f"l1_score_bank_full{i}") for i in range(4)]
        s1_tab = sem("alibi_table_ready")
        s1_masked = sem("l1_scores_masked")
        s1_exp = sem("l1_exp_done")
        s1_t = [sem(f"l1_transpose_bank_full{i}") for i in range(2)]
        s1_pT_h = sem("l1_pT_high_done")
        s1_pT = sem("l1_pT_ready")
        s1_pv = sem("l1_head_pv_done")
        s1_recip = sem("l1_reciprocals_ready")
        s1_rows = sem("l1_reciprocal_rows_copied")
        s1_xcols = sem("other_batch_columns_copied")
        s1_nat = sem("l1_out_normalised")
        s1_aT_h = sem("l1_aT_high_done")
        s1_aT = sem("l1_aT_ready")
        s1_pr = sem("l1_proj_full")
        s1_pr_free = sem("l1_proj_used")
        c_dve = sem("vector_chain")
        N_CONST = 9
        s_seen = {e: sem(f"wait_passed_{e}") for e in ("dve", "pool", "pe")}

        def free(eng, s, uses):
            eng.wait_ge(s, uses + 1)

        def word(ap):
            return ap.bitcast(f32)

        FILLS = {"q0": 4 + 1 + 4 + 1, "q1": 4 + 1 + 1, "o": 8 + 3, "kv0": 4, "kv1": 4, "m": 4}

        block = ctx.enter_context(nc.Block())

        @block.sync
        def _(sp):
            def load_x(hf, u):
                if hf > 0:
                    sp.wait_ge(s_store[u], 16 * hf)
                sp.dma_start(xn[:, u, :, :], x[hf * U + u]).then_inc(s_x[u], 16)

            def store(hf, u):
                sp.wait_ge(s_ln, hf * 8 + 7 + u)
                sp.dma_start(out[hf * U + u], xn[:, u, :, :]).then_inc(s_store[u], 16)

            def load(m, src, cols):
                for i in range(2):
                    free(sp, s_stage_free[i], m)
                    sp.dma_start(stage[:, i, 0:cols // 2], src[:, i * (cols // 2):(i + 1) * (cols // 2)]) \
                        .then_inc(s_stage[i], 16)

            def load_bias(k, row):
                free(sp, s_bias_used, k)
                sp.dma_start(bias_t[:, :], bias_rows[row]).then_inc(s_bias, 16)

            for s in (*s_stage_free, s_bias_used):
                sp.sem_inc(s, 1)
            sp.dma_start(ident_t[:, :], ident).then_inc(s_ident, 16)
            load_x(0, 0)
            load(0, wkv[0], 1024)
            for dst, src in ((cos_t, rope[0]), (sin_t, rope[1]), (mask_t, mask0), (rel_t, rel),
                             (slopes_t, slopes), (headmask_t, headmask), (battn_t, battn)):
                sp.dma_start(dst[:, :], src).then_inc(s_const, 16)
            for n in range(LAYERS):
                sp.dma_start(b12_t[:, n, :], b12[n]).then_inc(s_const, 16)
            for hf in range(HALVES):
                m = hf * SLABS
                if hf > 0:
                    load(m, wkv[0], 1024)
                load(m + 1, wq[0], 2048)
                if hf > 0:
                    store(hf - 1, 0)
                    load_x(hf, 0)
                    store(hf - 1, 1)
                load_x(hf, 1)
                load(m + 2, wo[0], 2048)
                load(m + 3, wkv[1], 1024)
                load(m + 4, wq[1], 2048)
                load(m + 5, wo[1], 2048)
                with sp.Fori(1, GROUPS // 2) as g2:
                    ms = [sp.snap(g2 * 6 + m + k) for k in range(6)]
                    gs = [sp.snap(g2 * 2 + p) for p in range(2)]
                    for p in range(2):
                        load(ms[3 * p], wkv[gs[p]], 1024)
                        load(ms[3 * p + 1], wq[gs[p]], 2048)
                        load(ms[3 * p + 2], wo[gs[p]], 2048)
                m += 24
                load(m, w12[0, 0], 2048)
                load(m + 1, w12[0, 1], 2048)
                load(m + 2, w3[0], 2048)
                load(m + 3, wc[0], 1536)
                load_bias(hf * 3, 0)
                load(m + 4, wc[1], 1536)
                load(m + 5, w12[1, 0], 2048)
                load(m + 6, wproj, 2048)
                load_bias(hf * 3 + 1, 1)
                for k in range(6):
                    load(m + 7 + k, wc[(2 + k) % CH], 1536)
                load(m + 13, w12[1, 1], 2048)
                load(m + 14, w3[1], 2048)
                load_bias(hf * 3 + 2, 2)
            for u in range(U):
                store(HALVES - 1, u)
            for u in range(U):
                sp.wait_ge(s_store[u], 16 * HALVES)

        @block.gpsimd
        def _(pool):
            def split(m, slot, fill, cols, also=()):
                free(pool, s_w_free[slot], fill)
                for name, val in also:
                    free(pool, s_w_free[name], val)
                key = {"kv0": "kv", "kv1": "kv", "m": "kv"}.get(slot, slot)
                off = 1024 if slot == "kv1" else 0
                for i in range(2):
                    part = slice(off + i * (cols // 2), off + (i + 1) * (cols // 2))
                    src = stage[:, i, 0:cols // 2]
                    pool.wait_ge(s_stage[i], 16 * m + 16)
                    pool.sem_inc(s_seen["pool"], 1)
                    nc.gpsimd.tensor_copy(w_h[key][:, part], src).then_inc(s_split, 1)
                    pool.wait_ge(s_split, 2 * m + i + 1)
                    low = nc.gpsimd.tensor_tensor(w_l[key][:, part], src, word(w_h[key][:, part]), ALU.subtract)
                    low.then_inc(s_stage_free[i], 1)
                    if i == 1:
                        free(pool, s_stage_free[1], m + 1)
                        pool.sem_inc(s_w[slot], 1)

            def add_bias(hf, k, stage_no, us=range(U)):
                pool.wait_ge(s_bias, hf * 48 + 16 * k + 16)
                for u in us:
                    pool.wait_ge(s_tr_done, hf * 8 + stage_no * 2 + u + 1)
                    bc = bias_t[:, :]
                    for t in range(TT):
                        last = nc.gpsimd.tensor_tensor(xn[:, u, t, :], xn[:, u, t, :], bc, ALU.add)
                        last.then_inc(s_biased, 1)
                if us[-1] == U - 1:
                    pool.wait_ge(s_biased, hf * 24 + k * 8 + 8)
                    pool.sem_inc(s_bias_used, 1)

            for s in s_w_free.values():
                pool.sem_inc(s, 1)
            with pool.Fori(0, HALVES) as hf:
                f = {s: hf * FILLS[s] for s in FILLS}
                with pool.Fori(0, GROUPS // 2) as g2:
                    m = hf * SLABS + g2 * 6
                    for p in range(2):
                        split(m + 3 * p, f"kv{p}", f[f"kv{p}"] + g2, 1024, also=[("m", f["m"])])
                        split(m + 3 * p + 1, f"q{p}", f[f"q{p}"] + g2, 2048)
                        split(m + 3 * p + 2, "o", f["o"] + g2 * 2 + p, 2048)
                m = hf * SLABS + 24
                split(m, "q0", f["q0"] + 4, 2048)
                split(m + 1, "q1", f["q1"] + 4, 2048)
                split(m + 2, "o", f["o"] + 8, 2048)
                split(m + 3, "m", f["m"], 1536, also=[("kv0", f["kv0"] + 4), ("kv1", f["kv1"] + 4)])
                add_bias(hf, 0, 1)
                split(m + 4, "q0", f["q0"] + 5, 1536)
                split(m + 5, "q1", f["q1"] + 5, 2048)
                split(m + 6, "o", f["o"] + 9, 2048)
                add_bias(hf, 1, 2, (0,))
                for k in range(6):
                    if k == 2:
                        add_bias(hf, 1, 2, (1,))
                    split(m + 7 + k, ("m", "q0")[k % 2], f["m"] + 1 + k // 2 if k % 2 == 0 else f["q0"] + 6 + k // 2, 1536)
                split(m + 13, "q0", f["q0"] + 9, 2048)
                split(m + 14, "o", f["o"] + 10, 2048)
                add_bias(hf, 2, 3)

        def three(out_ap, ah, al, bh, bl, first=True, last=True, skip=False):
            nc.tensor.matmul(out_ap, ah, bh, start=first, stop=False, skip_group_check=skip)
            nc.tensor.matmul(out_ap, ah, bl, start=False, stop=False, skip_group_check=skip)
            return nc.tensor.matmul(out_ap, al, bh, start=False, stop=last, skip_group_check=skip)

        def project(out_ap, key, width, col, u, off=0):
            for c in range(HC):
                a = off + c * width + col
                last = three(out_ap, w_h[key][:, a:a + P], w_l[key][:, a:a + P],
                             xT_h[:, u, c, :], xT_l[:, u, c, :], c == 0, c == HC - 1)
            return last

        def down(out_ap, key, t, chunks=range(4)):
            for c in chunks:
                last = three(out_ap, aT_h[:, c, t * P:(t + 1) * P], aT_l[:, c, t * P:(t + 1) * P],
                             w_h[key][:, c * 512:(c + 1) * 512], w_l[key][:, c * 512:(c + 1) * 512],
                             c == 0, c == 3)
            return last

        Q_BANK = ((1, 0), (1, 1), (0, 2), (1, 2))

        T_BLOCKS = [[(0, 0), (1, 0), (1, 1), (2, 1)], [(2, 2), (3, 2), (3, 3)]]

        Q_ORDER = (3, 2, 1, 0)

        PT_UNIT = ((0, 512), (512, 384), (896, 256), (1152, 128))

        def prep_bank(c, k):
            return (O[0], T[0], T[1])[k] if c == 0 else O[c % 2]

        def prep_use(c):
            return 5 * c - 1 if c else 0

        def rows_use(c):
            return 5 * c + 8 if c + 1 < CH else 5 * CH - 1

        @block.tensor
        def _(pe):
            pe.wait_ge(s_ident, 16)

            def transpose_x(hf, st, u):
                if st == 0:
                    pe.wait_ge(s_x[u], hf * 16 + 16)
                else:
                    pe.wait_ge(s_ln, hf * 8 + (st - 1) * 2 + u + 1)
                for c in range(HC):
                    free(pe, s_tr_free[c % 2], (hf * 8 + st * 2 + u) * 2 + c // 2)
                    for t in range(TT):
                        last = nc.tensor.transpose(T[c % 2][:, t * P:(t + 1) * P], xn[:, u, t, c * P:(c + 1) * P],
                                                   ident_t[:, :])
                    last.then_inc(s_tr[c % 2], 1)
                pe.wait_ge(s_tr[1], (hf * 8 + st * 2 + u) * 2 + 2)
                pe.sem_inc(s_tr_done, 1)

            def transpose_other(hf, u, c):
                use = hf * 8 + 5 + u
                pe.wait_ge(s1_xcols, (hf * 2 + u) * HC + c + 1)
                if c == 0:
                    free(pe, s1_nat, hf * 8 + u * 4 + CH - 1)
                else:
                    pe.wait_ge(s_xT, use * 4 + c)
                for t in range(TT):
                    last = nc.tensor.transpose(O[0][:, t * P:(t + 1) * P], work[:, 2 + c % 2, t * P:(t + 1) * P],
                                               ident_t[:, :])
                last.then_inc(s_tr[c % 2], 1)
                if c == HC - 1:
                    pe.wait_ge(s_tr[1], use * 2 + 2)
                    pe.sem_inc(s_tr_done, 1)

            def l0_step(n, hf, g, p, u, front, back, between=None):
                n1 = n - 1 if back else None
                pb, ub = (p if u == 1 else 1 - p), 1 - u

                def k():
                    pe.wait_ge(s_w[f"kv{p}"], hf * FILLS["kv0"] + g + 1)
                    free(pe, s_a_free[0], 3 * n)
                    project(A[0][:, :], "kv", 256, 0, u, off=1024 * p).then_inc(s_a[0], 1)

                def v():
                    free(pe, s_a_free[0], 3 * n + 1)
                    project(A[0][:, :], "kv", 256, P, u, off=1024 * p).then_inc(s_a[0], 1)

                def kv_used():
                    if u == 1:
                        pe.wait_ge(s_a[0], 3 * n + 2)
                        pe.sem_inc(s_w_free[f"kv{p}"], 1)

                def q(h):
                    if h == 0:
                        pe.wait_ge(s_w[f"q{p}"], hf * FILLS[f"q{p}"] + g + 1)
                    b, use = Q_BANK[h]
                    free(pe, s_a_free[b], 3 * n + use)
                    project(A[b][:, :], f"q{p}", 512, h * P, u).then_inc(s_a[b], 1)

                def q_used():
                    if u == 1:
                        pe.wait_ge(s_a[1], 3 * n + 3)
                        pe.sem_inc(s_w_free[f"q{p}"], 1)

                def scores(n, h, u):
                    pe.wait_ge(s_q, 4 * n + h + 1)
                    if h == 0:
                        pe.wait_ge(s_k, n + 1)
                    for i in range(TT):
                        if i % 2 == 0:
                            free(pe, s_s_free[i // 2], 4 * n + h)
                        lo = P if i == 0 else 0
                        k0 = (i - 1) * P + lo
                        last = three(S[i // 2][:, (i % 2) * 256 + lo:(i % 2) * 256 + 256],
                                     q_h[:, h % 2, i * P:(i + 1) * P], q_l[:, h % 2, i * P:(i + 1) * P],
                                     k_h[:, u, k0:(i + 1) * P], k_l[:, u, k0:(i + 1) * P])
                        if i % 2 == 1:
                            last.then_inc(s_s[i // 2], 1)

                def transposes(n, h):
                    pe.wait_ge(s_p, 4 * n + h + 1)
                    for b in range(2):
                        free(pe, s_t_free[b], (5 * n + h + (h > 0)) if b == 0 else (4 * n + h))
                        for k, (i, j) in enumerate(T_BLOCKS[b]):
                            c0 = (j - i + 1) * P
                            last = nc.tensor.transpose(T[b][:, k * P:(k + 1) * P],
                                                       probs[:, h % 2, i, c0:c0 + P], ident_t[:, :])
                        last.then_inc(s_t[b], 1)

                def v_transposes():
                    pe.wait_ge(s_vT, n + 1)
                    free(pe, s_t_free[0], 5 * n + 1)
                    for t in range(TT):
                        last = nc.tensor.transpose(T[0][:, t * P:(t + 1) * P], work[:, 4, t * P:(t + 1) * P],
                                                   ident_t[:, :])
                    last.then_inc(s_t[0], 1)

                def pv(n, h, u):
                    b = h % 2
                    pe.wait_ge(s_pT, 4 * n + h + 1)
                    if h == 0:
                        pe.wait_ge(s_v, n + 1)
                    free(pe, s_o_free[b], 4 * n + h // 2)
                    for j in range(TT):
                        w = 2 * P if j < 3 else P
                        seg = slice(j * 2 * P, j * 2 * P + w)
                        last = three(O[b][:, j * P:j * P + w], v_hl[:, u, 0, j, :], v_hl[:, u, 1, j, :],
                                     pT_h[:, h % 2, seg], pT_l[:, h % 2, seg], j == 0, j == 3, skip=True)
                    last.then_inc(s_o[b], 1)

                def wo_tile(n, t):
                    b = t % 2
                    if t == 0:
                        pe.wait_ge(s_w["o"], hf * FILLS["o"] + (g * 2 + p if u == 1 else g * 2 + p - 1) + 1)
                        pe.wait_ge(s_aT, 4 * n + 3)
                    free(pe, s_o_free[b], 4 * n + 2 + t // 2)
                    if t == 0:
                        down(O[b][:, :], "o", t, range(3))
                        pe.wait_ge(s_aT, 4 * n + 4)
                        down(O[b][:, :], "o", t, (3,)).then_inc(s_o[b], 1)
                    else:
                        down(O[b][:, :], "o", t).then_inc(s_o[b], 1)

                def wo_used(n):
                    if ub == 1:
                        pe.wait_ge(s_o[1], 4 * n + 4)
                        pe.sem_inc(s_w_free["o"], 1)

                if front:
                    k()
                if back:
                    pv(n1, 1, ub)
                if front:
                    q(0)
                if back:
                    transposes(n1, 3)
                    pv(n1, 2, ub)
                if front:
                    v()
                    q(1)
                if back:
                    pv(n1, 3, ub)
                if front:
                    kv_used()
                    scores(n, 0, u)
                    q(2)
                if back:
                    wo_tile(n1, 0)
                if front:
                    scores(n, 1, u)
                    if between:
                        q(3)
                        between()
                    transposes(n, 0)
                if back:
                    wo_tile(n1, 1)
                if front:
                    if not between:
                        q(3)
                    v_transposes()
                    scores(n, 2, u)
                if back:
                    wo_tile(n1, 2)
                if front:
                    transposes(n, 1)
                    q_used()
                if back:
                    wo_tile(n1, 3)
                if front:
                    scores(n, 3, u)
                    pv(n, 0, u)
                    transposes(n, 2)
                if back:
                    wo_used(n1)

            def ffn_up(hf, layer, u, ms):
                f = hf * 4 + layer * 2 + u
                pe.wait_ge(s_xT, (hf * 8 + (2 * layer + 1) * 2 + u) * 4 + 4)
                if layer == 1:
                    free(pe, s1_pr_free, hf * 8 + 8)
                for m in ms:
                    key = (("q0", "q1"), ("q1", "q0"))[layer][m // 2]
                    fills = {("q0", 0): 5, ("q1", 0): 5, ("q1", 1): 6, ("q0", 1): 10}[key, layer]
                    if m % 2 == 0:
                        pe.wait_ge(s_w[key], hf * FILLS[key] + fills)
                    free(pe, s_h_free[m % 2], 2 * f + m // 2)
                    b = (A, S)[m % 2]
                    project(b[0][:, :], key, 512, (m % 2) * P, u)
                    project(b[1][:, :], key, 512, 256 + (m % 2) * P, u).then_inc(s_h[m % 2], 1)
                    if m % 2 == 1 and u == 1:
                        pe.wait_ge(s_h[1], 2 * f + m // 2 + 1)
                        pe.sem_inc(s_w_free[key], 1)

            def ffn_down(hf, layer, u, between=None):
                f = hf * 4 + layer * 2 + u
                pe.wait_ge(s_w["o"], hf * FILLS["o"] + (9, 11)[layer])
                for t in range(2):
                    free(pe, s_d_free[t], 2 * f)
                for c in range(4):
                    pe.wait_ge(s_gT, 4 * f + c + 1)
                    for t in range(2):
                        last = down(O[t][:, :], "o", t, (c,))
                        if c == 3:
                            last.then_inc(s_d[t], 1)
                if between:
                    between()
                for t in range(2, TT):
                    free(pe, s_d_free[t % 2], 2 * f + 1)
                    down(O[t % 2][:, :], "o", t).then_inc(s_d[t % 2], 1)
                if u == 1:
                    pe.wait_ge(s_d[1], 2 * f + 2)
                    pe.sem_inc(s_w_free["o"], 1)

            def l1_batch(a0, hf, u):
                def project_chunk(c, k, col, width=384):
                    return project(prep_bank(c, k)[:, :], "q0" if c % 2 else "kv", width, col * P, u)

                def k(c):
                    slot = ("m", "q0")[c % 2]
                    pe.wait_ge(s_w[slot], hf * FILLS[slot] + u * 2 + (1, 6)[c % 2] + c // 2)
                    free(pe, s1_nat, a0 + max(c - 1, 0))
                    project_chunk(c, 0, 1).then_inc(s1_prep, 1)

                def q(c):
                    if c:
                        pe.wait_ge(s1_raw, 3 * (a0 + c) + 1)
                    project_chunk(c, 1, 0).then_inc(s1_prep, 1)

                def v(c):
                    if c:
                        pe.wait_ge(s1_raw, 3 * (a0 + c) + 2)
                    project_chunk(c, 2, 2).then_inc(s1_prep, 1)

                def v_transposes(c):
                    pe.wait_ge(s1_raw, 3 * (a0 + c) + 3)
                    pe.sem_inc(s_w_free[("m", "q0")[c % 2]], 1)
                    for t in range(TT):
                        last = nc.tensor.transpose(O[c % 2][:, t * P:(t + 1) * P], work[:, 4, t * P:(t + 1) * P],
                                                   ident_t[:, :])
                    last.then_inc(s1_prep, 1)

                def reciprocal_rows(c):
                    b = O[(c + 1) % 2]
                    pe.wait_ge(s1_recip, a0 + c + 1)
                    if c < CH - 1:
                        pe.wait_ge(s1_v, a0 + c + 2)
                    else:
                        pe.wait_ge(s_xT, (hf * 8 + 6 + u) * 4)
                    for t in range(TT):
                        last = nc.tensor.transpose(b[:, t * P:(t + 1) * P], work[:, 3, t * P:(t + 1) * P], ident_t[:, :])
                    last.then_inc(s1_prep, 1)

                def scores(H, i):
                    c, k = divmod(H, HPC)
                    par, r = divmod(k, 4)
                    if i == Q_ORDER[0] and k == 0:
                        pe.wait_ge(s1_k, a0 + c + 1)
                    if i == Q_ORDER[0] and r == 0:
                        pe.wait_ge(s1_q, 2 * (a0 + c) + par + 1)
                    if i == Q_ORDER[0] and H > 0:
                        pe.wait_ge(s1_exp, 4 * (a0 * HPC + H - 1) + 1)
                    rows = slice(32 * r, 32 * r + 32)
                    qs = slice(i * P, (i + 1) * P)
                    n = (i + 1) * P
                    three(bank[i][:, 0:n], q_h[rows, par, qs], q_l[rows, par, qs],
                          k_h[rows, c % 2, 0:n], k_l[rows, c % 2, 0:n]).then_inc(s1_s[i], 1)

                def transposes(H, j):
                    Hg = a0 * HPC + H
                    if j == 0:
                        pe.wait_ge(s1_exp, 4 * Hg + 4)
                    if j >= 2:
                        pe.wait_ge(s1_pT, 4 * Hg + j - 1)
                    for i in range(j, TT):
                        p0 = (i * (i + 1) // 2 + j) * P
                        last = nc.tensor.transpose(T[j % 2][:, (i - j) * P:(i - j + 1) * P],
                                                   probs1[:, H % 2, p0:p0 + P], ident_t[:, :])
                    last.then_inc(s1_t[j % 2], 1)

                def pv(H, j):
                    c, k = divmod(H, HPC)
                    Hg = a0 * HPC + H
                    if j == 0:
                        pe.wait_ge(s1_vone, Hg + 2)
                        if k == 0:
                            free(pe, s1_rows, a0 + c)
                    pe.wait_ge(s1_pT, 4 * Hg + j + 1)
                    vo = v_one[H % 2]
                    off, w = PT_UNIT[j]
                    last = three(O[c % 2][:, j * P:512], vo[0][:, j, :], vo[1][:, j, :],
                                 pT1_h[:, off:off + w], pT1_l[:, off:off + w], k == 0 and j == 0,
                                 k == HPC - 1 and j == TT - 1, skip=True)
                    if j == TT - 1:
                        last.then_inc(s1_pv, 1)

                k(0)
                q(0)
                v(0)
                v_transposes(0)
                free(pe, s1_pr_free, a0)
                for i in Q_ORDER:
                    scores(0, i)
                for H in range(H1):
                    c, k8 = divmod(H, HPC)
                    ahead = H + 1 < H1
                    if ahead:
                        scores(H + 1, Q_ORDER[0])
                    transposes(H, 0)
                    if k8 == 0 and c:
                        reciprocal_rows(c - 1)
                    if ahead:
                        scores(H + 1, Q_ORDER[1])
                    if H > 0:
                        pv(H - 1, 3)
                    transposes(H, 1)
                    if ahead:
                        scores(H + 1, Q_ORDER[2])
                        scores(H + 1, Q_ORDER[3])
                    transposes(H, 2)
                    if 2 <= k8 <= 5:
                        if c + 1 < CH:
                            (k, q, v, v_transposes)[k8 - 2](c + 1)
                        else:
                            transpose_other(hf, u, k8 - 2)
                    for j in range(3):
                        pv(H, j)
                        if j == 0:
                            transposes(H, 3)
                        if H == H1 - 1 and j == 1:
                            reciprocal_rows(c)
                pv(H1 - 1, 3)

            for s in (*s_tr_free, *s_a_free, *s_s_free, *s_t_free, *s_o_free, *s_h_free, *s_d_free, s1_nat, s1_rows,
                      s1_pr_free, s1_pv, s1_pv):
                pe.sem_inc(s, 1)
            with pe.Fori(0, HALVES) as hf:
                n0 = hf * STEPS
                transpose_x(hf, 0, 0)
                pe.wait_ge(s_xT, hf * 32 + 4)
                def other_batch():
                    transpose_x(hf, 0, 1)
                    pe.wait_ge(s_xT, hf * 32 + 8)

                l0_step(n0, hf, 0, 0, 0, True, False, other_batch)
                l0_step(n0 + 1, hf, 0, 0, 1, True, True)
                l0_step(n0 + 2, hf, 0, 1, 0, True, True)
                l0_step(n0 + 3, hf, 0, 1, 1, True, True)
                with pe.Fori(1, GROUPS // 2) as g2:
                    for s in range(4):
                        l0_step(n0 + g2 * 4 + s, hf, g2, s // 2, s % 2, True, True)
                l0_step(n0 + STEPS, hf, GROUPS // 2, 0, 0, False, True)

                def ffn(layer):
                    st = 2 * layer + 1
                    if layer == 0:
                        transpose_x(hf, st, 0)
                    ffn_up(hf, layer, 0, (0, 1))
                    transpose_x(hf, st, 1)
                    ffn_up(hf, layer, 0, (2, 3))
                    ffn_up(hf, layer, 1, (0, 1))
                    ffn_down(hf, layer, 0)
                    ffn_up(hf, layer, 1, (2, 3))
                    ffn_down(hf, layer, 1, (lambda: transpose_x(hf, 2, 0)) if layer == 0 else None)

                ffn(0)
                for s in s_d_free:
                    free(pe, s, 2 * (hf * 4 + 1) + 2)
                pe.sem_inc(s_seen["pe"], 1)
                with pe.Fori(0, U) as u:
                    pe.wait_ge(s_xT, (hf * 8 + 5 + u) * 4)
                    l1_batch(hf * 8 + u * 4, hf, u)
                    pe.wait_ge(s_w["o"], hf * FILLS["o"] + 10)
                    for c in range(CH):
                        pe.wait_ge(s1_aT, hf * 8 + u * 4 + c + 2)
                        for t in range(TT):
                            last = down(bank[t][:, :], "o", t, (c,))
                            if c == CH - 1:
                                last.then_inc(s1_pr, 1)
                pe.wait_ge(s1_pr, hf * 8 + 8)
                pe.sem_inc(s_w_free["o"], 1)
                ffn(1)

        @block.scalar
        def _(act):

            def copy(dst, src):
                return nc.scalar.activation(dst, src, ACT.Copy)

            def transpose_x(hf, st, u):
                for c in range(HC):
                    act.wait_ge(s_tr[c % 2], (hf * 8 + st * 2 + u) * 2 + c // 2 + 1)
                    copy(xT_h[:, u, c, :], T[c % 2][:, :]).then_inc(s_tr_h, 1)

            def l0_step(n, u, front, back, between=None):
                n1 = n - 1 if back else None
                ub = 1 - u

                def swap(item):
                    b, use = (0, 0) if item == 0 else Q_BANK[item - 1]
                    sbuf = item % 2
                    sidx = (3 * n + item // 2) if sbuf == 0 else (2 * n + item // 2)
                    act.wait_ge(s_a[b], 3 * n + use + 1)
                    free(act, s_swap_free[sbuf], sidx)
                    copy(work[0:64, sbuf, :], A[b][64:128, :])
                    copy(work[64:128, sbuf, :], A[b][0:64, :]).then_inc(s_swap[sbuf], 1)

                def high(item):
                    dst = k_h[:, u, :] if item == 0 else q_h[:, (item - 1) % 2, :]
                    act.wait_ge(s_rot, 5 * n + item + 1)
                    copy(dst, work[:, 2 + item % 2, :]).then_inc(s_rot_h, 1)

                def v_copy():
                    act.wait_ge(s_a[0], 3 * n + 2)
                    copy(work[:, 4, :], A[0][:, :]).then_inc(s_vT, 1)
                    act.wait_ge(s_vT, n + 1)
                    act.sem_inc(s_a_free[0], 1)

                def exps(n, h):
                    for i in range(TT):
                        lo = P if i == 0 else 0
                        act.wait_ge(s_masked, 16 * n + 4 * h + i + 1)
                        col = (h % 2) * 4 + i
                        nc.scalar.activation(probs[:, h % 2, i, lo:256], probs[:, h % 2, i, lo:256], ACT.Exp,
                                             bias=negmax[:, col:col + 1], scale=-1.0,
                                             accum_out=sums[:, 0, col:col + 1]).then_inc(s_exp, 1)

                def pT_high(n, h):
                    for b in range(2):
                        act.wait_ge(s_t[b], (5 * n + 1 + h + (h > 0)) if b == 0 else (4 * n + h + 1))
                        w = len(T_BLOCKS[b]) * P
                        copy(pT_h[:, h % 2, b * 512:b * 512 + w], T[b][:, 0:w]).then_inc(s_pT_h, 1)

                def v_high():
                    act.wait_ge(s_t[0], 5 * n + 2)
                    copy(v_hl[:, u, 0, :, :], T[0][:, :].rearrange("p (t d) -> p t d", d=P)).then_inc(s_v_h, 1)

                def aT_high(n, h):
                    act.wait_ge(s_o[h % 2], 4 * n + h // 2 + 1)
                    copy(aT_h[:, h, :], O[h % 2][:, :]).then_inc(s_aT_h, 1)

                if front:
                    swap(0)
                    high(0)
                if back:
                    aT_high(n1, 1)
                if front:
                    swap(1)
                if back:
                    pT_high(n1, 3)
                if front:
                    high(1)
                if back:
                    aT_high(n1, 2)
                if front:
                    v_copy()
                    swap(2)
                if back:
                    aT_high(n1, 3)
                if front:
                    high(2)
                    exps(n, 0)
                    swap(3)
                    high(3)
                    if between:
                        between()
                    pT_high(n, 0)
                    exps(n, 1)
                    swap(4)
                    v_high()
                    high(4)
                    exps(n, 2)
                    pT_high(n, 1)
                    exps(n, 3)
                    aT_high(n, 0)
                    pT_high(n, 2)

            def ffn_tanh(hf, layer, u, m):
                f = hf * 4 + layer * 2 + u
                act.wait_ge(s_h[m % 2], 2 * f + m // 2 + 1)
                if m >= 2:
                    act.wait_ge(s_g, 4 * f + m - 1)
                nc.scalar.activation(work[:, m % 2, :], (A, S)[m % 2][0][:, :], ACT.Tanh, scale=0.5,
                                     bias=hb12_t[:, layer, m:m + 1]).then_inc(s_tanh, 1)

            def gated_high(f, m):
                act.wait_ge(s_g, 4 * f + m + 1)
                copy(aT_h[:, m, :], work[:, 2 + m % 2, :]).then_inc(s_g_h, 1)

            def l1_batch(a0, hf, u):
                def raw(c, k, col, buf):
                    act.wait_ge(s1_prep, 5 * a0 + prep_use(c) + k + 1)
                    if k == 2:
                        act.wait_ge(s1_aT, a0 + max(c - 1, 0) + 1)
                    nc.scalar.activation(work[:, buf, :], prep_bank(c, k)[:, :], ACT.Identity,
                                         bias=battn_t[:, col * CH + c:col * CH + c + 1]).then_inc(s1_raw, 1)
                    act.wait_ge(s1_raw, 3 * (a0 + c) + k + 1)

                def k_prep(c):
                    raw(c, 0, 1, 3)
                    copy(k_h[:, c % 2, :], work[:, 3, :]).then_inc(s1_kh, 1)

                def q_prep(c):
                    raw(c, 1, 0, 2)

                def q_high(c, e):
                    nc.scalar.activation(q_h[:, e, :], work[:, 2, :], ACT.Copy,
                                         scale=headmask_t[:, e:e + 1]).then_inc(s1_qh, 1)

                def v_prep(c):
                    raw(c, 2, 2, 4)

                def v_high(c):
                    act.wait_ge(s1_prep, 5 * a0 + prep_use(c) + 4)
                    act.wait_ge(s1_vone, HPC * (a0 + c) + 1)
                    copy(v_hl[:, 0, 0, :, :], O[c % 2][:, :].rearrange("p (t d) -> p t d", d=P)).then_inc(s1_vh, 1)

                def rows_copy(c):
                    act.wait_ge(s1_prep, 5 * a0 + rows_use(c) + 1)
                    if c == CH - 1:
                        act.wait_ge(s1_aT, a0 + c + 1)
                    copy(work[:, 4, :], O[(c + 1) % 2][:, :]).then_inc(s1_rows, 1)

                def aT_high(c):
                    act.wait_ge(s1_nat, a0 + c + 2)
                    copy(aT_h[:, c, :], work[:, 4, :]).then_inc(s1_aT_h, 1)

                def table(H):
                    c, k = divmod(H, HPC)
                    par, r = divmod(k, 4)
                    h = c * HPC + 2 * r + par
                    nc.scalar.activation(work[:, H % 2, :], rel_t[:, :], ACT.Copy,
                                         scale=slopes_t[:, h:h + 1]).then_inc(s1_tab, 1)

                def exp(H, i):
                    c, k = divmod(H, HPC)
                    par, r = divmod(k, 4)
                    p0, w = i * (i + 1) // 2 * P, (i + 1) * P
                    col = i * HPC + 2 * r + par
                    act.wait_ge(s1_masked, 4 * (a0 * HPC + H) + Q_ORDER.index(i) + 1)
                    nm = k * 4 + i
                    nc.scalar.activation(probs1[:, H % 2, p0:p0 + w], probs1[:, H % 2, p0:p0 + w], ACT.Exp,
                                         bias=negmax[:, nm:nm + 1], scale=-1.0,
                                         accum_out=sums[:, c % 2, col:col + 1]).then_inc(s1_exp, 1)

                def pT_high(H, j):
                    off, w = PT_UNIT[j]
                    act.wait_ge(s1_t[j % 2], 2 * (a0 * HPC + H) + j // 2 + 1)
                    copy(pT1_h[:, off:off + w], T[j % 2][:, 0:w]).then_inc(s1_pT_h, 1)

                table(0)
                table(1)
                k_prep(0)
                q_prep(0)
                q_high(0, 0)
                q_high(0, 1)
                v_prep(0)
                v_high(0)
                for i in Q_ORDER:
                    exp(0, i)
                for H in range(H1):
                    c, k8 = divmod(H, HPC)
                    ahead = H + 1 < H1
                    pT_high(H, 0)
                    if k8 == 0 and c:
                        rows_copy(c - 1)
                    if ahead:
                        exp(H + 1, Q_ORDER[0])
                    pT_high(H, 1)
                    if ahead:
                        exp(H + 1, Q_ORDER[1])
                    pT_high(H, 2)
                    if ahead:
                        exp(H + 1, Q_ORDER[2])
                        exp(H + 1, Q_ORDER[3])
                    if k8 == 1 and c:
                        aT_high(c - 1)
                    if c == CH - 1 and 2 <= k8 <= 5:
                        act.wait_ge(s_tr[k8 % 2], (hf * 8 + 5 + u) * 2 + (k8 - 2) // 2 + 1)
                        copy(xT_h[:, 1 - u, k8 - 2, :], O[0][:, :]).then_inc(s_tr_h, 1)
                    if c + 1 < CH:
                        if k8 == 2:
                            k_prep(c + 1)
                        if k8 == 3:
                            q_prep(c + 1)
                            q_high(c + 1, 0)
                        if k8 == 4:
                            v_prep(c + 1)
                        if k8 == 6:
                            q_high(c + 1, 1)
                    pT_high(H, 3)
                    if H + 2 < H1:
                        table(H + 2)
                    if c + 1 < CH and k8 == 6:
                        v_high(c + 1)
                    if H == H1 - 1:
                        rows_copy(c)
                aT_high(CH - 1)

            for s in s_swap_free:
                act.sem_inc(s, 1)
            with act.Fori(0, HALVES) as hf:
                n0 = hf * STEPS
                transpose_x(hf, 0, 0)
                act.wait_ge(s_const, 16 * N_CONST)
                act.wait_ge(s_hb, 1)
                l0_step(n0, 0, True, False, lambda: transpose_x(hf, 0, 1))
                for s in range(1, 4):
                    l0_step(n0 + s, s % 2, True, True)
                with act.Fori(1, GROUPS // 2) as g2:
                    for s in range(4):
                        l0_step(n0 + g2 * 4 + s, s % 2, True, True)
                l0_step(n0 + STEPS, 0, False, True)

                def ffn(layer):
                    st = 2 * layer + 1
                    f0, f1 = (hf * 4 + layer * 2 + u for u in range(U))
                    if layer == 0:
                        transpose_x(hf, st, 0)
                    ffn_tanh(hf, layer, 0, 0)
                    ffn_tanh(hf, layer, 0, 1)
                    transpose_x(hf, st, 1)
                    gated_high(f0, 0)
                    ffn_tanh(hf, layer, 0, 2)
                    gated_high(f0, 1)
                    ffn_tanh(hf, layer, 0, 3)
                    gated_high(f0, 2)
                    gated_high(f0, 3)
                    ffn_tanh(hf, layer, 1, 0)
                    ffn_tanh(hf, layer, 1, 1)
                    act.wait_ge(s_d[1], 2 * f0 + 2)
                    gated_high(f1, 0)
                    gated_high(f1, 1)
                    ffn_tanh(hf, layer, 1, 2)
                    ffn_tanh(hf, layer, 1, 3)
                    gated_high(f1, 2)
                    gated_high(f1, 3)

                ffn(0)
                transpose_x(hf, 2, 0)
                with act.Fori(0, U) as u:
                    l1_batch(hf * 8 + u * 4, hf, u)
                ffn(1)

        @block.vector
        def _(dve):
            count = [0]

            def link(ins):
                count[0] += 1
                ins.then_inc(c_dve, 1)
                dve.wait_ge(c_dve, count[0])

            def restart():
                if count[0]:
                    dve.sem_clear(c_dve)
                    count[0] = 0

            def low(dst, src, high):
                return nc.vector.tensor_tensor(dst, src, word(high), ALU.subtract)


            def transpose_x(hf, st, u):
                for c in range(HC):
                    dve.wait_ge(s_tr_h, (hf * 8 + st * 2 + u) * 4 + c + 1)
                    low(xT_l[:, u, c, :], T[c % 2][:, :], xT_h[:, u, c, :]).then_inc(s_xT, 1)
                    dve.wait_ge(s_xT, (hf * 8 + st * 2 + u) * 4 + c + 1)
                    dve.sem_inc(s_tr_free[c % 2], 1)

            def l0_step(n, u, front, back, between=None):
                n1 = n - 1 if back else None
                ub = 1 - u

                def rotate(item):
                    b = 0 if item == 0 else Q_BANK[item - 1][0]
                    sbuf = item % 2
                    sidx = (3 * n + item // 2) if sbuf == 0 else (2 * n + item // 2)
                    rot = work[:, 2 + item % 2, :]
                    dve.wait_ge(s_swap[sbuf], sidx + 1)
                    nc.vector.tensor_tensor(rot, A[b][:, :], cos_t[:, :], ALU.mult).then_inc(s_a_free[b], 1)
                    link(nc.vector.tensor_tensor(work[:, sbuf, :], work[:, sbuf, :], sin_t[:, :], ALU.mult))
                    nc.vector.tensor_tensor(rot, rot, work[:, sbuf, :], ALU.add).then_inc(s_rot, 1)
                    dve.wait_ge(s_rot, 5 * n + item + 1)
                    dve.sem_inc(s_swap_free[sbuf], 1)

                def rot_low(item):
                    dve.wait_ge(s_rot_h, 5 * n + item + 1)
                    rot = work[:, 2 + item % 2, :]
                    if item == 0:
                        low(k_l[:, u, :], rot, k_h[:, u, :]).then_inc(s_k, 1)
                    else:
                        q = (item - 1) % 2
                        low(q_l[:, q, :], rot, q_h[:, q, :]).then_inc(s_q, 1)

                def mask(n, h):
                    for i in range(TT):
                        lo = P if i == 0 else 0
                        col = (h % 2) * 4 + i
                        if i % 2 == 0:
                            dve.wait_ge(s_s[i // 2], 4 * n + h + 1)
                            dve.sem_inc(s_seen["dve"], 1)
                        nc.vector.tensor_tensor_reduce(
                            out=probs[:, h % 2, i, lo:256], in0=S[i // 2][:, (i % 2) * 256 + lo:(i % 2) * 256 + 256],
                            in1=mask_t[:, lo:256], scale=-L0_SCALE, scalar=BIG, op0=ALU.add, op1=ALU.min,
                            accum_out=negmax[:, col:col + 1]).then_inc(s_masked, 1)
                        if i % 2 == 1:
                            dve.wait_ge(s_masked, 16 * n + 4 * h + i + 1)
                            dve.sem_inc(s_s_free[i // 2], 1)

                def normalise(n, h):
                    c0 = (h % 2) * 4
                    dve.wait_ge(s_exp, 16 * n + 4 * h + 4)
                    link(nc.vector.reciprocal(recips[:, c0:c0 + 4], sums[:, 0, c0:c0 + 4]))
                    for i in range(TT):
                        lo = P if i == 0 else 0
                        p = probs[:, h % 2, i, lo:256]
                        last = nc.vector.tensor_scalar(p, p, recips[:, c0 + i:c0 + i + 1], None, ALU.mult)
                    last.then_inc(s_p, 1)

                def pT_low(n, h):
                    for b in range(2):
                        w = len(T_BLOCKS[b]) * P
                        seg = slice(b * 512, b * 512 + w)
                        dve.wait_ge(s_pT_h, 8 * n + 2 * h + b + 1)
                        last = low(pT_l[:, h % 2, seg], T[b][:, 0:w], pT_h[:, h % 2, seg])
                        last.then_inc(s_t_free[b], 1)
                    free(dve, s_t_free[1], 4 * n + h + 1)
                    dve.sem_inc(s_pT, 1)

                def v_low():
                    dve.wait_ge(s_v_h, n + 1)
                    low(v_hl[:, u, 1, :, :], T[0][:, :].rearrange("p (t d) -> p t d", d=P),
                        v_hl[:, u, 0, :, :]).then_inc(s_v, 1)
                    dve.wait_ge(s_v, n + 1)
                    dve.sem_inc(s_t_free[0], 1)

                def aT_low(n, h):
                    dve.wait_ge(s_aT_h, 4 * n + h + 1)
                    low(aT_l[:, h, :], O[h % 2][:, :], aT_h[:, h, :]).then_inc(s_aT, 1)
                    dve.wait_ge(s_aT, 4 * n + h + 1)
                    dve.sem_inc(s_o_free[h % 2], 1)

                def accumulate(n, u, t):
                    dve.wait_ge(s_o[t % 2], 4 * n + 3 + t // 2)
                    nc.vector.tensor_tensor(xn[:, u, t, :], O[t % 2][:, :], xn[:, u, t, :], ALU.add)\
                        .then_inc(s_o_free[t % 2], 1)

                restart()
                if front:
                    rotate(0)
                    rot_low(0)
                if back:
                    aT_low(n1, 1)
                if not front:
                    free(dve, s_o_free[1], 4 * n1)
                    ln_stats(0, (0, 1))
                if front:
                    rotate(1)
                if back:
                    pT_low(n1, 3)
                if front:
                    rot_low(1)
                else:
                    ln_stats(0, (2, 3))
                if back:
                    aT_low(n1, 2)
                if front:
                    rotate(2)
                if back:
                    aT_low(n1, 3)
                if not front:
                    ln_rsqrt()
                    ln_apply(0)
                if front:
                    rot_low(2)
                    mask(n, 0)
                    normalise(n, 0)
                    rotate(3)
                    mask(n, 1)
                    if between:
                        between()
                    rot_low(3)
                    pT_low(n, 0)
                if back:
                    accumulate(n1, ub, 0)
                if front:
                    normalise(n, 1)
                if back:
                    accumulate(n1, ub, 1)
                if front:
                    rotate(4)
                    v_low()
                    mask(n, 2)
                    rot_low(4)
                    normalise(n, 2)
                if back:
                    accumulate(n1, ub, 2)
                if front:
                    pT_low(n, 1)
                if back:
                    accumulate(n1, ub, 3)
                if front:
                    mask(n, 3)
                    normalise(n, 3)
                    aT_low(n, 0)
                    pT_low(n, 2)

            def ln_stats(u, tiles):
                for t in tiles:
                    last = nc.vector.bn_stats(stats[:, t, :], xn[:, u, t, :])
                link(last)

            def ln_guess():
                for t in range(TT):
                    last = nc.vector.bn_aggr(meanvar[:, t, :], stats[:, t, :])
                link(last)
                var, y, y2, z = (newton[:, k, :] for k in range(4))
                link(nc.vector.tensor_scalar(var, meanvar[:, :, 1], EPS, None, ALU.add))
                link(nc.vector.tensor_scalar(y.bitcast(i32), var.bitcast(i32), 1, None, ALU.logical_shift_right))
                link(nc.vector.tensor_scalar(y.bitcast(i32), y.bitcast(i32), -1.0, RSQRT_MAGIC, ALU.mult, ALU.add))

            def ln_newton():
                var, y, y2, z = (newton[:, k, :] for k in range(4))
                link(nc.vector.tensor_tensor(y2, y, y, ALU.mult))
                link(nc.vector.scalar_tensor_tensor(z, y2, -0.5, var, ALU.mult, ALU.mult))
                link(nc.vector.scalar_tensor_tensor(y, z, 1.5, y, ALU.add, ALU.mult))

            def ln_rsqrt():
                ln_guess()
                for _ in range(3):
                    ln_newton()

            def ln_apply(u, tiles=range(TT)):
                for t in tiles:
                    last = nc.vector.tensor_scalar(xn[:, u, t, :], xn[:, u, t, :], meanvar[:, t, 0:1],
                                                   newton[:, 1, t:t + 1], ALU.subtract, ALU.mult)
                if t == TT - 1:
                    last.then_inc(s_ln, 1)

            def layernorm(u, taken=0):
                ln_stats(u, range(taken, TT))
                ln_rsqrt()
                ln_apply(u)

            def ffn_gate(hf, layer, u, m):
                f = hf * 4 + layer * 2 + u
                b = (A, S)[m % 2]
                e = work[:, m % 2, :]
                g = work[:, 2 + m % 2, :]
                dve.wait_ge(s_tanh, 4 * f + m + 1)
                link(nc.vector.tensor_scalar(e, e, 0.5, 0.5, ALU.mult, ALU.add))
                link(nc.vector.scalar_tensor_tensor(g, b[0][:, :], b12_t[:, layer, m:m + 1], e, ALU.add, ALU.mult))
                nc.vector.scalar_tensor_tensor(g, b[1][:, :], b12_t[:, layer, 4 + m:5 + m], g,
                                               ALU.add, ALU.mult).then_inc(s_g, 1)
                dve.wait_ge(s_g, 4 * f + m + 1)
                dve.sem_inc(s_h_free[m % 2], 1)

            def gated_low(hf, layer, u, m):
                dve.wait_ge(s_g_h, 4 * (hf * 4 + layer * 2 + u) + m + 1)
                low(aT_l[:, m, :], work[:, 2 + m % 2, :], aT_h[:, m, :]).then_inc(s_gT, 1)

            def ffn_residual(hf, layer, u, take_stats=True, tiles=range(TT)):
                f = hf * 4 + layer * 2 + u
                dve.wait_ge(s_biased, hf * 24 + layer * 16 + u * 4 + 4)
                for t in tiles:
                    dve.wait_ge(s_d[t % 2], 2 * f + t // 2 + 1)
                    nc.vector.tensor_tensor(xn[:, u, t, :], O[t % 2][:, :], xn[:, u, t, :], ALU.add)\
                        .then_inc(s_d_free[t % 2], 1)
                    if t > 0 and take_stats:
                        free(dve, s_d_free[(t - 1) % 2], 2 * f + (t - 1) // 2 + 1)
                        nc.vector.bn_stats(stats[:, t - 1, :], xn[:, u, t - 1, :])

            def ffn_layernorm(hf, layer, u):
                f = hf * 4 + layer * 2 + u
                free(dve, s_d_free[1], 2 * f + 2)
                layernorm(u, TT - 1)

            def l1_batch(a0, hf, u):
                def k_low(c):
                    dve.wait_ge(s1_kh, a0 + c + 1)
                    low(k_l[:, c % 2, :], work[:, 3, :], k_h[:, c % 2, :]).then_inc(s1_k, 1)

                def q_low(c, e):
                    dve.wait_ge(s1_qh, 2 * (a0 + c) + e + 1)
                    nc.vector.scalar_tensor_tensor(q_l[:, e, :], work[:, 2, :], headmask_t[:, e:e + 1],
                                                   word(q_h[:, e, :]), ALU.mult, ALU.subtract).then_inc(s1_q, 1)

                def v_low(c):
                    dve.wait_ge(s1_vh, a0 + c + 1)
                    low(v_hl[:, 0, 1, :, :], O[c % 2][:, :].rearrange("p (t d) -> p t d", d=P),
                        v_hl[:, 0, 0, :, :]).then_inc(s1_v, 1)

                def head_columns(v, H):
                    par, r = divmod(H % HPC, 4)
                    h = 2 * r + par
                    return v[:, :, h * D1:(h + 1) * D1]

                def v_head(H):
                    c, k = divmod(H, HPC)
                    vo = v_one[H % 2]
                    dve.wait_ge(s1_pv, a0 * HPC + H + 1)
                    for part in range(2):
                        nc.vector.tensor_copy(head_columns(vo[part], H - 2), zeros[:, 0:TT * D1].rearrange("p (t e) -> p t e", e=D1))
                    if k == 0:
                        dve.wait_ge(s1_v, a0 + c + 1)
                    for part in range(2):
                        last = nc.vector.tensor_copy(head_columns(vo[part], H), word(head_columns(v_hl[:, 0, part, :, :], H)))
                    last.then_inc(s1_vone, 1)

                def mask(H, i):
                    Hg = a0 * HPC + H
                    p0, w = i * (i + 1) // 2 * P, (i + 1) * P
                    nm = H % HPC * 4 + i
                    if i == Q_ORDER[0]:
                        dve.wait_ge(s1_tab, Hg + 1)
                    dve.wait_ge(s1_s[i], Hg + 1)
                    dve.sem_inc(s_seen["dve"], 1)
                    nc.vector.tensor_tensor_reduce(
                        out=probs1[:, H % 2, p0:p0 + w], in0=bank[i][:, 0:w], in1=work[:, H % 2, 512 - w:512],
                        scale=-1.0, scalar=BIG, op0=ALU.add, op1=ALU.min,
                        accum_out=negmax[:, nm:nm + 1]).then_inc(s1_masked, 1)

                def pT_low(H, j):
                    off, w = PT_UNIT[j]
                    dve.wait_ge(s1_pT_h, 4 * (a0 * HPC + H) + j + 1)
                    low(pT1_l[:, off:off + w], T[j % 2][:, 0:w], pT1_h[:, off:off + w]).then_inc(s1_pT, 1)

                def reciprocals(c):
                    dve.wait_ge(s1_exp, 4 * HPC * (a0 + c + 1))
                    link(nc.vector.reciprocal(recips[:, :], sums[:, c % 2, :]))
                    nc.vector.tensor_copy(work[:, 3, :].rearrange("p (s e) -> p s e", e=D1),
                                          recips[:, :].unsqueeze(2).to_broadcast([P, 32, D1])).then_inc(s1_recip, 1)

                def normalise(c):
                    dve.wait_ge(s1_pv, HPC * (a0 + c + 1) + 2)
                    dve.wait_ge(s1_rows, a0 + c + 2)
                    nc.vector.tensor_tensor(work[:, 4, :], O[c % 2][:, :], work[:, 4, :], ALU.mult).then_inc(s1_nat, 1)

                def aT_low(c):
                    dve.wait_ge(s1_aT_h, a0 + c + 1)
                    low(aT_l[:, c, :], work[:, 4, :], aT_h[:, c, :]).then_inc(s1_aT, 1)

                k_low(0)
                q_low(0, 0)
                q_low(0, 1)
                v_low(0)
                for i in Q_ORDER:
                    mask(0, i)
                v_head(0)
                for H in range(H1):
                    c, k8 = divmod(H, HPC)
                    ahead = H + 1 < H1
                    if H == H1 - 1:
                        reciprocals(c)
                    if ahead:
                        mask(H + 1, Q_ORDER[0])
                    pT_low(H, 0)
                    if ahead:
                        mask(H + 1, Q_ORDER[1])
                    pT_low(H, 1)
                    if k8 == 7 and c + 1 < CH:
                        v_low(c + 1)
                    if ahead:
                        mask(H + 1, Q_ORDER[2])
                    pT_low(H, 2)
                    if ahead:
                        mask(H + 1, Q_ORDER[3])
                        if k8 == 7:
                            reciprocals(c)
                        v_head(H + 1)
                    if k8 == 0 and c:
                        normalise(c - 1)
                    if k8 == 1 and c:
                        aT_low(c - 1)
                    if c + 1 < CH:
                        if k8 == 2:
                            k_low(c + 1)
                        if k8 == 3:
                            q_low(c + 1, 0)
                        if k8 == 6:
                            q_low(c + 1, 1)
                    if H == 2:
                        free(dve, s1_pr_free, hf * 8 + u * 4)
                        dve.sem_inc(s_seen["dve"], 1)
                    if 2 <= H <= 5:
                        ln_stats(1 - u, (H - 2,))
                    if H == 10:
                        ln_guess()
                    if 11 <= H <= 13:
                        ln_newton()
                    if H == 18:
                        ln_apply(1 - u, (0, 1))
                    if 19 <= H <= 20:
                        ln_apply(1 - u, (H - 17,))
                    if c == CH - 1 and 1 <= k8 <= 4:
                        if k8 == 1:
                            dve.wait_ge(s_ln, hf * 8 + 4 + u)
                            dve.sem_inc(s_seen["dve"], 1)
                        nc.vector.tensor_copy(work[:, 2 + (k8 - 1) % 2, :].rearrange("p (t k) -> p t k", k=P),
                                              xn[:, 1 - u, :, (k8 - 1) * P:k8 * P]).then_inc(s1_xcols, 1)
                    if c == CH - 1 and 2 <= k8 <= 5:
                        use = (hf * 8 + 5 + u) * 4 + k8 - 2
                        dve.wait_ge(s_tr_h, use + 1)
                        low(xT_l[:, 1 - u, k8 - 2, :], O[0][:, :], xT_h[:, 1 - u, k8 - 2, :]).then_inc(s_xT, 1)
                        dve.wait_ge(s_xT, use + 1)
                        dve.sem_inc(s_tr_free[k8 % 2], 1)
                    pT_low(H, 3)
                normalise(CH - 1)
                aT_low(CH - 1)

            def l1_residual(hf, u):
                dve.wait_ge(s_biased, hf * 24 + 8 + u * 4 + 4)
                for t in range(TT):
                    dve.wait_ge(s1_pr, hf * 8 + u * 4 + t + 1)
                    nc.vector.tensor_tensor(xn[:, u, t, :], bank[t][:, :], xn[:, u, t, :], ALU.add)\
                        .then_inc(s1_pr_free, 1)

            nc.vector.memset(zeros[:, :], 0.0).then_inc(s_zero, 1)
            dve.wait_ge(s_zero, 1)
            for s in (s1_vone, s1_aT):
                dve.sem_inc(s, 1)
            with dve.Fori(0, HALVES) as hf:
                restart()
                n0 = hf * STEPS
                transpose_x(hf, 0, 0)
                dve.wait_ge(s_const, 16 * N_CONST)
                nc.vector.tensor_scalar(hb12_t[:, :, :], b12_t[:, :, :], 0.5, None, ALU.mult).then_inc(s_hb, 1)
                l0_step(n0, 0, True, False, lambda: transpose_x(hf, 0, 1))
                for s in range(1, 4):
                    l0_step(n0 + s, s % 2, True, True)
                restart()
                with dve.Fori(1, GROUPS // 2) as g2:
                    for s in range(4):
                        l0_step(n0 + g2 * 4 + s, s % 2, True, True)
                    restart()
                l0_step(n0 + STEPS, 0, False, True)

                def ffn(layer):
                    st = 2 * layer + 1
                    if layer == 0:
                        transpose_x(hf, st, 0)
                        free(dve, s_o_free[1], 4 * (n0 + STEPS))
                    else:
                        free(dve, s1_pr_free, hf * 8 + 8)
                    layernorm(1)
                    restart()
                    ffn_gate(hf, layer, 0, 0)
                    transpose_x(hf, st, 1)
                    for m in range(1, 4):
                        ffn_gate(hf, layer, 0, m)
                        gated_low(hf, layer, 0, m - 1)
                    gated_low(hf, layer, 0, 3)
                    ffn_gate(hf, layer, 1, 0)
                    ffn_gate(hf, layer, 1, 1)
                    ffn_residual(hf, layer, 0)
                    gated_low(hf, layer, 1, 0)
                    gated_low(hf, layer, 1, 1)
                    restart()
                    ffn_layernorm(hf, layer, 0)
                    ffn_gate(hf, layer, 1, 2)
                    ffn_gate(hf, layer, 1, 3)
                    gated_low(hf, layer, 1, 2)
                    gated_low(hf, layer, 1, 3)
                    restart()
                    ffn_residual(hf, layer, 1, layer == 1, (0, 1))
                    if layer == 0:
                        transpose_x(hf, 2, 0)
                    ffn_residual(hf, layer, 1, layer == 1, (2, 3))
                    if layer == 1:
                        ffn_layernorm(hf, layer, 1)

                ffn(0)
                free(dve, s_d_free[1], 2 * (hf * 4 + 1) + 2)
                restart()
                for vo in v_one:
                    for part in vo:
                        for t in range(TT):
                            nc.vector.tensor_copy(part[:, t, :], zeros[:, :])
                with dve.Fori(0, U) as u:
                    l1_batch(hf * 8 + u * 4, hf, u)
                    l1_residual(hf, u)
                    restart()
                ffn(1)
                restart()


SLABS = 24 + 15


def kernel(**inputs):
    import concourse.bacc as bacc
    from concourse.bass_utils import run_bass_kernel_spmd as run

    g = {k: np.asarray(v) for k, v in inputs.items()}

    def slab(w):
        return np.ascontiguousarray(w.reshape(4, P, -1).transpose(1, 0, 2).reshape(P, -1))

    arrays = {"x": np.ascontiguousarray(g["L0_attn_x"].reshape(BATCH, TT, P, HID).transpose(0, 2, 1, 3))}
    gq = QH * HD
    arrays["wq"] = np.stack([slab(g["L0_attn_wq"][:, k * gq:(k + 1) * gq]) for k in range(GROUPS)])
    arrays["wkv"] = np.stack([slab(np.concatenate([g[n][:, k * HD:(k + 1) * HD] for n in ("L0_attn_wk", "L0_attn_wv")], 1))
                              for k in range(GROUPS)])
    arrays["wo"] = np.stack([slab(g["L0_attn_wo"][k * gq:(k + 1) * gq]) for k in range(GROUPS)])
    arrays["w12"] = np.stack([np.stack([slab(np.concatenate([g[f"L{n}_ffn_w12"].T[:, s * 256:(s + 1) * 256],
                                                             g[f"L{n}_ffn_w12"].T[:, 512 + s * 256:768 + s * 256]], 1))
                                        for s in range(2)]) for n in range(2)])
    arrays["b12"] = np.stack([np.ascontiguousarray(g[f"L{n}_ffn_b12"].reshape(8, P).T) for n in range(2)])
    arrays["w3"] = np.stack([slab(g[f"L{n}_ffn_w3"].T) for n in range(2)])
    wa = g["L1_attn_w_attn"]
    arrays["wc"] = np.stack([slab(np.concatenate([wa[:, k * HID + c * P:k * HID + (c + 1) * P] for k in range(3)], 1))
                             for c in range(CH)])
    arrays["battn"] = np.ascontiguousarray(g["L1_attn_b_attn"].reshape(12, P).T)
    arrays["wproj"] = slab(g["L1_attn_w_proj"])
    arrays["bias_rows"] = np.stack([np.ascontiguousarray(np.broadcast_to(g[n], (P, HID)))
                                    for n in ("L0_ffn_b3", "L1_attn_b_proj", "L1_ffn_b3")])
    half = HD // 2
    inv = (np.float32(10000.0) ** (-np.arange(half, dtype=np.float32) / np.float32(half))).astype(np.float32)
    ang = (inv[:, None] * np.arange(SEQ, dtype=np.float32)[None, :]).astype(np.float32)
    cos, sin = np.cos(ang).astype(np.float32), np.sin(ang).astype(np.float32)
    arrays["rope"] = np.stack([np.concatenate([cos, cos]), np.concatenate([-sin, sin])])
    qi, kj = np.arange(P)[:, None], np.arange(P)[None, :]
    zero = np.zeros((P, P), np.float32)
    arrays["mask0"] = np.concatenate([np.where(kj > qi, zero, -BIG), np.where(kj <= qi, zero, -BIG)], 1).astype(np.float32)
    r = np.arange(512)[None, :] - 384 - qi
    arrays["rel"] = np.where(r <= 0, r, -BIG).astype(np.float32)
    base = 2.0 ** (-2.0 ** (-(np.log2(H1) - 3)))
    sl = (base ** np.arange(1, H1 + 1, dtype=np.float32)).astype(np.float32)
    arrays["slopes"] = np.ascontiguousarray(np.broadcast_to(sl, (P, H1)))
    arrays["ident"] = np.eye(P, dtype=np.float32)
    odd = (np.arange(P) // D1) % 2
    arrays["headmask"] = np.stack([(odd == e) / D1 for e in range(2)], 1).astype(np.float32)

    nc = bacc.Bacc("TRN2", target_bir_lowering=False, num_devices=1)
    args = {k: nc.dram_tensor(f"in_{k}", v.shape, mybir.dt.from_np(v.dtype), kind="ExternalInput").ap()
            for k, v in arrays.items()}
    out = nc.dram_tensor("out", (BATCH, P, TT, HID), mybir.dt.float32, kind="ExternalOutput").ap()
    build(nc, out=out, **args)
    got = run(nc, [{f"in_{k}": v for k, v in arrays.items()}], core_ids=[0]).results[0]["out"]
    return np.ascontiguousarray(got.transpose(0, 2, 1, 3)).reshape(BATCH, SEQ, HID)
```
